# Optimizing a Trainium2 kernel written in Bass

```python
import numpy as np
import jax
import jax.numpy as jnp

def _softmax(x, axis=-1):
    return jax.nn.softmax(x, axis=axis)

def _gelu(x):
    return jax.nn.gelu(x, approximate=True)

def _silu(x):
    return jax.nn.silu(x)

def _sigmoid(x):
    return jax.nn.sigmoid(x)

def _layernorm(x, axis=-1, eps=1e-05):
    m = jnp.mean(x, axis=axis, keepdims=True)
    v = jnp.var(x, axis=axis, keepdims=True)
    return (x - m) / jnp.sqrt(v + eps)

def _scatter_add(tgt, idx, src, axis=0):
    return tgt.at[idx].add(src)

def _segment_sum(src, seg, n):
    return jax.ops.segment_sum(src, seg, n)
kernel_name = 'mk_xattn_ffn_d4_seqx_r8_931282'

def setup_inputs(seed: int=0):
    np.random.seed(seed)
    _w = jnp.asarray

    def _rec_inputs():
        import jax
        import jax.numpy as jnp
        _rk = jax.random.key(seed)
        x = -0.000929 + 1 * jax.random.normal(jax.random.fold_in(_rk, 1), (8, 100, 256), jnp.float32)
        _lenS = 100 - jax.random.randint(jax.random.fold_in(_rk, 7), (8,), 0, max(1, 100 // 4) + 1, jnp.int32)
        _lenS2 = 1444 - jax.random.randint(jax.random.fold_in(_rk, 8), (8,), 0, max(1, 1444 // 4) + 1, jnp.int32)
        _ctx_2048P = jax.random.normal(jax.random.fold_in(_rk, 11), (8, 16, 256), jnp.float32)
        _ctx_2048c = jax.random.dirichlet(jax.random.fold_in(_rk, 511), 0.3 * jnp.ones((16,), jnp.float32), (8, 1444))
        _ctx_2048t = jnp.einsum('bsk,bkd->bsd', _ctx_2048c, _ctx_2048P)
        _ctx_2048t = _ctx_2048t * jax.lax.rsqrt(jnp.mean(jnp.square(_ctx_2048t)) + 1e-12) * 0.953939
        ctx_2048 = 2.81802e-05 + 1.00001 * (_ctx_2048t + 0.3 * jax.random.normal(jax.random.fold_in(_rk, 611), (8, 1444, 256), jnp.float32))
        _validS = jnp.arange(100)[None, :] < _lenS[:, None]
        _validS2 = jnp.arange(1444)[None, :] < _lenS2[:, None]
        _causal = jnp.tril(jnp.ones((100, 100), dtype=bool))
        mask_BxSxS2_ff0 = jnp.where(jnp.ones((8, 100, 1444), dtype=bool), 0.0, -1000000000.0).astype(jnp.float32)
        mask_BxS2_bk0 = jnp.logical_not(jnp.broadcast_to(_validS2[:, :], (8, 1444)))
        return (x, ctx_2048, mask_BxSxS2_ff0, mask_BxS2_bk0)
    x, ctx_2048, mask_BxSxS2_ff0, mask_BxS2_bk0 = _rec_inputs()

    def _L0_xattn_setup():
        import jax, jax.numpy as jnp
        import numpy as np
        from jax import lax
        LN_EPS = 1e-05
        key = jax.random.key(seed)
        ks = jax.random.split(key, 8)
        B, S, T, D = (4, 128, 256, 256)
        scale = 0.02
        return {'Z': jax.random.normal(ks[0], (B, S, D), dtype=jnp.float32), 'kv': jax.random.normal(ks[1], (B, T, D), dtype=jnp.float32), 'decay': jnp.float32(0.9), 'W_in': jax.random.normal(ks[2], (D, D), dtype=jnp.float32) * scale, 'b_in': jnp.zeros((D,), dtype=jnp.float32), 'W_out': jax.random.normal(ks[3], (D, D), dtype=jnp.float32) * scale, 'b_out': jnp.zeros((D,), dtype=jnp.float32), 'gamma': jnp.ones((D,), dtype=jnp.float32), 'beta': jnp.zeros((D,), dtype=jnp.float32)}
    _L0_xattn_all = _L0_xattn_setup()
    _L0_xattn_in = {k: v for k, v in _L0_xattn_all.items() if k in ('decay', 'W_in', 'b_in', 'W_out', 'b_out', 'gamma', 'beta')}
    del _L0_xattn_all

    def _L0_ffn_setup():
        import jax, jax.numpy as jnp
        import numpy as np
        HIDDEN = 256
        FFN = 176
        N_EXPERTS = 16
        TOP_K = 4
        SHARED_FFN = 2 * FFN

        def _glu_ffn(x, gate_up, down):
            gu = x @ gate_up.T
            g, u = jnp.split(gu, 2, axis=-1)
            return jax.nn.silu(g) * u @ down.T
        key = jax.random.key(seed)
        ks = jax.random.split(key, 6)
        s = 0.02
        return {'hidden_states': jax.random.normal(ks[0], (1, 256, HIDDEN), jnp.float32), 'gate_weight': jax.random.normal(ks[1], (N_EXPERTS, HIDDEN), jnp.float32) * s, 'gate_up_weights': jax.random.normal(ks[2], (N_EXPERTS, 2 * FFN, HIDDEN), jnp.float32) * s, 'down_weights': jax.random.normal(ks[3], (N_EXPERTS, HIDDEN, FFN), jnp.float32) * s, 'shared_gate_up': jax.random.normal(ks[4], (2 * SHARED_FFN, HIDDEN), jnp.float32) * s, 'shared_down': jax.random.normal(ks[5], (HIDDEN, SHARED_FFN), jnp.float32) * s}
    _L0_ffn_all = _L0_ffn_setup()
    _L0_ffn_in = {k: v for k, v in _L0_ffn_all.items() if k in ('gate_weight', 'gate_up_weights', 'down_weights', 'shared_gate_up', 'shared_down')}
    del _L0_ffn_all

    def _L1_xattn_setup():
        import math
        import jax, jax.numpy as jnp
        import numpy as np
        HEADS = 16
        MASKED_BIAS = -10000.0

        def _mha(q, k, v):
            B, Sq, D = q.shape
            Sk = k.shape[-2]
            hd = D // HEADS
            qh = q.reshape(B, Sq, HEADS, hd).transpose(0, 2, 1, 3)
            kh = k.reshape(B, Sk, HEADS, hd).transpose(0, 2, 1, 3)
            vh = v.reshape(B, Sk, HEADS, hd).transpose(0, 2, 1, 3)
            scores = jnp.einsum('bhqd,bhkd->bhqk', qh, kh) / math.sqrt(hd)
            qi = jnp.arange(Sq)[:, None] + (Sk - Sq)
            ki = jnp.arange(Sk)[None, :]
            causal = ki <= qi
            scores = jnp.where(causal[None, None], scores, jnp.asarray(MASKED_BIAS, scores.dtype))
            attn = jax.nn.softmax(scores, axis=-1)
            out = jnp.einsum('bhqk,bhkd->bhqd', attn, vh)
            return out.transpose(0, 2, 1, 3).reshape(B, Sq, D)
        key = jax.random.key(seed)
        kq, kk, kv = jax.random.split(key, 3)
        B, S, D = (4, 128, 256)
        q = jax.random.normal(kq, (B, S, D), dtype=jnp.float32)
        k = jax.random.normal(kk, (B, S, D), dtype=jnp.float32)
        v = jax.random.normal(kv, (B, S, D), dtype=jnp.float32)
        return {'q': q, 'k': k, 'v': v}
    _L1_xattn_all = _L1_xattn_setup()
    _L1_xattn_in = {k: v for k, v in _L1_xattn_all.items() if k in ()}
    del _L1_xattn_all

    def _L1_ffn_setup():
        import jax, jax.numpy as jnp
        import numpy as np
        TOP_K = 2
        SCALING = 2.0
        key = jax.random.key(seed)
        ks = jax.random.split(key, 10)
        B, S, H, I, E, R = (1, 64, 256, 128, 8, 16)
        w = 1.0 / np.sqrt(H)
        inp = {'x': jax.random.normal(ks[0], (B, S, H), jnp.float32), 'gate_weight': jax.random.normal(ks[1], (E, H), jnp.float32) * w, 'gate_lora_A': jax.random.normal(ks[2], (R, H), jnp.float32) * 0.02, 'gate_lora_B': jax.random.normal(ks[3], (E, R), jnp.float32) * 0.02, 'gate_up_proj': jax.random.normal(ks[4], (E, H, 2 * I), jnp.float32) * w, 'down_proj': jax.random.normal(ks[5], (E, I, H), jnp.float32) * (1.0 / np.sqrt(I)), 'gup_lora_A': jax.random.normal(ks[6], (E, R, H), jnp.float32) * 0.02, 'gup_lora_B': jax.random.normal(ks[7], (E, 2 * I, R), jnp.float32) * 0.02, 'down_lora_A': jax.random.normal(ks[8], (E, R, I), jnp.float32) * 0.02, 'down_lora_B': jax.random.normal(ks[9], (E, H, R), jnp.float32) * 0.02}
        return inp
    _L1_ffn_all = _L1_ffn_setup()
    _L1_ffn_in = {k: v for k, v in _L1_ffn_all.items() if k in ('gate_weight', 'gate_lora_A', 'gate_lora_B', 'gate_up_proj', 'down_proj', 'gup_lora_A', 'gup_lora_B', 'down_lora_A', 'down_lora_B')}
    del _L1_ffn_all

    def _L2_xattn_setup():
        import jax, jax.numpy as jnp
        import numpy as np
        B, Q_LEN, E = (8, 16, 256)
        CACHE_LEN = 512
        key = jax.random.key(seed)
        ks = jax.random.split(key, 9)
        s = 1.0 / np.sqrt(E)
        return {'x': jax.random.normal(ks[0], (B, Q_LEN, E), jnp.float32), 'attention_mask': jnp.zeros((B, Q_LEN, CACHE_LEN), jnp.float32), 'k_cache': jax.random.normal(ks[1], (B, CACHE_LEN, E), jnp.float32), 'v_cache': jax.random.normal(ks[2], (B, CACHE_LEN, E), jnp.float32), 'Wq': jax.random.normal(ks[3], (E, E), jnp.float32) * s, 'bq': jax.random.normal(ks[4], (E,), jnp.float32) * s, 'Wk': jax.random.normal(ks[5], (E, E), jnp.float32) * s, 'bk': jax.random.normal(ks[6], (E,), jnp.float32) * s, 'Wv': jax.random.normal(ks[7], (E, E), jnp.float32) * s, 'bv': jax.random.normal(ks[8], (E,), jnp.float32) * s}
    _L2_xattn_all = _L2_xattn_setup()
    _L2_xattn_in = {k: v for k, v in _L2_xattn_all.items() if k in ('Wq', 'bq', 'Wk', 'bk', 'Wv', 'bv')}
    del _L2_xattn_all

    def _L2_ffn_setup():
        import jax, jax.numpy as jnp
        import numpy as np
        NUM_EXPERTS = 32
        TOP_K = 8
        SELECT_TOP_K = 4
        THRESHOLD = 0.5
        HIDDEN = 256
        D_FF = 96

        def _moe_forward(hidden_states, gate_weight, gate_up_proj, down_proj, similarity):
            B, S_len, H = hidden_states.shape
            E, K, Ssel = (NUM_EXPERTS, TOP_K, SELECT_TOP_K)
            x = hidden_states.reshape(-1, H)
            router_logits = x @ gate_weight.T
            router_probs = jax.nn.softmax(router_logits.astype(jnp.float32), axis=-1).astype(router_logits.dtype)
            router_top_value, router_indices = jax.lax.top_k(router_probs, K)
            routing_weights = router_top_value / jnp.clip(jnp.sum(router_top_value, axis=-1, keepdims=True), 1e-12, None)
            sim = similarity.astype(jnp.float32)
            sim = sim.at[jnp.arange(E), jnp.arange(E)].set(1.0)
            prim = router_indices[:, :Ssel]
            sec = router_indices[:, Ssel:]
            sim_cand = sim[sec[:, :, None], prim[:, None, :]]
            best_sim = jnp.max(sim_cand, axis=-1)
            best_i = jnp.argmax(sim_cand, axis=-1)
            prim_rep = jnp.broadcast_to(prim[:, None, :], sim_cand.shape)
            best_primary = jnp.take_along_axis(prim_rep, best_i[..., None], axis=-1)[..., 0]
            new_sec = jnp.where(best_sim < THRESHOLD, sec, best_primary) if THRESHOLD > 0.0 else best_primary
            rerouted_indices = jnp.concatenate([prim, new_sec], axis=1)
            combine = jnp.sum(jax.nn.one_hot(rerouted_indices, E, dtype=routing_weights.dtype) * routing_weights[..., None], axis=1)

            def expert_step(y, params):
                wgu, wd, cw = params
                gu = x @ wgu.T
                g, u = jnp.split(gu, 2, axis=-1)
                h = jax.nn.silu(g) * u
                y = y + h @ wd.T * cw[:, None]
                return (y, None)
            y0 = jnp.zeros_like(x)
            y, _ = jax.lax.scan(expert_step, y0, (gate_up_proj, down_proj, combine.T))
            return y.reshape(B, S_len, H)
        key = jax.random.key(seed)
        ks = jax.random.split(key, 5)
        hidden_states = jax.random.normal(ks[0], (4, 256, HIDDEN), dtype=jnp.float32)
        gate_weight = jax.random.normal(ks[1], (NUM_EXPERTS, HIDDEN), dtype=jnp.float32) * 0.02
        gate_up_proj = jax.random.normal(ks[2], (NUM_EXPERTS, 2 * D_FF, HIDDEN), dtype=jnp.float32) * 0.02
        down_proj = jax.random.normal(ks[3], (NUM_EXPERTS, HIDDEN, D_FF), dtype=jnp.float32) * 0.02
        similarity = jax.random.uniform(ks[4], (NUM_EXPERTS, NUM_EXPERTS), dtype=jnp.float32)
        return {'hidden_states': hidden_states, 'gate_weight': gate_weight, 'gate_up_proj': gate_up_proj, 'down_proj': down_proj, 'similarity': similarity}
    _L2_ffn_all = _L2_ffn_setup()
    _L2_ffn_in = {k: v for k, v in _L2_ffn_all.items() if k in ('gate_weight', 'gate_up_proj', 'down_proj', 'similarity')}
    del _L2_ffn_all

    def _L3_xattn_setup():
        import jax, jax.numpy as jnp
        import numpy as np
        key = jax.random.key(seed)
        k1, k2, k3 = jax.random.split(key, 3)
        B, S, D, M = (8, 256, 256, 128)
        hidden_states = jax.random.normal(k1, (B, S, D), dtype=jnp.float32)
        memory_tokens = jax.random.normal(k2, (B, M, D), dtype=jnp.float32)
        memory_mask = jax.random.randint(k3, (B, M), 0, 2).astype(jnp.bool_)
        return {'hidden_states': hidden_states, 'memory_tokens': memory_tokens, 'memory_mask': memory_mask}
    _L3_xattn_all = _L3_xattn_setup()
    _L3_xattn_in = {k: v for k, v in _L3_xattn_all.items() if k in ()}
    del _L3_xattn_all

    def _L3_ffn_setup():
        import jax, jax.numpy as jnp
        import numpy as np
        TOPK = 2
        key = jax.random.key(seed)
        ks = jax.random.split(key, 6)
        B, T, H, S, r, ad = (2, 512, 256, 32, 16, 32)
        h = jax.random.normal(ks[0], (B, T, H), dtype=jnp.float32)
        Wr = jax.random.normal(ks[1], (S, H), dtype=jnp.float32) * 0.02
        U = jax.random.normal(ks[2], (S, H, r), dtype=jnp.float32) * 0.02
        V = jax.random.normal(ks[3], (S, r, H), dtype=jnp.float32) * 0.02
        attr = jax.random.normal(ks[4], (S, ad), dtype=jnp.float32) * 0.02
        Wa = jax.random.normal(ks[5], (1, ad), dtype=jnp.float32) * 0.02
        return {'h': h, 'Wr': Wr, 'U': U, 'V': V, 'attr': attr, 'Wa': Wa}
    _L3_ffn_all = _L3_ffn_setup()
    _L3_ffn_in = {k: v for k, v in _L3_ffn_all.items() if k in ('Wr', 'U', 'V', 'attr', 'Wa')}
    del _L3_ffn_all
    return {'x': x, 'ctx_2048': ctx_2048, 'mask_BxSxS2_ff0': mask_BxSxS2_ff0, 'mask_BxS2_bk0': mask_BxS2_bk0, 'L0_xattn_decay': _L0_xattn_in['decay'], 'L0_xattn_W_in': _L0_xattn_in['W_in'], 'L0_xattn_b_in': _L0_xattn_in['b_in'], 'L0_xattn_W_out': _L0_xattn_in['W_out'], 'L0_xattn_b_out': _L0_xattn_in['b_out'], 'L0_xattn_gamma': _L0_xattn_in['gamma'], 'L0_xattn_beta': _L0_xattn_in['beta'], 'L0_ffn_gate_weight': _L0_ffn_in['gate_weight'], 'L0_ffn_gate_up_weights': _L0_ffn_in['gate_up_weights'], 'L0_ffn_down_weights': _L0_ffn_in['down_weights'], 'L0_ffn_shared_gate_up': _L0_ffn_in['shared_gate_up'], 'L0_ffn_shared_down': _L0_ffn_in['shared_down'], 'L1_ffn_gate_weight': _L1_ffn_in['gate_weight'], 'L1_ffn_gate_lora_A': _L1_ffn_in['gate_lora_A'], 'L1_ffn_gate_lora_B': _L1_ffn_in['gate_lora_B'], 'L1_ffn_gate_up_proj': _L1_ffn_in['gate_up_proj'], 'L1_ffn_down_proj': _L1_ffn_in['down_proj'], 'L1_ffn_gup_lora_A': _L1_ffn_in['gup_lora_A'], 'L1_ffn_gup_lora_B': _L1_ffn_in['gup_lora_B'], 'L1_ffn_down_lora_A': _L1_ffn_in['down_lora_A'], 'L1_ffn_down_lora_B': _L1_ffn_in['down_lora_B'], 'L2_xattn_Wq': _L2_xattn_in['Wq'], 'L2_xattn_bq': _L2_xattn_in['bq'], 'L2_xattn_Wk': _L2_xattn_in['Wk'], 'L2_xattn_bk': _L2_xattn_in['bk'], 'L2_xattn_Wv': _L2_xattn_in['Wv'], 'L2_xattn_bv': _L2_xattn_in['bv'], 'L2_ffn_gate_weight': _L2_ffn_in['gate_weight'], 'L2_ffn_gate_up_proj': _L2_ffn_in['gate_up_proj'], 'L2_ffn_down_proj': _L2_ffn_in['down_proj'], 'L2_ffn_similarity': _L2_ffn_in['similarity'], 'L3_ffn_Wr': _L3_ffn_in['Wr'], 'L3_ffn_U': _L3_ffn_in['U'], 'L3_ffn_V': _L3_ffn_in['V'], 'L3_ffn_attr': _L3_ffn_in['attr'], 'L3_ffn_Wa': _L3_ffn_in['Wa']}

def reference(x, ctx_2048, mask_BxSxS2_ff0, mask_BxS2_bk0, L0_xattn_decay, L0_xattn_W_in, L0_xattn_b_in, L0_xattn_W_out, L0_xattn_b_out, L0_xattn_gamma, L0_xattn_beta, L0_ffn_gate_weight, L0_ffn_gate_up_weights, L0_ffn_down_weights, L0_ffn_shared_gate_up, L0_ffn_shared_down, L1_ffn_gate_weight, L1_ffn_gate_lora_A, L1_ffn_gate_lora_B, L1_ffn_gate_up_proj, L1_ffn_down_proj, L1_ffn_gup_lora_A, L1_ffn_gup_lora_B, L1_ffn_down_lora_A, L1_ffn_down_lora_B, L2_xattn_Wq, L2_xattn_bq, L2_xattn_Wk, L2_xattn_bk, L2_xattn_Wv, L2_xattn_bv, L2_ffn_gate_weight, L2_ffn_gate_up_proj, L2_ffn_down_proj, L2_ffn_similarity, L3_ffn_Wr, L3_ffn_U, L3_ffn_V, L3_ffn_attr, L3_ffn_Wa):
    import jax
    import jax.numpy as jnp

    def _L0_xattn_ref(Z, kv, decay, W_in, b_in, W_out, b_out, gamma, beta):
        import jax, jax.numpy as jnp
        import numpy as np
        from jax import lax
        LN_EPS = 1e-05
        B, T, D = kv.shape
        K = jax.nn.sigmoid(decay)
        x = jnp.einsum('btd,ed->bte', kv, W_in) + b_in

        def scan_fn(s, xt):
            s = K * s + xt
            return (s, s)
        s0 = jnp.zeros((B, D), dtype=kv.dtype)
        _, states = lax.scan(scan_fn, s0, jnp.swapaxes(x, 0, 1))
        states = jnp.swapaxes(states, 0, 1)
        proj = jnp.einsum('btd,ed->bte', states, W_out) + b_out
        summary = jnp.mean(proj, axis=1, keepdims=True)
        y = Z + summary
        mu = jnp.mean(y, axis=-1, keepdims=True)
        var = jnp.mean((y - mu) ** 2, axis=-1, keepdims=True)
        return (y - mu) / jnp.sqrt(var + LN_EPS) * gamma + beta

    def _L0_ffn_ref(hidden_states, gate_weight, gate_up_weights, down_weights, shared_gate_up, shared_down):
        import jax, jax.numpy as jnp
        import numpy as np
        HIDDEN = 256
        FFN = 176
        N_EXPERTS = 16
        TOP_K = 4
        SHARED_FFN = 2 * FFN

        def _glu_ffn(x, gate_up, down):
            gu = x @ gate_up.T
            g, u = jnp.split(gu, 2, axis=-1)
            return jax.nn.silu(g) * u @ down.T
        orig_shape = hidden_states.shape
        x = hidden_states.reshape(-1, orig_shape[-1])
        scores = jax.nn.softmax(x @ gate_weight.T, axis=-1)
        topk_weight, topk_idx = jax.lax.top_k(scores, TOP_K)
        y = jnp.zeros_like(x)
        for e in range(N_EXPERTS):
            w_e = jnp.sum(jnp.where(topk_idx == e, topk_weight, 0.0), axis=-1)
            y = y + w_e[:, None] * _glu_ffn(x, gate_up_weights[e], down_weights[e])
        y = y + _glu_ffn(x, shared_gate_up, shared_down)
        return y.reshape(orig_shape)

    def _L1_xattn_ref(q, k, v):
        import math
        import jax, jax.numpy as jnp
        import numpy as np
        HEADS = 16
        MASKED_BIAS = -10000.0

        def _mha(q, k, v):
            B, Sq, D = q.shape
            Sk = k.shape[-2]
            hd = D // HEADS
            qh = q.reshape(B, Sq, HEADS, hd).transpose(0, 2, 1, 3)
            kh = k.reshape(B, Sk, HEADS, hd).transpose(0, 2, 1, 3)
            vh = v.reshape(B, Sk, HEADS, hd).transpose(0, 2, 1, 3)
            scores = jnp.einsum('bhqd,bhkd->bhqk', qh, kh) / math.sqrt(hd)
            qi = jnp.arange(Sq)[:, None] + (Sk - Sq)
            ki = jnp.arange(Sk)[None, :]
            causal = ki <= qi
            scores = jnp.where(causal[None, None], scores, jnp.asarray(MASKED_BIAS, scores.dtype))
            attn = jax.nn.softmax(scores, axis=-1)
            out = jnp.einsum('bhqk,bhkd->bhqd', attn, vh)
            return out.transpose(0, 2, 1, 3).reshape(B, Sq, D)
        return _mha(q, k, v)

    def _L1_ffn_ref(x, gate_weight, gate_lora_A, gate_lora_B, gate_up_proj, down_proj, gup_lora_A, gup_lora_B, down_lora_A, down_lora_B):
        import jax, jax.numpy as jnp
        import numpy as np
        TOP_K = 2
        SCALING = 2.0
        B, S, H = x.shape
        xf = x.reshape(-1, H)
        gate_delta = SCALING * (gate_lora_B @ gate_lora_A)
        router_logits = xf @ gate_weight.T + xf @ gate_delta.T
        probs = jax.nn.softmax(router_logits.astype(jnp.float32), axis=-1)
        routing_weights, selected = jax.lax.top_k(probs, TOP_K)
        routing_weights = routing_weights / routing_weights.sum(-1, keepdims=True)
        routing_weights = routing_weights.astype(xf.dtype)
        gup = jnp.einsum('th,eho->teo', xf, gate_up_proj)
        gup = gup + SCALING * jnp.einsum('ter,eor->teo', jnp.einsum('th,erh->ter', xf, gup_lora_A), gup_lora_B)
        gates, h = jnp.split(gup, 2, axis=-1)
        h = jax.nn.silu(gates) * h
        out = jnp.einsum('tei,eih->teh', h, down_proj)
        out = out + SCALING * jnp.einsum('ter,ehr->teh', jnp.einsum('tei,eri->ter', h, down_lora_A), down_lora_B)
        out_sel = jnp.take_along_axis(out, selected[:, :, None], axis=1)
        y = jnp.einsum('tkh,tk->th', out_sel, routing_weights)
        return y.reshape(B, S, H)

    def _L2_xattn_ref(x, attention_mask, k_cache, v_cache, Wq, bq, Wk, bk, Wv, bv):
        import jax, jax.numpy as jnp
        import numpy as np
        B, Q_LEN, E = (8, 16, 256)
        CACHE_LEN = 512
        Q = jnp.einsum('bqe,fe->bqf', x, Wq) + bq
        K_new = jnp.einsum('bqe,fe->bqf', x, Wk) + bk
        V_new = jnp.einsum('bqe,fe->bqf', x, Wv) + bv
        q_len = x.shape[1]
        end_step = attention_mask.shape[-1]
        past_kv_len = end_step - q_len
        k_cache = jax.lax.dynamic_update_slice(k_cache, K_new, (0, past_kv_len, 0))
        v_cache = jax.lax.dynamic_update_slice(v_cache, V_new, (0, past_kv_len, 0))
        K = k_cache[:, :end_step, :]
        V = v_cache[:, :end_step, :]
        scale = 1.0 / jnp.sqrt(jnp.asarray(Q.shape[-1], Q.dtype))
        scores = jnp.einsum('bqe,bke->bqk', Q, K) * scale + attention_mask
        attn = jax.nn.softmax(scores, axis=-1)
        return jnp.einsum('bqk,bke->bqe', attn, V)

    def _L2_ffn_ref(hidden_states, gate_weight, gate_up_proj, down_proj, similarity):
        import jax, jax.numpy as jnp
        import numpy as np
        NUM_EXPERTS = 32
        TOP_K = 8
        SELECT_TOP_K = 4
        THRESHOLD = 0.5
        HIDDEN = 256
        D_FF = 96

        def _moe_forward(hidden_states, gate_weight, gate_up_proj, down_proj, similarity):
            B, S_len, H = hidden_states.shape
            E, K, Ssel = (NUM_EXPERTS, TOP_K, SELECT_TOP_K)
            x = hidden_states.reshape(-1, H)
            router_logits = x @ gate_weight.T
            router_probs = jax.nn.softmax(router_logits.astype(jnp.float32), axis=-1).astype(router_logits.dtype)
            router_top_value, router_indices = jax.lax.top_k(router_probs, K)
            routing_weights = router_top_value / jnp.clip(jnp.sum(router_top_value, axis=-1, keepdims=True), 1e-12, None)
            sim = similarity.astype(jnp.float32)
            sim = sim.at[jnp.arange(E), jnp.arange(E)].set(1.0)
            prim = router_indices[:, :Ssel]
            sec = router_indices[:, Ssel:]
            sim_cand = sim[sec[:, :, None], prim[:, None, :]]
            best_sim = jnp.max(sim_cand, axis=-1)
            best_i = jnp.argmax(sim_cand, axis=-1)
            prim_rep = jnp.broadcast_to(prim[:, None, :], sim_cand.shape)
            best_primary = jnp.take_along_axis(prim_rep, best_i[..., None], axis=-1)[..., 0]
            new_sec = jnp.where(best_sim < THRESHOLD, sec, best_primary) if THRESHOLD > 0.0 else best_primary
            rerouted_indices = jnp.concatenate([prim, new_sec], axis=1)
            combine = jnp.sum(jax.nn.one_hot(rerouted_indices, E, dtype=routing_weights.dtype) * routing_weights[..., None], axis=1)

            def expert_step(y, params):
                wgu, wd, cw = params
                gu = x @ wgu.T
                g, u = jnp.split(gu, 2, axis=-1)
                h = jax.nn.silu(g) * u
                y = y + h @ wd.T * cw[:, None]
                return (y, None)
            y0 = jnp.zeros_like(x)
            y, _ = jax.lax.scan(expert_step, y0, (gate_up_proj, down_proj, combine.T))
            return y.reshape(B, S_len, H)
        return _moe_forward(hidden_states, gate_weight, gate_up_proj, down_proj, similarity)

    def _L3_xattn_ref(hidden_states, memory_tokens, memory_mask):
        import jax, jax.numpy as jnp
        import numpy as np
        B, S, D = hidden_states.shape
        scale = 1.0 / jnp.sqrt(jnp.asarray(D, hidden_states.dtype))
        scores = jnp.einsum('bsd,bmd->bsm', hidden_states, memory_tokens) * scale
        neg_inf = jnp.asarray(-1e+30, scores.dtype)
        scores = jnp.where(memory_mask[:, None, :], scores, neg_inf)
        attn = jax.nn.softmax(scores, axis=-1)
        readout = jnp.einsum('bsm,bmd->bsd', attn, memory_tokens)
        valid_b = jnp.any(memory_mask, axis=-1)
        out = jnp.where(valid_b[:, None, None], readout, jnp.zeros_like(readout))
        return out

    def _L3_ffn_ref(h, Wr, U, V, attr, Wa):
        import jax, jax.numpy as jnp
        import numpy as np
        TOPK = 2
        S = Wr.shape[0]
        sc = jnp.einsum('bth,sh->bts', h, Wr)
        _, idx = jax.lax.top_k(sc, TOPK)
        m = jax.nn.one_hot(idx, S, dtype=sc.dtype).sum(axis=-2)
        g = jax.nn.softmax(sc, axis=-1) * m
        g = g / (g.sum(axis=-1, keepdims=True) + 1e-08)
        hU = jnp.einsum('bth,shr->btsr', h, U)
        out = jnp.einsum('bts,btsr,srh->bth', g, hU, V)
        aw = jax.nn.sigmoid(attr @ Wa[0])
        gate = (g @ aw)[..., None]
        return out * (0.9 + 0.2 * gate)
    x = x + _L0_xattn_ref(_layernorm(x, axis=-1), ctx_2048, L0_xattn_decay, L0_xattn_W_in, L0_xattn_b_in, L0_xattn_W_out, L0_xattn_b_out, L0_xattn_gamma, L0_xattn_beta)
    x = x + _L0_ffn_ref(_layernorm(x, axis=-1), L0_ffn_gate_weight, L0_ffn_gate_up_weights, L0_ffn_down_weights, L0_ffn_shared_gate_up, L0_ffn_shared_down)
    x = x + _L1_xattn_ref(_layernorm(x, axis=-1), ctx_2048, ctx_2048)
    x = x + _L1_ffn_ref(_layernorm(x, axis=-1), L1_ffn_gate_weight, L1_ffn_gate_lora_A, L1_ffn_gate_lora_B, L1_ffn_gate_up_proj, L1_ffn_down_proj, L1_ffn_gup_lora_A, L1_ffn_gup_lora_B, L1_ffn_down_lora_A, L1_ffn_down_lora_B)
    x = x + _L2_xattn_ref(_layernorm(x, axis=-1), mask_BxSxS2_ff0, ctx_2048, ctx_2048, L2_xattn_Wq, L2_xattn_bq, L2_xattn_Wk, L2_xattn_bk, L2_xattn_Wv, L2_xattn_bv)
    x = x + _L2_ffn_ref(_layernorm(x, axis=-1), L2_ffn_gate_weight, L2_ffn_gate_up_proj, L2_ffn_down_proj, L2_ffn_similarity)
    x = x + _L3_xattn_ref(_layernorm(x, axis=-1), ctx_2048, mask_BxS2_bk0)
    x = x + _L3_ffn_ref(_layernorm(x, axis=-1), L3_ffn_Wr, L3_ffn_U, L3_ffn_V, L3_ffn_attr, L3_ffn_Wa)
    return x

_drawn_inputs = setup_inputs


def setup_inputs(seed=0):
    import zlib

    import numpy as np

    out = dict(_drawn_inputs(seed))
    spreads = {'L0_xattn_b_in': (0.0, 0.1),
     'L0_xattn_b_out': (0.0, 0.1),
     'L0_xattn_gamma': (1.0, 0.2),
     'L0_xattn_beta': (0.0, 0.1)}
    factors = {'L0_ffn_gate_weight': 8.0,
     'L0_ffn_gate_up_weights': 8.0,
     'L0_ffn_down_weights': 8.0,
     'L0_ffn_shared_gate_up': 3.51,
     'L0_ffn_shared_down': 4.064,
     'L1_ffn_gup_lora_A': 4.67,
     'L1_ffn_gup_lora_B': 4.675,
     'L1_ffn_down_lora_A': 8.0,
     'L1_ffn_down_lora_B': 8.0,
     'L2_xattn_bq': 8.0,
     'L2_xattn_Wk': 7.922,
     'L2_xattn_bk': 64.0,
     'L2_xattn_Wv': 5.486,
     'L2_xattn_bv': 8.0,
     'L2_ffn_gate_weight': 8.0,
     'L2_ffn_gate_up_proj': 8.0,
     'L2_ffn_down_proj': 8.0,
     'L2_ffn_similarity': 8.0,
     'L3_ffn_Wr': 8.0,
     'L3_ffn_U': 8.0,
     'L3_ffn_V': 8.0,
     'L3_ffn_attr': 64.0,
     'L3_ffn_Wa': 64.0}
    for name, (base, spread) in spreads.items():
        noise = np.random.default_rng([zlib.crc32(name.encode()), seed]).standard_normal(out[name].shape)
        drawn = base * np.exp(spread * noise) if base else spread * noise
        out[name] = jnp.asarray(drawn.astype(out[name].dtype))
    for name, factor in factors.items():
        out[name] = (out[name] * factor).astype(out[name].dtype)
    return out
```

```python
from contextlib import ExitStack

import numpy as np

import concourse.bass as bass
from concourse import mybir

F32 = mybir.dt.float32
BF16 = mybir.dt.bfloat16
U32 = mybir.dt.uint32
U8 = mybir.dt.uint8
ACT = mybir.ActivationFunctionType
ALU = mybir.AluOpType
AX = mybir.AxisListType

B, Q, D, T = 8, 100, 256, 1444
TOK = B * Q
DM = D // 128
HT = TOK // 2
PAST = T - Q
HEADS, HD = 16, 16
SETS, GRP, PAD = 4, 4, 32
VW = HD + 1
LN_EPS = 1e-5
FAR = -1.0e30
FULL = PAST // 128
NCH = 12
CA = (T - FULL * 128) // 2
CB = (PAST - FULL * 128, Q)
AW = T // 3 + 1
A0 = (0, T // 3, T - AW)


class Ffn:

    def __init__(self, name, experts, top, chunks, shared=0, gated=True):
        self.name, self.E, self.K, self.C, self.shared, self.gated = name, experts, top, chunks, shared, gated
        self.rep = 128 // experts
        self.cols = DM * (2 if gated else 1) * 128


FFN0 = Ffn("l0", 16, 4, 25, shared=3)
FFN1 = Ffn("l1", 8, 2, 8)
FFN2 = Ffn("l2", 32, 8, 24)
FFN3 = Ffn("l3", 32, 2, 4, gated=False)


NORMS = ("n0", "n1", "n2", "n3", "n4", "n5", "n6", "n7", "n8")
TURNED = ("n2", "n4", "n5", "n6", "n7", "n8")
ROUTERS = ("l0", "l1r", "l2r", "l3r")


def xn_count(name, b=B):
    return NORMS.index(name) * B + b


def tr_count(name, b):
    return TURNED.index(name) * B + b


def xnT_count(name):
    return TURNED.index(name) * 4 + 4


def w_count(r):
    return ROUTERS.index(r) * 2 + 2


class Chain:

    def __init__(self, eng, sem):
        self.eng, self.sem, self.n, self.base = eng, sem, 0, 0

    def add(self, ins):
        ins.then_inc(self.sem, 1)
        self.n += 1

    def wait(self):
        self.eng.wait_ge(self.sem, self.base + self.n)

    def link(self, ins):
        self.add(ins)
        self.wait()

    def enter(self, i, first, per):
        self.base = (i - first) * per
        self.n0 = self.n

    def leave(self, turns, per):
        assert self.n - self.n0 == per, (self.n - self.n0, per)
        self.n = self.n0 + turns * per
        self.base = 0


def build(nc, d, out):
    ctx = ExitStack()
    with ctx:
        def sb(name, shape, dt=F32):
            return ctx.enter_context(nc.sbuf_tensor("sb_" + name, shape, dt))

        sems = {}

        def sem(name):
            if name not in sems:
                sems[name] = ctx.enter_context(nc.semaphore(name))
            return sems[name]

        x = sb("x", [Q, B, D])
        xn = sb("xn", [Q, B, D])
        xnT = sb("xnT", [128, DM, TOK])
        yT = sb("yT", [128, DM, TOK])
        ident = sb("ident", [128, 128])
        flip = sb("flip", [128, 128])
        identb = sb("identb", [Q, Q], BF16)
        farb = sb("farb", [Q, Q], BF16)
        iota = sb("iota", [Q, 32])
        mhalf = sb("mhalf", [Q, B])
        Wb = sb("Wb", [128, TOK])
        stat = sb("stat", [Q, B, 6])
        mv = sb("mv", [Q, B, 2])
        rstd = sb("rstd", [Q, B])
        wgu = [sb(f"wgu{i}", [128, FFN0.cols]) for i in range(2)]
        wd = [sb(f"wd{i}", [128, D]) for i in range(2)]
        sg = [sb(f"sg{i}", [128, HT]) for i in range(2)]
        hb = [sb(f"hb{i}", [128, HT]) for i in range(2)]
        gate = {0: sb("gate0", [128, DM, 16]), 1: sb("gate1", [128, DM, 8]),
                2: sb("gate2", [128, DM, 32]), 3: sb("gate3", [128, DM, 32])}
        awcol = sb("awcol", [128, 1])
        awmat = sb("awmat", [128, 128])
        simb = sb("simb", [128, 128])
        arena = sb("arena", [128, 38912])
        parts = nc.dram_tensor("parts", (3, B, D, T), BF16).ap()
        merged_gu = nc.dram_tensor("merged_gu", (FFN1.C, 128, FFN1.cols), F32).ap()
        merged_dn = nc.dram_tensor("merged_dn", (FFN1.C, 128, D), F32).ap()

        def ar(at, n, p=128):
            return arena[0:p, at:at + n]

        ps = ctx.enter_context(nc.psum_tensor("ps", [128, 8, 512], F32))

        ct = [ar(1444 * i, T) for i in range(3)]
        part = [ar(4332 + 2166 * i, 2166).bitcast(BF16).rearrange("p (t k) -> p t k", t=3) for i in range(3)]
        rest = [ar(10830 + 1444 * i, T) for i in range(2)]
        crow = ar(13718, T)
        krow = ar(15162, T)
        orow = ar(16606, T)
        prod = ar(18050, T)
        dk = ar(19850, 2)
        csum = ar(19840, 2)
        wkv = ar(19850, DM * B).rearrange("p (m b) -> p m b", m=DM)
        s1 = ar(19870, DM * B).rearrange("p (m b) -> p m b", m=DM)
        s1r = ar(19900, DM * B * Q).rearrange("p (m b q) -> p m b q", m=DM, b=B)
        winT = ar(21600, DM * D).rearrange("p (m e) -> p m e", m=DM)
        woutT = ar(22200, DM * D).rearrange("p (m e) -> p m e", m=DM)
        bin_c = ar(22800, DM)
        bout_b = ar(22810, D, Q)
        gam_b = ar(23070, D, Q)
        bet_b = ar(23330, D, Q)
        ones1 = ar(23600, 128)
        agup = ar(23800, D)
        bblk = ar(24060, 2048).rearrange("p (c n) -> p c n", c=FFN1.C)
        adn = ar(26110, 1024).rearrange("p (c n) -> p c n", c=FFN1.C)
        bdn = ar(27140, D)
        glA = ar(27400, D, 16)
        glB = ar(27660, 8, 16)
        sim1 = ar(27700, 32, 32)
        attr_r = ar(27740, 32)
        wa_b = ar(27780, 32)
        aw_t = ar(27820, 32)
        mgu = ar(31000, FFN1.C * FFN1.cols).rearrange("p (c n) -> p c n", c=FFN1.C)
        mdn = ar(31000 + FFN1.C * FFN1.cols, FFN1.C * D).rearrange("p (c n) -> p c n", c=FFN1.C)
        rl = ar(28000, B * 32, Q)
        rp = ar(28260, B * 32, Q)
        rmx = ar(28520, B, Q)
        rsum = ar(28530, B, Q)
        v8 = ar(28540, B * 8, Q).rearrange("p (b k) -> p b k", b=B)
        i8 = ar(28610, B * 8, Q).bitcast(U32).rearrange("p (b k) -> p b k", b=B)
        if8 = ar(28680, B * 8, Q).rearrange("p (b k) -> p b k", b=B)
        rw = ar(28750, B * 32, Q)
        rsel = ar(29010, B * 32, Q)
        wrep = ar(29270, B * 128, Q).rearrange("p (b n) -> p b n", b=B)
        oh = ar(0, B * 8 * 32, Q)
        cand = ar(2100, B * 16 * 32, Q)
        pick = ar(6300, B * 16, Q).rearrange("p (b j i) -> p b j i", b=B, j=4)
        first = ar(6440, B * 16, Q).rearrange("p (b j i) -> p b j i", b=B, j=4)
        left = ar(6580, B * 4, Q).rearrange("p (b j) -> p b j", b=B)
        best = ar(6620, B * 4, Q).rearrange("p (b j) -> p b j", b=B)
        keep = ar(6660, B * 4, Q).rearrange("p (b j) -> p b j", b=B)
        moved = ar(6700, B * 4, Q).rearrange("p (b j) -> p b j", b=B)
        w8 = ar(6740, B * 8, Q).rearrange("p (b k) -> p b k", b=B)
        secT = ar(6810, TOK)
        scand = ar(7700, B * 128, Q)
        kstk = [ar(11552 * i, 11552).bitcast(BF16).rearrange("p (h k) -> p h k", h=HEADS) for i in range(2)]
        vnat = ar(23104, 3072).rearrange("p (c d) -> p c d", c=NCH)
        vaug = [ar(26176 + 3264 * i, 3264).rearrange("p (c h v) -> p c h v", c=NCH, h=HEADS) for i in range(2)]
        pr = [ar(32704 + 1200 * i, 1200).rearrange("p (c q) -> p c q", c=NCH) for i in range(2)]
        qs = [ar(35104 + 800 * i, 800).bitcast(BF16).rearrange("p (h q) -> p h q", h=HEADS) for i in range(2)]
        xs = [ar(36704 + 768 * i, 768, Q).bitcast(BF16).rearrange("p (h t r) -> p h t r", h=HEADS, t=6) for i in range(2)]
        xr = ar(38240, D, Q).rearrange("p (h r) -> p h r", h=HEADS)
        nm = [ar(38496 + 8 * i, 8, Q).bitcast(BF16) for i in range(2)]
        ot = ar(38512, SETS * Q)
        den = sb("den", [Q, HEADS])
        att = sb("att", [Q, HEADS, HD])
        ctT = [ar(2888 * i, 2888).rearrange("p (m k) -> p m k", m=DM) for i in range(2)]
        vn2 = [ar(5776 + 3072 * i, 3072).rearrange("p (c d) -> p c d", c=NCH) for i in range(2)]
        bias = [ar(11920 + T * i, T, Q) for i in range(2)]
        sc = ar(14808, T, Q)
        pb = [ar(16252, T, Q), ar(27000, T, Q)]
        mk8 = [ar(17700 + 361 * i, 361, Q).bitcast(U8) for i in range(2)]
        ptt = ar(18500, 1200).rearrange("p (c q) -> p c q", c=NCH)
        qst = [ar(20900 + 200 * i, 200).rearrange("p (m q) -> p m q", m=DM) for i in range(2)]
        knT = ar(21300, DM * TOK).rearrange("p (m t) -> p m t", m=DM)
        vnew = ar(22900, B * D, Q).rearrange("p (b d) -> p b d", b=B)
        wqkv = ar(24950, 3 * 512).rearrange("p (w m e) -> p w m e", w=3, m=DM)
        bqk = ar(26500, 4).rearrange("p (w m) -> p w m", w=2)
        bv_b = ar(26510, D, Q)
        nmx = ar(26770, 1, Q)
        ssum = ar(26772, 1, Q)
        rsm = ar(26774, 1, Q)
        anym = [ar(26776 + 2 * i, 1, Q) for i in range(2)]

        block = ctx.enter_context(nc.Block())

        def v_load(eng, b):
            eng.dma_start(vnat[:, 0:FULL, :], d["ctx"][bass.ds(b, 1), 0:FULL * 128, :]
                          .rearrange("a (c p) d -> p (a c) d", p=128)).then_inc(sem("in_vnat"), 16)
            eng.dma_start(vnat[0:CA, FULL:NCH, :], d["ctx"][bass.ds(b, 1), FULL * 128:T, :]
                          .rearrange("a (c p) d -> p (a c) d", p=CA)).then_inc(sem("in_vnat"), 16)

        def stack_loads(eng, b, k, s):
            h = slice(GRP * s, GRP * s + GRP)
            at = 0
            for n in (3, 2, 1):
                for t in range(n):
                    src = parts[t, bass.ds(b, 1), GRP * HD * s:GRP * HD * (s + 1), :].rearrange("a (h r) k -> (a r) h k", r=HD)
                    eng.dma_start(kstk[k][at:at + HD, h, :], src).then_inc(sem(f"in_stk{k}{s}"), 16)
                    at += HD

        @block.sync
        def _(sp):
            def load(name, dst, src, **kw):
                sp.dma_start(dst, src, **kw).then_inc(sem(name), 16)

            load("in_x", x[:, :, :], d["x"].rearrange("b q d -> q b d"))
            load("in_const", ident[:, :], d["ident"])
            load("in_const", flip[:, :], d["flip"])
            load("in_const", iota[:, :], d["iota"].partition_broadcast(Q))
            load("in_decay", dk[:, 0:1], d["decay"].partition_broadcast(128))
            load("in_l0w", winT, d["winT"].rearrange("(m p) e -> p m e", p=128))
            load("in_l0w", woutT, d["woutT"].rearrange("(m p) e -> p m e", p=128))
            load("in_l0w", bin_c, d["b_in"])
            load("in_l0w", bout_b, d["b_out"].partition_broadcast(Q))
            load("in_l0w", gam_b, d["gamma"].partition_broadcast(Q))
            load("in_l0w", bet_b, d["beta"].partition_broadcast(Q))
            for n in range(4):
                load("in_gate", gate[n][:, :, :], d[f"gate{n}T"].rearrange("(m p) e -> p m e", p=128))

            def ct_load(u):
                sp.dma_start(ct[u % 3], d["ctxT"][u // DM, (u % DM) * 128:(u % DM) * 128 + 128, :]).then_inc(sem(f"in_ct{u % 3}"), 16)

            for u in range(3):
                ct_load(u)
            load("in_lora", mgu[:, :, :], d["l1_gu"].rearrange("c p n -> p c n"))
            load("in_lora", mdn[:, :, :], d["l1_dn"].rearrange("c p n -> p c n"))
            load("in_lora", agup, d["gupA"])
            load("in_lora", bdn, d["dnB"])
            load("in_lora", glA, d["glA"])
            load("in_lora", glB, d["glB"])
            load("in_lora", sim1, d["sim"])
            load("in_lora", attr_r, d["attr"])
            load("in_lora", wa_b, d["Wa"].partition_broadcast(128))
            sp.wait_ge(sem("zeroed"), 4)
            for e in range(8):
                s = slice(16 * e, 16 * e + 16)
                load("in_blk", bblk[s, :, :].rearrange("p c (g n) -> p c g n", g=2)[:, :, :, s],
                     d["gupB"][e].rearrange("r c g f -> r c g f"))
                load("in_blk", adn[s, :, s], d["dnA"][e])
            for j in range(4):
                load("in_blk", simb[32 * j:32 * j + 32, 32 * j:32 * j + 32], d["sim"])
            for u in range(DM * B):
                sp.wait_ge(sem("kl_done"), u + 1)
                sp.dma_start(parts[:, u // DM, (u % DM) * 128:(u % DM) * 128 + 128, :].rearrange("t p k -> p t k"), part[u % 3])\
                    .then_inc(sem(f"parts_out{u % 3}"), 16)
                if u + 3 < DM * B:
                    sp.wait_ge(sem("rest_done"), u + 1)
                    ct_load(u + 3)
            sp.wait_ge(sem("merged"), 2 * FFN1.C)
            sp.dma_start(merged_gu.rearrange("c p n -> p c n"), mgu).then_inc(sem("merged_out"), 16)
            sp.dma_start(merged_dn.rearrange("c p n -> p c n"), mdn).then_inc(sem("merged_out"), 16)

            def ffn_loads(f, gu, dn):
                def chunk(c, k):
                    if k is None:
                        k = c % 2
                    if not isinstance(c, int) or c >= 2:
                        sp.wait_ge(sem(f.name + "_gu_done"), 2 * c - 2)
                    sp.dma_start(wgu[k][:, 0:f.cols], gu(c)).then_inc(sem(f"{f.name}_wgu{k}"), 16)
                    if not isinstance(c, int) or c >= 2:
                        sp.wait_ge(sem(f.name + "_down_done"), 2 * c - 2)
                    sp.dma_start(wd[k][:, :], dn(c)).then_inc(sem(f"{f.name}_wd{k}"), 16)

                head = 3 if f.C % 2 else 2
                for c in range(head):
                    chunk(c, None)
                if f.C - head > 2:
                    with sp.Fori(0, (f.C - head) // 2) as i:
                        c = i * 2 + head
                        chunk(c, head % 2)
                        chunk(c + 1, (head + 1) % 2)
                else:
                    for c in range(head, f.C):
                        chunk(c, None)

            def dram_chunks(name):
                return (lambda c: d[name + "_gu"][bass.ds(c, 1), :, :].rearrange("a p n -> p (a n)"),
                        lambda c: d[name + "_dn"][bass.ds(c, 1), :, :].rearrange("a p n -> p (a n)"))

            ffn_loads(FFN0, *dram_chunks("l0"))

            sp.wait_ge(sem("l1_vfree"), 1)
            v_load(sp, 1)
            with sp.Fori(0, (B - 2) // 2) as i:
                for k in range(2):
                    b = i * 2 + (k + 2)
                    sp.wait_ge(sem("l1_vfree"), b)
                    sp.sem_inc(sem("sp_turns"), 1)
                    v_load(sp, b)
                    for s in range(SETS):
                        sp.wait_ge(sem("l1_sc"), b * (3 * HEADS) + 3 * GRP * (s + 1))
                        sp.sem_inc(sem("sp_turns"), 1)
                        stack_loads(sp, b, k, s)

            sp.wait_ge(sem("merged_out"), 32)
            ffn_loads(FFN1, lambda c: merged_gu[bass.ds(c, 1), :, :].rearrange("a p n -> p (a n)"),
                      lambda c: merged_dn[bass.ds(c, 1), :, :].rearrange("a p n -> p (a n)"))

            def single_loads(name, b, k, masked):
                sp.wait_ge(sem(name + "_o"), b + 1)
                sp.dma_start(ctT[k][:, :, :], d["ctxT"][bass.ds(b, 1), :, :].rearrange("a (m p) k -> p (a m) k", p=128))\
                    .then_inc(sem(f"{name}_in{k}"), 16)
                sp.dma_start(vn2[k][:, 0:FULL, :], d["ctx"][bass.ds(b, 1), 0:FULL * 128, :]
                             .rearrange("a (c p) d -> p (a c) d", p=128)).then_inc(sem(f"{name}_in{k}"), 16)
                at = FULL * 128
                for j, n in enumerate(CB):
                    sp.dma_start(vn2[k][0:n, FULL + j, :], d["ctx"][bass.ds(b, 1), at:at + n, :]
                                 .rearrange("a p d -> p (a d)")).then_inc(sem(f"{name}_in{k}"), 16)
                    at += n
                if masked:
                    sp.dma_start(bias[k], d["mask"][bass.ds(b, 1), :, :].rearrange("a q k -> q (a k)"))\
                        .then_inc(sem(f"{name}_in{k}"), 16)
                else:
                    sp.dma_start(mk8[k], d["bkmask"][bass.ds(b, 1), :].rearrange("a k -> (a k)").partition_broadcast(Q))\
                        .then_inc(sem(f"{name}_in{k}"), 16)

            sp.wait_ge(sem("w_ready"), w_count("l1r"))
            load("in_qkv", wqkv[:, :, :, :], d["wqkvT"].rearrange("w (m p) e -> p w m e", p=128))
            load("in_qkv", bqk[:, :, :], d["bqk"])
            load("in_qkv", bv_b, d["bv"].partition_broadcast(Q))
            with sp.Fori(0, B // 2) as i:
                b = i * 2
                single_loads("l2a", b, 0, True)
                single_loads("l2a", b + 1, 1, True)
            ffn_loads(FFN2, *dram_chunks("l2"))
            sp.wait_ge(sem("w_ready"), w_count("l2r"))
            with sp.Fori(0, B // 2) as i:
                b = i * 2
                single_loads("l3a", b, 0, False)
                single_loads("l3a", b + 1, 1, False)
            ffn_loads(FFN3, *dram_chunks("l3"))
            for j in range(4):
                sp.wait_ge(sem("l3_x"), j + 1)
                sp.dma_start(out[2 * j:2 * j + 2, :, :].rearrange("b q d -> q b d"), x[:, 2 * j:2 * j + 2, :])\
                    .then_inc(sem("out_done"), 16)
            sp.wait_ge(sem("out_done"), 64)

        @block.gpsimd
        def _(pool):
            ch = Chain(pool, sem("pool_own"))

            def wait_register(name, value):
                pool.wait_ge(sem(name), value)
                pool.sem_inc(sem("pool_turns"), 1)

            pool.memset(mhalf[:, :], -0.5).then_inc(sem("mhalf_set"), 1)
            pool.memset(bblk[:, :, :], 0.0).then_inc(sem("zeroed"), 1)
            pool.memset(adn[:, :, :], 0.0).then_inc(sem("zeroed"), 1)
            pool.memset(simb[:, :], 0.0).then_inc(sem("zeroed"), 1)
            pool.memset(ones1, 1.0).then_inc(sem("zeroed"), 1)
            pool.memset(ot, 0.0).then_inc(sem("zeroed"), 1)
            pool.wait_ge(sem("in_const"), 48)
            ch.link(pool.tensor_copy(identb[:, :], ident[0:Q, 0:Q]))
            ch.link(pool.memset(farb[:, :], 0.0))
            pool.affine_select(out=farb[:, :], in_=farb[:, :], pattern=[[-1, Q]], compare_op=ALU.is_ge, fill=FAR,
                               base=0, channel_multiplier=1).then_inc(sem("far_ready"), 1)

            def norm(name):
                pool.wait_ge(sem("stat"), NORMS.index(name) + 1)
                ch.link(pool.tensor_scalar(rstd[:, :], mv[:, :, 1], LN_EPS, None, ALU.add))
                pool.tensor_tensor(rstd[:, :], rstd[:, :], mhalf[:, :], ALU.pow).then_inc(sem("rstd"), 1)
                pool.wait_ge(sem("rstd"), NORMS.index(name) + 1)

            pool.wait_ge(sem("mhalf_set"), 1)

            def prepare_queries(b, k):
                pool.wait_ge(sem("l1_q"), b * 6 + 3)
                src = xn[:, bass.ds(b, 1), :].rearrange("q a (h r) -> q (a h) r", h=HEADS)
                at = 0 if isinstance(b, int) else b
                pool.tensor_copy(xs[k][:, :, 0:3, :], src.unsqueeze(2).broadcast_to([Q, HEADS, 3, HD])).then_inc(sem("l1_xs"), 1)
                wait_register("l1_xs", b * 4 + 1)
                pool.tensor_tensor(xr, src, xs[k][:, :, 0, :], ALU.subtract).then_inc(sem("l1_xs"), 1)
                wait_register("l1_xs", b * 4 + 2)
                pool.tensor_copy(xs[k][:, :, 3:5, :], xr.unsqueeze(2).broadcast_to([Q, HEADS, 2, HD])).then_inc(sem("l1_xs"), 1)
                wait_register("l1_xs", b * 4 + 3)
                pool.tensor_tensor(xs[k][:, :, 5, :], xr, xs[k][:, :, 3, :], ALU.subtract).then_inc(sem("l1_xs"), 1)
                wait_register("l1_xs", b * 4 + 4)

            def copy_values(b, k, c):
                if c == 0:
                    wait_register("in_vnat", b * 32 + 32)
                    wait_register("l1_out", b + 1)
                n = 128 if c < FULL else CA
                pool.tensor_copy(vaug[k][0:n, c, :, 0:HD], vnat[0:n, c, :].rearrange("p (h v) -> p h v", h=HEADS))\
                    .then_inc(sem("l1_vaug"), 1)
                if c == NCH - 1:
                    pool.wait_ge(sem("l1_vaug"), b * NCH + NCH)
                    pool.sem_inc(sem("l1_vfree"), 1)

            def masks(b, nk):
                for h in range(HEADS):
                    wait_register("l1_exp", (b * HEADS + h) * 4 + 8)
                    tail = pr[h % 2][0:CA, FULL:NCH, :]
                    pool.affine_select(out=tail, in_=tail, pattern=[[-CA, 2], [1, Q]], compare_op=ALU.is_ge, fill=0.0,
                                       base=PAST - FULL * 128, channel_multiplier=-1).then_inc(sem("l1_masked"), 1)
                    if nk is not None and h < NCH:
                        copy_values(b + 1, nk, h)

            for u in range(DM * B):
                pool.wait_ge(sem("km_done"), u + 1)
                pool.tensor_tensor(part[u % 3][:, 2, :], rest[u % 2], part[u % 3][:, 1, :], ALU.subtract).then_inc(sem("kl_done"), 1)
            norm("n0")
            norm("n1")
            norm("n2")
            pool.wait_ge(sem("w_ready"), w_count("l0"))
            for n in range(3):
                pool.wait_ge(sem(f"parts_out{n}"), 16 * ((DM * B + 2 - n) // 3))
            pool.wait_ge(sem("merged_out"), 32)
            for k in range(2):
                pool.memset(kstk[k][96:97, :, :], 1.0).then_inc(sem("stack_ones"), 1)
                pool.wait_ge(sem("stack_ones"), k + 1)
            for k in range(2):
                pool.memset(vaug[k][:, :, :, HD], 1.0).then_inc(sem("value_ones"), 1)
                pool.wait_ge(sem("value_ones"), k + 1)
            pool.wait_ge(sem("in_vnat"), 32)
            for c in range(NCH):
                copy_values(0, 0, c)
            norm("n3")
            pool.wait_ge(sem("xn"), xn_count("n3"))
            prepare_queries(0, 0)
            prepare_queries(1, 1)
            with pool.Fori(0, (B - 2) // 2) as i:
                b = i * 2
                prepare_queries(b + 2, 0)
                masks(b, 1)
                prepare_queries(b + 3, 1)
                masks(b + 1, 0)
            masks(B - 2, 1)
            masks(B - 1, None)
            norm("n4")
            norm("n5")

            def stage_queries(name, src, b, k):
                wait_register(name + "_sc", b + 1)
                pool.tensor_copy(qst[k][:, :, :], src[:, :, bass.ds(b * Q, Q)]).then_inc(sem(name + "_q"), 1)

            pool.wait_ge(sem("l2a_qT"), 4)
            with pool.Fori(0, B // 2) as i:
                b = i * 2
                stage_queries("l2a", yT, b, 0)
                stage_queries("l2a", yT, b + 1, 1)
            norm("n6")
            norm("n7")
            pool.wait_ge(sem("xnT"), xnT_count("n7"))

            with pool.Fori(0, B // 2) as i:
                b = i * 2
                stage_queries("l3a", xnT, b, 0)
                stage_queries("l3a", xnT, b + 1, 1)
            norm("n8")

        @block.scalar
        def _(act):
            ch = Chain(act, sem("act_own"))
            act.wait_ge(sem("in_decay"), 16)
            act.activation(dk[:, 1:2], dk[:, 0:1], ACT.Sigmoid).then_inc(sem("decayed"), 1)
            act.sem_inc(sem("l1_exp"), 4)
            act.sem_inc(sem("l1_q"), 13)
            for u in range(DM * B + 1):
                if u < DM * B:
                    act.wait_ge(sem(f"in_ct{u % 3}"), 16 * (u // 3 + 1))
                    if u >= 3:
                        act.wait_ge(sem(f"parts_out{u % 3}"), 16 * (u // 3))
                    act.activation(part[u % 3][:, 0, :], ct[u % 3], ACT.Copy).then_inc(sem("kh_done"), 1)
                if u:
                    act.wait_ge(sem("rest_done"), u)
                    act.activation(part[(u - 1) % 3][:, 1, :], rest[(u - 1) % 2], ACT.Copy).then_inc(sem("km_done"), 1)
            act.wait_ge(sem("aw_dot"), 1)
            act.activation(awcol[:, :], aw_t[:, 0:1], ACT.Sigmoid).then_inc(sem("aw_sig"), 1)

            def transposed(name, dst=xnT):
                for j in range(2):
                    for m in range(DM):
                        act.wait_ge(sem("tr"), tr_count(name, 4 * (j + 1)))
                        act.activation(dst[:, m, j * HT:(j + 1) * HT], ps[:, 2 * j + m, 0:HT], ACT.Copy)\
                            .then_inc(sem("xnT"), 1)

            def router(r, f):
                act.wait_ge(sem("r_shift"), ROUTERS.index(r) + 1)
                act.activation(rp[:, 0:B * f.E], rp[:, 0:B * f.E], ACT.Exp).then_inc(sem("r_exp"), 1)
                for j in range(2):
                    act.wait_ge(sem("r_wT"), ROUTERS.index(r) * B + 4 * (j + 1))
                    act.activation(Wb[:, j * HT:(j + 1) * HT], ps[:, 5 + j, 0:HT], ACT.Copy)\
                        .then_inc(sem("w_ready"), 1)

            def ffn(f):
                def unit(c, hf):
                    act.wait_ge(sem(f.name + "_gu_done"), 2 * c + (hf + 1))
                    act.activation(sg[hf][:, :], ps[:, 2 * hf, 0:HT], ACT.Silu).then_inc(sem(f.name + "_silu"), 1)

                if f.gated:
                    head = 3 if f.C % 2 else 2
                    for c in range(head):
                        for hf in range(2):
                            unit(c, hf)
                    with act.Fori(head, f.C, 1) as c:
                        for hf in range(2):
                            unit(c, hf)
                for m in range(DM):
                    act.wait_ge(sem(f.name + "_down_done"), 2 * f.C)
                    act.activation(yT[:, m, 0:HT], ps[:, 4 + 2 * m, 0:HT], ACT.Copy).then_inc(sem(f.name + "_yT"), 1)

            transposed("n2")
            router("l0", FFN0)
            act.wait_ge(sem("w_ready"), w_count("l0"))
            for n in range(3):
                act.wait_ge(sem(f"parts_out{n}"), 16 * ((DM * B + 2 - n) // 3))
            act.wait_ge(sem("merged_out"), 32)
            v_load(act, 0)
            for k in range(2):
                for s in range(SETS):
                    stack_loads(act, k, k, s)
            ffn(FFN0)

            def query_copies(b, k):
                for n in range(2):
                    act.wait_ge(sem("l1_qtr"), b * 2 + (n + 1))
                    act.activation(qs[k][0:96, 8 * n:8 * n + 8, :],
                                   ps[0:96, 7, :].bitcast(BF16)[:, 0:8 * Q].rearrange("p (h q) -> p h q", h=8), ACT.Copy)\
                        .then_inc(sem("l1_q"), 1)

            def max_copy(b, k, s):
                act.wait_ge(sem("l1_mtr"), b * SETS + (s + 1))
                act.activation(qs[k][96:97, GRP * s:GRP * s + GRP, :],
                               ps[96:97, 7, 0:GRP * Q].rearrange("p (h q) -> p h q", h=GRP), ACT.Copy).then_inc(sem("l1_q"), 1)

            def exps(b, h):
                n = b * HEADS + h
                act.wait_ge(sem("l1_pv"), n + 1)
                for j in range(3):
                    act.wait_ge(sem("l1_sc"), n * 3 + (j + 1 + 6 * HEADS))
                    for c0, c1, rows in (((0, 4, 128),), ((4, 8, 128),), ((8, 10, 128), (10, 12, CA)))[j]:
                        act.activation(pr[h % 2][0:rows, c0:c1, :],
                                       ps[0:rows, 3 + j, (c0 - 4 * j) * Q:(c1 - 4 * j) * Q].rearrange("p (c q) -> p c q", q=Q),
                                       ACT.Exp, scale=HD ** -0.5).then_inc(sem("l1_exp"), 1)

            def batch(b, k, ahead):
                if ahead:
                    query_copies(b + 1, 1 - k)
                for h in range(HEADS):
                    if ahead and h and h % GRP == 0:
                        max_copy(b + 1, 1 - k, h // GRP - 1)
                    exps(b, h)
                act.wait_ge(sem("l1_pv"), b * HEADS + (HEADS + 2))
                for g in range(GRP):
                    act.activation(ot[32 * g:32 * g + VW, :], ps[32 * g:32 * g + VW, 6, 0:SETS * Q], ACT.Copy).then_inc(sem("l1_ot"), 1)
                if ahead:
                    max_copy(b + 1, 1 - k, SETS - 1)

            query_copies(0, 0)
            for s in range(SETS):
                max_copy(0, 0, s)
            with act.Fori(0, (B - 2) // 2) as i:
                batch(i * 2, 0, True)
                batch(i * 2 + 1, 1, True)
            batch(B - 2, 0, True)
            batch(B - 1, 1, False)

            transposed("n4")
            router("l1r", FFN1)
            ffn(FFN1)
            transposed("n5")

            def single(name):
                act.sem_inc(sem(name + "_pt"), 3)

                def body(b, k):
                    act.wait_ge(sem(name + "_max"), b + 1)
                    act.activation(pb[k], sc, ACT.Exp, bias=nmx, accum_out=ssum).then_inc(sem(name + "_exp"), 1)
                    for j in range(3):
                        act.wait_ge(sem(name + "_ptr"), b * 3 + (j + 1))
                        if j < 2:
                            act.activation(ptt[:, 4 * j:4 * j + 4, :],
                                           ps[:, 3 + j, 0:4 * Q].rearrange("p (c q) -> p c q", c=4), ACT.Copy)\
                                .then_inc(sem(name + "_pt"), 1)
                        else:
                            ch.add(act.activation(ptt[:, 8:10, :],
                                                  ps[:, 5, 0:2 * Q].rearrange("p (c q) -> p c q", c=2), ACT.Copy))
                            ch.add(act.activation(ptt[0:CB[0], 10, :], ps[0:CB[0], 5, 2 * Q:3 * Q], ACT.Copy))
                            act.activation(ptt[0:CB[1], 11, :], ps[0:CB[1], 5, 3 * Q:4 * Q], ACT.Copy)\
                                .then_inc(sem(name + "_pt"), 1)

                with act.Fori(0, B // 2) as i:
                    b = i * 2
                    ch.enter(i, 0, 4)
                    body(b, 0)
                    body(b + 1, 1)
                    ch.leave(B // 2, 4)

            single("l2a")
            transposed("n6")
            router("l2r", FFN2)
            ffn(FFN2)
            transposed("n7")
            single("l3a")
            transposed("n8")
            router("l3r", FFN3)
            ffn(FFN3)

        @block.tensor
        def _(pe):
            def mm(o, l, r, start, stop, **kw):
                return pe.matmul(o, l, r, start=start, stop=stop, **kw)

            pe.wait_ge(sem("zeroed"), 5)
            pe.wait_ge(sem("in_const"), 48)
            pe.wait_ge(sem("in_lora"), 9 * 16)
            pe.wait_ge(sem("in_blk"), 20 * 16)
            for c in range(FFN1.C):
                if c >= 2:
                    pe.wait_ge(sem("merged"), 2 * (c - 1))
                k = 2 + 2 * (c % 2)
                for m in range(DM):
                    last = mm(ps[:, k, m * 256:m * 256 + 256], agup[:, m * 128:m * 128 + 128], bblk[:, c, :], True, True)
                last = mm(ps[:, k + 1, 0:D], adn[:, c, :], bdn, True, True)
                last.then_inc(sem("lora"), 1)
            for m in range(DM):
                last = mm(ps[:, 6, m * 8:m * 8 + 8], glA[:, m * 128:m * 128 + 128], glB, True, True)
            last.then_inc(sem("lora_gate"), 1)
            pe.wait_ge(sem("wkv_ready"), 1)
            pe.wait_ge(sem("in_l0w"), 96)
            for e in range(DM):
                for m in range(DM):
                    last = mm(ps[:, 7, e * B:(e + 1) * B], winT[:, m, e * 128:e * 128 + 128], wkv[:, m, :], m == 0, m == DM - 1)
            last.then_inc(sem("s1_done"), 1)
            pe.wait_ge(sem("s1_ready"), 2)
            for b in range(B):
                for m in range(DM):
                    last = mm(ps[0:Q, b // 2, (b % 2) * D:(b % 2) * D + D], s1r[:, m, b, :], woutT[:, m, :], m == 0, m == DM - 1)
            last.then_inc(sem("summed"), 1)

            def transposes(name):
                for b in range(B):
                    pe.wait_ge(sem("xn"), xn_count(name, b + 1))
                    for m in range(DM):
                        last = pe.transpose(ps[:, 2 * (b // 4) + m, (b % 4) * Q:(b % 4) * Q + Q],
                                            xn[:, b, m * 128:m * 128 + 128], ident[0:Q, 0:Q])
                    last.then_inc(sem("tr"), 1)

            def router(name, r, f, n):
                pe.wait_ge(sem("xnT"), xnT_count(name))
                for b in range(B):
                    for m in range(DM):
                        last = mm(ps[0:Q, 4, b * f.E:(b + 1) * f.E], xnT[:, m, b * Q:(b + 1) * Q], gate[n][:, m, :], m == 0, m == DM - 1)
                last.then_inc(sem("r_logits"), 1)
                if r == "l2r":
                    pe.wait_ge(sem("l2r_onehot"), 1)
                    for b in range(B):
                        last = pe.transpose(ps[:, 5 + b // 4, (b % 4) * Q:(b % 4) * Q + Q],
                                            oh[:, b * 256 + 128:b * 256 + 256], ident[0:Q, 0:Q])
                    last.then_inc(sem("l2r_secT"), 1)
                    pe.wait_ge(sem("l2r_secT_sb"), 1)
                    for b in range(B):
                        last = mm(ps[0:Q, b // 4, (b % 4) * 128:(b % 4) * 128 + 128], secT[:, b * Q:(b + 1) * Q], simb[:, :], True, True)
                    last.then_inc(sem("l2r_sims"), 1)
                pe.wait_ge(sem("r_wrep"), ROUTERS.index(r) + 1)
                for b in range(B):
                    pe.transpose(ps[:, 5 + b // 4, (b % 4) * Q:(b % 4) * Q + Q], wrep[:, b, :], ident[0:Q, 0:Q])\
                        .then_inc(sem("r_wT"), 1)

            def ffn(f):
                nm = f.name

                def gu(c, k, hf):
                    if hf == 0:
                        pe.wait_ge(sem(f"{nm}_wgu{k}"), (c // 2 + 1 if isinstance(c, int) else c[1]) * 16)
                    cc = c if isinstance(c, int) else c[0]
                    if not isinstance(c, int) or c >= 1:
                        pe.wait_ge(sem(nm + "_h"), 2 * cc + (hf - 1))
                    for w in range(2 if f.gated else 1):
                        for m in range(DM):
                            at = (m * 2 + w) * 128 if f.gated else m * 128
                            last = mm(ps[:, 2 * hf + w, 0:HT], wgu[k][:, at:at + 128], xnT[:, m, hf * HT:(hf + 1) * HT],
                                      m == 0, m == DM - 1)
                    last.then_inc(sem(nm + "_gu_done"), 1)

                def down(c, k, hf, first):
                    cc = c if isinstance(c, int) else c[0]
                    if hf == 0:
                        pe.wait_ge(sem(f"{nm}_wd{k}"), (c // 2 + 1 if isinstance(c, int) else c[1]) * 16)
                    pe.wait_ge(sem(nm + "_h"), 2 * cc + (hf + 1))
                    for m in range(DM):
                        last = mm(ps[:, 4 + 2 * m + hf, 0:HT], wd[k][:, m * 128:m * 128 + 128], hb[hf][:, :],
                                  first, True, skip_group_check=True)
                    last.then_inc(sem(nm + "_down_done"), 1)

                def chunk(c, k, prev, pk, prev_first):
                    gu(c, k, 0)
                    if prev is not None:
                        down(prev, pk, 1, prev_first)
                    gu(c, k, 1)
                    down(c, k, 0, prev is None)

                head = 3 if f.C % 2 else 2
                for c in range(head):
                    chunk(c, c % 2, c - 1 if c else None, (c - 1) % 2, c == 1)
                if f.C - head > 2:
                    with pe.Fori(0, (f.C - head) // 2) as i:
                        k0 = head % 2
                        c = i * 2 + head
                        n0 = i + (head // 2 + 1)
                        chunk((c, n0), k0, (c - 1, None), 1 - k0, False)
                        chunk((c + 1, i + ((head + 1) // 2 + 1)), 1 - k0, (c, None), k0, False)
                else:
                    for c in range(head, f.C):
                        chunk(c, c % 2, c - 1, (c - 1) % 2, False)
                down(f.C - 1, (f.C - 1) % 2, 1, False)
                pe.wait_ge(sem(nm + "_yT"), 4)
                for b in range(B):
                    for m in range(DM):
                        last = pe.transpose(ps[0:Q, b // 2, (b % 2) * D + m * 128:(b % 2) * D + m * 128 + 128],
                                            yT[:, m, b * Q:(b + 1) * Q], ident[:, :])
                    if b % 2:
                        last.then_inc(sem(nm + "_back"), 1)

            transposes("n2")
            router("n2", "l0", FFN0, 0)
            pe.wait_ge(sem("w_ready"), w_count("l0"))
            ffn(FFN0)

            pe.wait_ge(sem("far_ready"), 1)

            def query_turns(b, k):
                pe.wait_ge(sem("l1_xs"), b * 4 + 4)
                for n in range(2):
                    pe.wait_ge(sem("l1_q"), b * 6 + (n + 13))
                    for h in range(8):
                        last = pe.transpose(ps[0:96, 7, :].bitcast(BF16)[:, h * Q:(h + 1) * Q],
                                            xs[k][:, 8 * n + h, :, :].rearrange("q t r -> q (t r)"), identb[:, :])
                    last.then_inc(sem("l1_qtr"), 1)

            def max_turn(b, k, s):
                pe.wait_ge(sem("l1_amax"), b * HEADS + (GRP * (s + 1) + 1))
                pe.wait_ge(sem("l1_q"), b * 6 + (s + 15))
                for g in range(GRP):
                    h = GRP * s + g
                    last = mm(ps[96:97, 7, g * Q:(g + 1) * Q], nm[k][:, h:h + 1], identb[:, :], True, True)
                last.then_inc(sem("l1_mtr"), 1)

            def a_head(b, k, h):
                if h % GRP == 0:
                    s = h // GRP
                    pe.wait_ge(sem(f"in_stk{k}{s}"), 96 * (b // 2 + 1) if isinstance(b, int) else b[1])
                b = b if isinstance(b, int) else b[0]
                pe.wait_ge(sem("l1_amax"), b * HEADS + (h + 1))
                for j, a in enumerate(A0):
                    last = mm(ps[0:Q, j, 0:AW], qs[k][0:96, h, :], kstk[k][0:96, h, a:a + AW], True, True)
                last = mm(ps[0:Q, 2, AW - Q:AW], identb[:, :], farb[:, :], False, True, skip_group_check=True)
                last.then_inc(sem("l1_a"), 1)

            def chunk_keys(c):
                return (c * 128, 128) if c < FULL else (FULL * 128 + CA * (c - FULL), CA)

            def b_scores(b, k, h):
                if h % GRP == 0:
                    pe.wait_ge(sem("l1_q"), b * 6 + (h // GRP + 16))
                for j in range(3):
                    pe.wait_ge(sem("l1_exp"), (b * HEADS + h) * 4 + (1, 2, 4)[j])
                    for c in range(4 * j, 4 * j + 4):
                        at, n = chunk_keys(c)
                        last = mm(ps[0:n, 3 + j, (c % 4) * Q:(c % 4) * Q + Q], kstk[k][0:97, h, at:at + n],
                                  qs[k][0:97, h, :], True, True)
                    last.then_inc(sem("l1_sc"), 1)

            def b_values(b, k, h):
                s, g = h // GRP, h % GRP
                pe.wait_ge(sem("l1_masked"), b * HEADS + (h + 1))
                if h == 0:
                    pe.wait_ge(sem("l1_ofree"), b + 1)
                    pe.wait_ge(sem("l1_vaug"), b * NCH + NCH)
                for c in range(NCH):
                    n = 128 if c < FULL else CA
                    last = mm(ps[32 * g:32 * g + VW, 6, s * Q:(s + 1) * Q], vaug[k][0:n, c, h, :], pr[h % 2][0:n, c, :],
                              c == 0, c == NCH - 1)
                last.then_inc(sem("l1_pv"), 1)

            def out_turn(b):
                pe.wait_ge(sem("l1_ot"), b * GRP + GRP)
                for s in range(SETS):
                    last = pe.transpose(ps[0:Q, 6, s * 128:(s + 1) * 128], ot[:, s * Q:(s + 1) * Q], ident[:, :])
                last.then_inc(sem("l1_oT"), 1)

            def both(b, k, na, before=True):
                if na is not None:
                    query_turns(b + 1, 1 - k)
                    pe.wait_ge(sem("l1_q"), b * 6 + 21)
                for h in range(HEADS):
                    if na is not None and h and h % GRP == 0:
                        max_turn(b + 1, 1 - k, h // GRP - 1)
                    b_scores(b, k, h)
                    if na is not None:
                        a_head(b + 1 if isinstance(b, int) else (b + 1, na), 1 - k, h)
                    if h == 0 and before:
                        out_turn(b - 1)
                    if h:
                        b_values(b, k, h - 1)
                b_values(b, k, HEADS - 1)
                if na is not None:
                    max_turn(b + 1, 1 - k, SETS - 1)

            pe.sem_inc(sem("l1_pv"), 2)
            pe.sem_inc(sem("l1_sc"), 6 * HEADS)
            query_turns(0, 0)
            pe.wait_ge(sem("l1_q"), 15)
            for h in range(HEADS):
                a_head(0, 0, h)
                if h % GRP == GRP - 1:
                    max_turn(0, 0, h // GRP)
            both(0, 0, 1, before=False)
            both(1, 1, 1)
            with pe.Fori(1, (B - 2) // 2) as i:
                both(i * 2, 0, (i + 1) * 96)
                both(i * 2 + 1, 1, (i + 2) * 96)
            both(B - 2, 0, 1)
            both(B - 1, 1, None)
            out_turn(B - 1)

            transposes("n4")
            router("n4", "l1r", FFN1, 1)
            pe.wait_ge(sem("w_ready"), w_count("l1r"))
            ffn(FFN1)
            transposes("n5")
            pe.wait_ge(sem("xnT"), xnT_count("n5"))
            pe.wait_ge(sem("in_qkv"), 48)
            for w in range(2):
                for e in range(DM):
                    for hf in range(2):
                        for m in range(DM):
                            last = mm(ps[:, 4 * w + 2 * e + hf, 0:HT], wqkv[:, w, m, e * 128:e * 128 + 128],
                                      xnT[:, m, hf * HT:(hf + 1) * HT], m == 0, m == DM - 1)
                last.then_inc(sem("l2_proj"), 1)
            for b in range(B):
                if b < 4:
                    pe.wait_ge(sem("l2a_qT"), 4)
                else:
                    pe.wait_ge(sem("l2_vnew"), b - 3)
                for m in range(DM):
                    last = mm(ps[0:Q, b % 4, 0:D], xnT[:, m, b * Q:(b + 1) * Q], wqkv[:, 2, m, :], m == 0, m == DM - 1)
                last.then_inc(sem("l2_vproj"), 1)

            def single(name, new):
                def scores(b, k, n):
                    pe.wait_ge(sem(f"{name}_in{k}"), n * 5 * 16)
                    pe.wait_ge(sem(name + "_q"), b + 1)
                    pe.wait_ge(sem(name + "_scfree"), b + 1)
                    for j, (a, w) in enumerate(((0, 512), (512, 512), (1024, T - 1024))):
                        if new and j == 2:
                            w -= Q
                        for m in range(DM):
                            last = mm(ps[0:Q, j, 0:w], qst[k][:, m, :], ctT[k][:, m, a:a + w], m == 0, m == DM - 1)
                    if new:
                        for m in range(DM):
                            last = mm(ps[0:Q, 2, w:w + Q], qst[k][:, m, :], knT[:, m, bass.ds(b * Q, Q)], m == 0, m == DM - 1)
                    last.then_inc(sem(name + "_sc"), 1)

                def values(b, k):
                    pe.wait_ge(sem(name + "_p"), b + 1)
                    at = 0
                    for c in range(NCH):
                        n = 128 if c < FULL else CB[c - FULL]
                        if c % 4 == 0:
                            pe.wait_ge(sem(name + "_pt"), b * 3 + (c // 4 + 1))
                        last = pe.transpose(ps[0:n, 3 + c // 4, (c % 4) * Q:(c % 4) * Q + Q], pb[k][:, at:at + n], ident[0:Q, 0:Q])
                        at += n
                        if c % 4 == 3:
                            last.then_inc(sem(name + "_ptr"), 1)
                    pe.wait_ge(sem(name + "_ofree"), b + 1)
                    for c in range(NCH):
                        n = 128 if c < FULL else CB[c - FULL]
                        if c % 4 == 0:
                            pe.wait_ge(sem(name + "_pt"), b * 3 + (c // 4 + 4))
                        v = vnew[:, bass.ds(b, 1), :].rearrange("q a d -> q (a d)") if new and c == NCH - 1 else vn2[k][0:n, c, :]
                        last = mm(ps[0:Q, 6, 0:D], ptt[0:n, c, :], v, c == 0, c == NCH - 1)
                    last.then_inc(sem(name + "_o"), 1)

                pe.sem_inc(sem(name + "_sc"), 2)
                pe.sem_inc(sem(name + "_o"), 2)
                scores(0, 0, 1)
                with pe.Fori(0, (B - 2) // 2) as i:
                    scores(i * 2 + 1, 1, i + 1)
                    values(i * 2, 0)
                    scores(i * 2 + 2, 0, i + 2)
                    values(i * 2 + 1, 1)
                scores(B - 1, 1, B // 2)
                values(B - 2, 0)
                values(B - 1, 1)

            pe.wait_ge(sem("l2_vnew"), B)
            pe.wait_ge(sem("l2a_kT"), 4)
            single("l2a", True)
            transposes("n6")
            router("n6", "l2r", FFN2, 2)
            pe.wait_ge(sem("w_ready"), w_count("l2r"))
            ffn(FFN2)
            transposes("n7")
            pe.wait_ge(sem("xnT"), xnT_count("n7"))
            single("l3a", False)
            transposes("n8")
            router("n8", "l3r", FFN3, 3)
            pe.wait_ge(sem("w_ready"), w_count("l3r"))
            for hf in range(2):
                last = mm(ps[:, 1 + 2 * hf, 0:HT], awmat[:, :], Wb[:, hf * HT:(hf + 1) * HT], True, True)
            last.then_inc(sem("l3_gate"), 1)
            ffn(FFN3)

        @block.vector
        def _(dve):
            ch = Chain(dve, sem("dve_own"))
            link, add = ch.link, ch.add

            def bc(ap, shape):
                return ap.broadcast_to(shape)

            dve.sem_inc(sem("l1_ofree"), 1)
            dve.sem_inc(sem("l1_amax"), 1)
            dve.sem_inc(sem("l1_out"), 2)
            dve.wait_ge(sem("decayed"), 1)
            link(dve.memset(orow, 1.0))
            link(dve.tensor_scalar(krow, orow, dk[:, 1:2], None, ALU.mult))
            link(dve.tensor_tensor_scan(crow[:, ::-1], krow, orow, 0.0, ALU.mult, ALU.add))
            link(dve.tensor_reduce(csum[:, 0:1], crow, AX.X, ALU.add))
            for u in range(DM * B):
                dve.wait_ge(sem(f"in_ct{u % 3}"), 16 * (u // 3 + 1))
                add(dve.tensor_tensor_reduce(out=prod, in0=ct[u % 3], in1=crow, scale=1.0 / T, scalar=0.0, op0=ALU.mult, op1=ALU.add,
                                             accum_out=wkv[:, u % DM, u // DM:u // DM + 1]))
                dve.wait_ge(sem("kh_done"), u + 1)
                if u >= 2:
                    dve.wait_ge(sem("kl_done"), u - 1)
                ch.wait()
                dve.tensor_tensor(rest[u % 2], ct[u % 3], part[u % 3][:, 0, :], ALU.subtract).then_inc(sem("rest_done"), 1)
            dve.engine_nop().then_inc(sem("wkv_ready"), 1)
            dve.wait_ge(sem("in_lora"), 9 * 16)
            link(dve.tensor_tensor(aw_t, attr_r, wa_b, ALU.mult))
            dve.tensor_reduce(aw_t[:, 0:1], aw_t, AX.X, ALU.add).then_inc(sem("aw_dot"), 1)
            for c in range(FFN1.C):
                dve.wait_ge(sem("lora"), c + 1)
                k = 2 + 2 * (c % 2)
                dve.scalar_tensor_tensor(mgu[:, c, :], ps[:, k, :], 2.0, mgu[:, c, :], ALU.mult, ALU.add).then_inc(sem("merged"), 1)
                dve.scalar_tensor_tensor(mdn[:, c, :], ps[:, k + 1, 0:D], 2.0, mdn[:, c, :], ALU.mult, ALU.add).then_inc(sem("merged"), 1)
            dve.wait_ge(sem("lora_gate"), 1)
            dve.wait_ge(sem("in_gate"), 64)
            add(dve.scalar_tensor_tensor(gate[1][:, :, :], ps[:, 6, 0:16].rearrange("p (m e) -> p m e", m=DM), 2.0, gate[1][:, :, :], ALU.mult, ALU.add))
            dve.wait_ge(sem("in_blk"), 20 * 16)
            add(dve.tensor_scalar(awmat[:, :], ident[:, :], -1.0, 1.0, ALU.mult, ALU.add))
            ch.wait()
            link(dve.tensor_tensor(simb[:, :], simb[:, :], awmat[:, :], ALU.mult))
            link(dve.tensor_tensor(simb[:, :], simb[:, :], ident[:, :], ALU.add))
            dve.wait_ge(sem("aw_sig"), 1)
            link(dve.memset(awmat[:, :], 0.2 / FFN3.rep))
            link(dve.tensor_scalar(awmat[:, :], awmat[:, :], awcol[:, :], None, ALU.mult))

            def stats(name, src):
                for b in range(B):
                    add(dve.bn_stats(stat[:, b, :], src[:, b, :]))
                ch.wait()
                for b in range(B):
                    last = dve.bn_aggr(mv[:, b, :], stat[:, b, :])
                    if b < B - 1:
                        add(last)
                last.then_inc(sem("stat"), 1)
                dve.wait_ge(sem("rstd"), NORMS.index(name) + 1)

            def norm(name, src=x):
                stats(name, src)
                for b in range(B):
                    dve.tensor_scalar(xn[:, b, :], src[:, b, :], mv[:, b, 0:1], rstd[:, b:b + 1], ALU.subtract, ALU.mult)\
                        .then_inc(sem("xn"), 1)

            dve.wait_ge(sem("in_x"), 16)
            norm("n0")
            dve.wait_ge(sem("s1_done"), 1)
            for m in range(DM):
                link(dve.tensor_scalar(csum[:, 1:2], csum[:, 0:1], bin_c[:, m:m + 1], 1.0 / T, ALU.mult, ALU.mult))
                link(dve.tensor_scalar(s1[:, m, :], ps[:, 7, m * B:(m + 1) * B], csum[:, 1:2], None, ALU.add))
            for m in range(DM):
                dve.tensor_copy(s1r[:, m, :, :], bc(s1[:, m, :].unsqueeze(2), [128, B, Q])).then_inc(sem("s1_ready"), 1)
            dve.wait_ge(sem("summed"), 1)
            dve.wait_ge(sem("xn"), xn_count("n0"))
            for j in range(4):
                add(dve.tensor_tensor(xn[:, 2 * j:2 * j + 2, :], xn[:, 2 * j:2 * j + 2, :], ps[0:Q, j, :].rearrange("q (b d) -> q b d", b=2), ALU.add))
            ch.wait()
            link(dve.tensor_tensor(xn[:, :, :], xn[:, :, :], bc(bout_b.unsqueeze(1), [Q, B, D]), ALU.add))
            norm("n1", xn)
            dve.wait_ge(sem("xn"), xn_count("n1"))
            link(dve.tensor_tensor(xn[:, :, :], xn[:, :, :], bc(gam_b.unsqueeze(1), [Q, B, D]), ALU.mult))
            link(dve.tensor_tensor(x[:, :, :], x[:, :, :], xn[:, :, :], ALU.add))
            link(dve.tensor_tensor(x[:, :, :], x[:, :, :], bc(bet_b.unsqueeze(1), [Q, B, D]), ALU.add))

            def router(r, f):
                E, K = f.E, f.K

                def v3(t):
                    return t[:, 0:B * E].rearrange("q (b e) -> q b e", b=B)

                dve.wait_ge(sem("r_logits"), ROUTERS.index(r) + 1)
                link(dve.tensor_copy(rl[:, 0:B * E], ps[0:Q, 4, 0:B * E]))
                link(dve.tensor_reduce(rmx, v3(rl), AX.X, ALU.max))
                dve.tensor_tensor(v3(rp), v3(rl), bc(rmx.unsqueeze(2), [Q, B, E]), ALU.subtract).then_inc(sem("r_shift"), 1)
                dve.wait_ge(sem("r_exp"), ROUTERS.index(r) + 1)
                link(dve.tensor_reduce(rsum, v3(rp), AX.X, ALU.add))
                link(dve.reciprocal(rsum, rsum))
                link(dve.tensor_tensor(v3(rp), v3(rp), bc(rsum.unsqueeze(2), [Q, B, E]), ALU.mult))
                src = v3(rl) if r == "l3r" else v3(rp)
                for b in range(B):
                    add(dve.max(v8[:, b, :], src[:, b, :]))
                ch.wait()
                for b in range(B):
                    add(dve.max_index(i8[:, b, :], v8[:, b, :], src[:, b, :]))
                ch.wait()
                link(dve.tensor_copy(if8, i8))
                o = oh[:, 0:B * K * E].rearrange("q (b k e) -> q b k e", b=B, k=K)
                ins = dve.tensor_tensor(o, bc(iota[:, 0:E].unsqueeze(1).unsqueeze(1), [Q, B, K, E]),
                                        bc(if8[:, :, 0:K].unsqueeze(3), [Q, B, K, E]), ALU.is_equal)
                w = v3(rw)
                if r != "l2r":
                    link(ins)
                    link(dve.tensor_reduce(v3(rsel), o.rearrange("q b k e -> q b e k"), AX.X, ALU.add))
                    link(dve.tensor_tensor(w, v3(rp), v3(rsel), ALU.mult))
                    if r != "l0":
                        link(dve.tensor_reduce(rsum, w, AX.X, ALU.add))
                        if r == "l3r":
                            link(dve.tensor_scalar(rsum, rsum, 1e-8, None, ALU.add))
                        link(dve.reciprocal(rsum, rsum))
                        link(dve.tensor_tensor(w, w, bc(rsum.unsqueeze(2), [Q, B, E]), ALU.mult))
                else:
                    ins.then_inc(sem("l2r_onehot"), 1)
                    dve.wait_ge(sem("l2r_onehot"), 1)
                    link(dve.tensor_reduce(rsum, v8, AX.X, ALU.add))
                    link(dve.tensor_scalar(rsum, rsum, 1e-12, None, ALU.max))
                    link(dve.reciprocal(rsum, rsum))
                    link(dve.tensor_tensor(w8, v8, bc(rsum.unsqueeze(2), [Q, B, 8]), ALU.mult))
                    dve.wait_ge(sem("l2r_secT"), 1)
                    add(dve.tensor_copy(secT[:, 0:HT], ps[:, 5, 0:HT]))
                    ch.wait()
                    dve.tensor_copy(secT[:, HT:TOK], ps[:, 6, 0:HT]).then_inc(sem("l2r_secT_sb"), 1)
                    dve.wait_ge(sem("l2r_sims"), 1)
                    for j in range(2):
                        add(dve.tensor_copy(scand[:, j * 512:j * 512 + 512], ps[0:Q, j, :]))
                    ch.wait()
                    for b in range(B):
                        add(dve.tensor_tensor(cand[:, b * 512:(b + 1) * 512].rearrange("q (j i e) -> q j i e", j=4, i=4),
                                              bc(scand[:, b * 128:(b + 1) * 128].rearrange("q (j e) -> q j e", j=4).unsqueeze(2), [Q, 4, 4, 32]),
                                              bc(o[:, b, 0:4, :].unsqueeze(1), [Q, 4, 4, 32]), ALU.mult))
                    ch.wait()
                    link(dve.tensor_reduce(pick, cand.rearrange("q (b j i e) -> q (b j) i e", b=B, j=4, i=4), AX.X, ALU.add))
                    link(dve.tensor_reduce(best, pick, AX.X, ALU.max))
                    link(dve.tensor_scalar(keep, best, 0.5, None, ALU.is_lt))
                    link(dve.tensor_scalar(left, keep, -1.0, 1.0, ALU.mult, ALU.add))
                    link(dve.tensor_tensor(pick, pick, bc(best.unsqueeze(3), [Q, B, 4, 4]), ALU.is_equal))
                    for i in range(4):
                        link(dve.tensor_tensor(first[:, :, :, i], left, pick[:, :, :, i], ALU.mult))
                        if i < 3:
                            link(dve.tensor_tensor(left, left, first[:, :, :, i], ALU.subtract))
                    link(dve.tensor_tensor(first, first, bc(w8[:, :, 4:8].unsqueeze(3), [Q, B, 4, 4]), ALU.mult))
                    link(dve.tensor_reduce(moved, first.rearrange("q b j i -> q b i j"), AX.X, ALU.add))
                    link(dve.tensor_tensor(w8[:, :, 0:4], w8[:, :, 0:4], moved, ALU.add))
                    link(dve.tensor_tensor(w8[:, :, 4:8], w8[:, :, 4:8], keep, ALU.mult))
                    link(dve.tensor_tensor(o, o, bc(w8.unsqueeze(3), [Q, B, 8, 32]), ALU.mult))
                    link(dve.tensor_reduce(w, o.rearrange("q b k e -> q b e k"), AX.X, ALU.add))
                dve.tensor_copy(wrep.rearrange("q b (e r) -> q b e r", e=E), bc(w.unsqueeze(3), [Q, B, E, f.rep]))\
                    .then_inc(sem("r_wrep"), 1)
                dve.wait_ge(sem("w_ready"), w_count(r))
                if r == "l3r":
                    dve.wait_ge(sem("l3_gate"), 1)
                    for hf in range(2):
                        t = Wb[:, hf * HT:(hf + 1) * HT]
                        add(dve.scalar_tensor_tensor(t, ps[:, 1 + 2 * hf, 0:HT], 0.9, t, ALU.add, ALU.mult))
                    ch.wait()

            def ffn(f):
                nm = f.name

                def unit(c, hf, weighted, i=None):
                    if f.gated:
                        dve.wait_ge(sem(nm + "_silu"), 2 * c + (hf + 1))
                        if weighted:
                            link(dve.tensor_tensor(sg[hf][:, :], sg[hf][:, :], Wb[:, hf * HT:(hf + 1) * HT], ALU.mult))
                        a, o = sg[hf][:, :], ps[:, 2 * hf + 1, 0:HT]
                    else:
                        dve.wait_ge(sem(nm + "_gu_done"), 2 * c + (hf + 1))
                        a, o = Wb[:, hf * HT:(hf + 1) * HT], ps[:, 2 * hf, 0:HT]
                    if not isinstance(c, int) or c >= 1:
                        dve.wait_ge(sem(nm + "_down_done"), 2 * c + (hf - 1))
                    dve.tensor_tensor(hb[hf][:, :], a, o, ALU.mult).then_inc(sem(nm + "_h"), 1)

                head = 3 if f.C % 2 else 2
                if f.C - head <= 2:
                    head = f.C
                for c in range(head):
                    for hf in range(2):
                        unit(c, hf, c >= f.shared)
                if head < f.C:
                    with dve.Fori(head, f.C, 1) as c:
                        ch.enter(c, head, 2)
                        for hf in range(2):
                            unit(c, hf, True)
                        ch.leave(f.C - head, 2)
                dve.wait_ge(sem(nm + "_down_done"), 2 * f.C)
                for m in range(DM):
                    dve.tensor_copy(yT[:, m, HT:TOK], ps[:, 5 + 2 * m, 0:HT]).then_inc(sem(nm + "_yT"), 1)
                for j in range(4):
                    dve.wait_ge(sem(nm + "_back"), j + 1)
                    o = ps[0:Q, j, :].rearrange("q (b d) -> q b d", b=2)
                    ins = dve.tensor_tensor(x[:, 2 * j:2 * j + 2, :], x[:, 2 * j:2 * j + 2, :], o, ALU.add)
                    if nm == "l3":
                        ins.then_inc(sem("l3_x"), 1)
                    else:
                        add(ins)
                ch.wait()

            norm("n2")
            for n in range(3):
                dve.wait_ge(sem(f"parts_out{n}"), 16 * ((DM * B + 2 - n) // 3))
            router("l0", FFN0)
            ffn(FFN0)
            norm("n3")

            def l1_o(b):
                dve.wait_ge(sem("l1_oT"), b + 1)
                o = ps[0:Q, 6, :].rearrange("q (h v) -> q h v", h=HEADS)
                link(dve.reciprocal(den[:, :], o[:, :, HD]))
                dve.tensor_tensor(att[:, :, :], o[:, :, 0:HD], bc(den[:, :].unsqueeze(2), [Q, HEADS, HD]), ALU.mult)\
                    .then_inc(sem("l1_ofree"), 1)
                dve.wait_ge(sem("l1_ofree"), b + 2)
                xb = x[:, bass.ds(b, 1), :].rearrange("q a d -> q (a d)")
                dve.tensor_tensor(xb, xb, att[:, :, :].rearrange("q h v -> q (h v)"), ALU.add).then_inc(sem("l1_out"), 1)

            def l1_a(b, k, before=True):
                for h in range(HEADS):
                    dve.wait_ge(sem("l1_a"), b * HEADS + (h + 1))
                    dve.tensor_reduce(nm[k][:, h:h + 1], ps[0:Q, 0:3, 0:AW], AX.XY, ALU.max, negate=True)\
                        .then_inc(sem("l1_amax"), 1)
                    if h == 0 and before:
                        l1_o(b - 2)

            l1_a(0, 0, before=False)
            l1_a(1, 1, before=False)
            with dve.Fori(1, B // 2) as i:
                ch.enter(i, 1, 2)
                l1_a(i * 2, 0)
                l1_a(i * 2 + 1, 1)
                ch.leave(B // 2 - 1, 2)
            l1_o(B - 2)
            l1_o(B - 1)
            dve.wait_ge(sem("l1_out"), B + 2)

            norm("n4")
            router("l1r", FFN1)
            ffn(FFN1)
            norm("n5")
            dve.wait_ge(sem("in_qkv"), 48)
            for w, dst in ((0, yT), (1, knT)):
                dve.wait_ge(sem("l2_proj"), w + 1)
                for e in range(DM):
                    for hf in range(2):
                        dve.tensor_scalar(dst[:, e, hf * HT:(hf + 1) * HT], ps[:, 4 * w + 2 * e + hf, 0:HT], bqk[:, w, e:e + 1], None, ALU.add)\
                            .then_inc(sem("l2a_qT" if w == 0 else "l2a_kT"), 1)
            dve.wait_ge(sem("l2a_kT"), 4)

            def single(name, masked):
                def front(b, k, n):
                    dve.wait_ge(sem(f"{name}_in{k}"), n * 5 * 16)
                    if not masked:
                        link(dve.tensor_copy(bias[k], mk8[k]))
                        link(dve.tensor_reduce(anym[k], bias[k], AX.X, ALU.max))
                        link(dve.tensor_scalar(bias[k], bias[k], -1.0, -FAR, ALU.add, ALU.mult))
                    dve.wait_ge(sem(name + "_sc"), b + 3)
                    flat = ps[0:Q, 0:3, :].rearrange("q j n -> q (j n)")[:, 0:T]
                    dve.scalar_tensor_tensor(sc, flat, D ** -0.5, bias[k], ALU.mult, ALU.add).then_inc(sem(name + "_scfree"), 1)
                    dve.wait_ge(sem(name + "_scfree"), b + 2)
                    dve.tensor_reduce(nmx, sc, AX.X, ALU.max, negate=True).then_inc(sem(name + "_max"), 1)

                def middle(b, k):
                    dve.wait_ge(sem(name + "_exp"), b + 1)
                    link(dve.reciprocal(rsm, ssum))
                    if not masked:
                        link(dve.tensor_tensor(rsm, rsm, anym[k], ALU.mult))
                    dve.tensor_scalar(pb[k], pb[k], rsm, None, ALU.mult).then_inc(sem(name + "_p"), 1)

                def end(b):
                    dve.wait_ge(sem(name + "_o"), b + 3)
                    xb = x[:, bass.ds(b, 1), :].rearrange("q a d -> q (a d)")
                    dve.tensor_tensor(xb, xb, ps[0:Q, 6, 0:D], ALU.add).then_inc(sem(name + "_ofree"), 1)

                dve.sem_inc(sem(name + "_scfree"), 1)
                dve.sem_inc(sem(name + "_ofree"), 1)
                per = 1 if masked else 5
                front(0, 0, 1)
                with dve.Fori(0, B // 2 - 1) as i:
                    ch.enter(i, 0, 2 * per)
                    middle(i * 2, 0)
                    front(i * 2 + 1, 1, i + 1)
                    end(i * 2)
                    middle(i * 2 + 1, 1)
                    front(i * 2 + 2, 0, i + 2)
                    end(i * 2 + 1)
                    ch.leave(B // 2 - 1, 2 * per)
                middle(B - 2, 0)
                front(B - 1, 1, B // 2)
                end(B - 2)
                middle(B - 1, 1)
                end(B - 1)
                dve.wait_ge(sem(name + "_ofree"), B + 1)

            for b in range(B):
                dve.wait_ge(sem("l2_vproj"), b + 1)
                dve.tensor_tensor(vnew[:, b, :], ps[0:Q, b % 4, 0:D], bv_b, ALU.add).then_inc(sem("l2_vnew"), 1)
            single("l2a", True)
            norm("n6")
            router("l2r", FFN2)
            ffn(FFN2)
            norm("n7")
            single("l3a", False)
            norm("n8")
            router("l3r", FFN3)
            ffn(FFN3)


def kernel(**inputs):
    import numpy as _np
    import concourse.bacc as _bacc
    from concourse import mybir as _mybir
    from concourse.bass_utils import run_bass_kernel_spmd as _run

    a = {k: _np.asarray(v) for k, v in inputs.items()}

    def halves(t):
        c, w, n = t.shape
        return t.reshape(c, w // 128, 128, n).transpose(0, 2, 1, 3).reshape(c, 128, (w // 128) * n)

    def gated(gu, dn, experts):
        e, f2, w = gu.shape
        per, f = 128 // experts, f2 // 2
        g = gu.reshape(e, 2, f // per, per, w).transpose(2, 4, 1, 0, 3).reshape(f // per, w, 2 * 128)
        n = dn.reshape(e, w, f // per, per).transpose(2, 0, 3, 1).reshape(f // per, 128, w)
        return halves(g), n

    gu0, dn0 = gated(a["L0_ffn_gate_up_weights"], a["L0_ffn_down_weights"], FFN0.E)
    sgu, sdn = a["L0_ffn_shared_gate_up"], a["L0_ffn_shared_down"]
    fs = sdn.shape[1]
    fill = FFN0.shared * 128 - fs
    sgu = _np.pad(sgu.reshape(2, fs, D), ((0, 0), (0, fill), (0, 0))).reshape(1, 2 * (fs + fill), D)
    sdn = _np.pad(sdn, ((0, 0), (0, fill))).reshape(1, D, fs + fill)
    gus, dns = gated(sgu, sdn, 1)
    gu2, dn2 = gated(a["L2_ffn_gate_up_proj"], a["L2_ffn_down_proj"], FFN2.E)
    e1 = FFN1.E
    gup = a["L1_ffn_gate_up_proj"].reshape(e1, D, 2, FFN1.C, FFN1.rep).transpose(3, 1, 2, 0, 4).reshape(FFN1.C, D, 256)
    dnp = a["L1_ffn_down_proj"].reshape(e1, FFN1.C, FFN1.rep, D).transpose(1, 0, 2, 3).reshape(FFN1.C, 128, D)
    u3 = a["L3_ffn_U"].reshape(32, D, FFN3.C, FFN3.rep).transpose(2, 1, 0, 3).reshape(FFN3.C, D, 128)
    v3 = a["L3_ffn_V"].reshape(32, FFN3.C, FFN3.rep, D).transpose(1, 0, 2, 3).reshape(FFN3.C, 128, D)
    ctx = a["ctx_2048"]
    arrays = {
        "x": a["x"], "ctx": ctx, "ctxT": ctx.transpose(0, 2, 1), "mask": a["mask_BxSxS2_ff0"],
        "bkmask": a["mask_BxS2_bk0"],
        "decay": a["L0_xattn_decay"].reshape(1, 1), "winT": a["L0_xattn_W_in"].T, "woutT": a["L0_xattn_W_out"].T,
        "b_in": a["L0_xattn_b_in"].reshape(DM, 128).T, "b_out": a["L0_xattn_b_out"], "gamma": a["L0_xattn_gamma"], "beta": a["L0_xattn_beta"],
        "gate0T": a["L0_ffn_gate_weight"].T, "gate1T": a["L1_ffn_gate_weight"].T,
        "gate2T": a["L2_ffn_gate_weight"].T, "gate3T": a["L3_ffn_Wr"].T,
        "l0_gu": _np.concatenate([gus, gu0]), "l0_dn": _np.concatenate([dns, dn0]),
        "l1_gu": halves(gup), "l1_dn": dnp, "l2_gu": gu2, "l2_dn": dn2, "l3_gu": halves(u3), "l3_dn": v3,
        "gupA": a["L1_ffn_gup_lora_A"].reshape(128, D),
        "gupB": a["L1_ffn_gup_lora_B"].transpose(0, 2, 1).reshape(e1, 16, 2, FFN1.C, 16).transpose(0, 1, 3, 2, 4),
        "dnA": a["L1_ffn_down_lora_A"].reshape(e1, 16, FFN1.C, 16),
        "dnB": a["L1_ffn_down_lora_B"].transpose(0, 2, 1).reshape(128, D),
        "glA": a["L1_ffn_gate_lora_A"], "glB": a["L1_ffn_gate_lora_B"].T,
        "sim": a["L2_ffn_similarity"],
        "attr": _np.repeat(a["L3_ffn_attr"], FFN3.rep, axis=0), "Wa": a["L3_ffn_Wa"].reshape(32),
        "wqkvT": _np.stack([a["L2_xattn_Wq"].T, a["L2_xattn_Wk"].T, a["L2_xattn_Wv"].T]),
        "bqk": _np.stack([a["L2_xattn_bq"], a["L2_xattn_bk"]]).reshape(2, DM, 128).transpose(2, 0, 1), "bv": a["L2_xattn_bv"],
        "ident": _np.eye(128, dtype=_np.float32), "flip": _np.eye(128, dtype=_np.float32)[::-1],
        "iota": _np.arange(32, dtype=_np.float32),
    }
    nc = _bacc.Bacc("TRN2", target_bir_lowering=False, num_devices=1)
    maps, d = {}, {}
    for name, v in arrays.items():
        v = _np.ascontiguousarray(v)
        maps["in_" + name] = v
        d[name] = nc.dram_tensor("in_" + name, v.shape, _mybir.dt.from_np(v.dtype), kind="ExternalInput").ap()
    out = nc.dram_tensor("out_x", (B, Q, D), F32, kind="ExternalOutput").ap()
    build(nc, d, out)
    r = _run(nc, [maps], core_ids=[0])
    return r.results[0]["out_x"]
```

```python
from contextlib import ExitStack

import numpy as np

import concourse.bass as bass
from concourse import mybir

F32 = mybir.dt.float32
BF16 = mybir.dt.bfloat16
U32 = mybir.dt.uint32
U8 = mybir.dt.uint8
ACT = mybir.ActivationFunctionType
ALU = mybir.AluOpType
AX = mybir.AxisListType

B, Q, D, T = 8, 100, 256, 1444
TOK = B * Q
DM = D // 128
HT = TOK // 2
PAST = T - Q
HEADS, HD = 16, 16
SETS, GRP, PAD = 4, 4, 32
VW = HD + 1
LN_EPS = 1e-5
FAR = -1.0e30
FULL = PAST // 128
NCH = 12
CA = (T - FULL * 128) // 2
CB = (PAST - FULL * 128, Q)
LAG = 3
AW = T // 3 + 1
A0 = (0, T // 3, T - AW)


class Ffn:

    def __init__(self, name, experts, top, chunks, shared=0, gated=True):
        self.name, self.E, self.K, self.C, self.shared, self.gated = name, experts, top, chunks, shared, gated
        self.rep = 128 // experts
        self.cols = DM * (2 if gated else 1) * 128


FFN0 = Ffn("l0", 16, 4, 25, shared=3)
FFN1 = Ffn("l1", 8, 2, 8)
FFN2 = Ffn("l2", 32, 8, 24)
FFN3 = Ffn("l3", 32, 2, 4, gated=False)


NORMS = ("n0", "n1", "n2", "n3", "n4", "n5", "n6", "n7", "n8")
TURNED = ("n2", "n4", "n5", "n6", "n7", "n8")
ROUTERS = ("l0", "l1r", "l2r", "l3r")


def xn_count(name, b=B):
    return NORMS.index(name) * B + b


def tr_count(name, b):
    return TURNED.index(name) * B + b


def xnT_count(name):
    return TURNED.index(name) * 4 + 4


def w_count(r):
    return ROUTERS.index(r) * 2 + 2


def q_turn(b, n):
    return b * 7 + n


def o_turn(b):
    return b * 7 + 16


def m_turn(b, s):
    return b * 7 + (4 + s if s < SETS - 1 else 10)


class Chain:

    def __init__(self, eng, sem):
        self.eng, self.sem, self.n, self.base = eng, sem, 0, 0

    def add(self, ins):
        ins.then_inc(self.sem, 1)
        self.n += 1

    def wait(self):
        self.eng.wait_ge(self.sem, self.base + self.n)

    def link(self, ins):
        self.add(ins)
        self.wait()

    def enter(self, i, first, per):
        self.base = (i - first) * per
        self.n0 = self.n

    def leave(self, turns, per):
        assert self.n - self.n0 == per, (self.n - self.n0, per)
        self.n = self.n0 + turns * per
        self.base = 0


def build(nc, d, out):
    ctx = ExitStack()
    with ctx:
        def sb(name, shape, dt=F32):
            return ctx.enter_context(nc.sbuf_tensor("sb_" + name, shape, dt))

        sems = {}

        def sem(name):
            if name not in sems:
                sems[name] = ctx.enter_context(nc.semaphore(name))
            return sems[name]

        x = sb("x", [Q, B, D])
        xn = sb("xn", [Q, B, D])
        xnT = sb("xnT", [128, DM, TOK])
        yT = sb("yT", [128, DM, TOK])
        ident = sb("ident", [128, 128])
        flip = sb("flip", [128, 128])
        identb = sb("identb", [Q, Q], BF16)
        farb = sb("farb", [Q, Q], BF16)
        iota = sb("iota", [Q, 32])
        mhalf = sb("mhalf", [Q, B])
        Wb = sb("Wb", [128, TOK])
        stat = sb("stat", [Q, B, 6])
        mv = sb("mv", [Q, B, 2])
        rstd = sb("rstd", [Q, B])
        wgu = [sb(f"wgu{i}", [128, FFN0.cols]) for i in range(2)]
        wd = [sb(f"wd{i}", [128, D]) for i in range(2)]
        sg = [sb(f"sg{i}", [128, HT]) for i in range(2)]
        hb = [sb(f"hb{i}", [128, HT]) for i in range(2)]
        gate = {0: sb("gate0", [128, DM, 16]), 1: sb("gate1", [128, DM, 8]),
                2: sb("gate2", [128, DM, 32]), 3: sb("gate3", [128, DM, 32])}
        awcol = sb("awcol", [128, 1])
        awmat = sb("awmat", [128, 128])
        simb = sb("simb", [128, 128])
        arena = sb("arena", [128, 38912])
        parts = nc.dram_tensor("parts", (3, B, D, T), BF16).ap()
        merged_gu = nc.dram_tensor("merged_gu", (FFN1.C, 128, FFN1.cols), F32).ap()
        merged_dn = nc.dram_tensor("merged_dn", (FFN1.C, 128, D), F32).ap()

        def ar(at, n, p=128):
            return arena[0:p, at:at + n]

        ps = ctx.enter_context(nc.psum_tensor("ps", [128, 8, 512], F32))

        ct = [ar(1444 * i, T) for i in range(3)]
        part = [ar(4332 + 2166 * i, 2166).bitcast(BF16).rearrange("p (t k) -> p t k", t=3) for i in range(3)]
        rest = [ar(10830 + 1444 * i, T) for i in range(2)]
        crow = ar(13718, T)
        krow = ar(15162, T)
        orow = ar(16606, T)
        prod = ar(18050, T)
        dk = ar(19850, 2)
        csum = ar(19840, 2)
        wkv = ar(19850, DM * B).rearrange("p (m b) -> p m b", m=DM)
        s1 = ar(19870, DM * B).rearrange("p (m b) -> p m b", m=DM)
        s1r = ar(19900, DM * B * Q).rearrange("p (m b q) -> p m b q", m=DM, b=B)
        winT = ar(21600, DM * D).rearrange("p (m e) -> p m e", m=DM)
        woutT = ar(22200, DM * D).rearrange("p (m e) -> p m e", m=DM)
        bin_c = ar(22800, DM)
        bout_b = ar(22810, D, Q)
        gam_b = ar(23070, D, Q)
        bet_b = ar(23330, D, Q)
        ones1 = ar(23600, 128)
        agup = ar(23800, D)
        bblk = ar(24060, 2048).rearrange("p (c n) -> p c n", c=FFN1.C)
        adn = ar(26110, 1024).rearrange("p (c n) -> p c n", c=FFN1.C)
        bdn = ar(27140, D)
        glA = ar(27400, D, 16)
        glB = ar(27660, 8, 16)
        sim1 = ar(27700, 32, 32)
        attr_r = ar(27740, 32)
        wa_b = ar(27780, 32)
        aw_t = ar(27820, 32)
        mgu = ar(31000, FFN1.C * FFN1.cols).rearrange("p (c n) -> p c n", c=FFN1.C)
        mdn = ar(31000 + FFN1.C * FFN1.cols, FFN1.C * D).rearrange("p (c n) -> p c n", c=FFN1.C)
        rl = ar(28000, B * 32, Q)
        rp = ar(28260, B * 32, Q)
        rmx = ar(28520, B, Q)
        rsum = ar(28530, B, Q)
        v8 = ar(28540, B * 8, Q).rearrange("p (b k) -> p b k", b=B)
        i8 = ar(28610, B * 8, Q).bitcast(U32).rearrange("p (b k) -> p b k", b=B)
        if8 = ar(28680, B * 8, Q).rearrange("p (b k) -> p b k", b=B)
        rw = ar(28750, B * 32, Q)
        rsel = ar(29010, B * 32, Q)
        wrep = ar(29270, B * 128, Q).rearrange("p (b n) -> p b n", b=B)
        oh = ar(0, B * 8 * 32, Q)
        cand = ar(2100, B * 16 * 32, Q)
        pick = ar(6300, B * 16, Q).rearrange("p (b j i) -> p b j i", b=B, j=4)
        first = ar(6440, B * 16, Q).rearrange("p (b j i) -> p b j i", b=B, j=4)
        left = ar(6580, B * 4, Q).rearrange("p (b j) -> p b j", b=B)
        best = ar(6620, B * 4, Q).rearrange("p (b j) -> p b j", b=B)
        keep = ar(6660, B * 4, Q).rearrange("p (b j) -> p b j", b=B)
        moved = ar(6700, B * 4, Q).rearrange("p (b j) -> p b j", b=B)
        w8 = ar(6740, B * 8, Q).rearrange("p (b k) -> p b k", b=B)
        secT = ar(6810, TOK)
        scand = ar(7700, B * 128, Q)
        kstk = [ar(11552 * i, 11552).bitcast(BF16).rearrange("p (h k) -> p h k", h=HEADS) for i in range(2)]
        vnat = ar(23104, 3072).rearrange("p (c d) -> p c d", c=NCH)
        vaug = [ar(26176 + 3264 * i, 3264).rearrange("p (c h v) -> p c h v", c=NCH, h=HEADS) for i in range(2)]
        pr = [ar(32704 + 1200 * i, 1200).rearrange("p (c q) -> p c q", c=NCH) for i in range(2)]
        qs = [ar(35104 + 800 * i, 800).bitcast(BF16).rearrange("p (h q) -> p h q", h=HEADS) for i in range(2)]
        xs = [ar(36704 + 768 * i, 768, Q).bitcast(BF16).rearrange("p (h t r) -> p h t r", h=HEADS, t=6) for i in range(2)]
        xr = ar(38240, D, Q).rearrange("p (h r) -> p h r", h=HEADS)
        nm = [ar(38496 + 8 * i, 8, Q).bitcast(BF16) for i in range(2)]
        ot = ar(38512, SETS * Q)
        mx = sb("mx", [Q, GRP, 3])
        den = sb("den", [Q, HEADS])
        att = sb("att", [Q, HEADS, HD])
        ctT = [ar(2888 * i, 2888).rearrange("p (m k) -> p m k", m=DM) for i in range(2)]
        vn2 = [ar(5776 + 3072 * i, 3072).rearrange("p (c d) -> p c d", c=NCH) for i in range(2)]
        bias = [ar(11920 + T * i, T, Q) for i in range(2)]
        sc = ar(14808, T, Q)
        pb = [ar(16252, T, Q), ar(27000, T, Q)]
        mk8 = [ar(17700 + 361 * i, 361, Q).bitcast(U8) for i in range(2)]
        ptt = ar(18500, 1200).rearrange("p (c q) -> p c q", c=NCH)
        qst = [ar(20900 + 200 * i, 200).rearrange("p (m q) -> p m q", m=DM) for i in range(2)]
        knT = ar(21300, DM * TOK).rearrange("p (m t) -> p m t", m=DM)
        vnew = ar(22900, B * D, Q).rearrange("p (b d) -> p b d", b=B)
        wqkv = ar(24950, 3 * 512).rearrange("p (w m e) -> p w m e", w=3, m=DM)
        bqk = ar(26500, 4).rearrange("p (w m) -> p w m", w=2)
        bv_b = ar(26510, D, Q)
        nmx = ar(26770, 1, Q)
        ssum = ar(26772, 1, Q)
        rsm = ar(26774, 1, Q)
        anym = [ar(26776 + 2 * i, 1, Q) for i in range(2)]

        block = ctx.enter_context(nc.Block())

        def v_load(eng, b):
            eng.dma_start(vnat[:, 0:FULL, :], d["ctx"][bass.ds(b, 1), 0:FULL * 128, :]
                          .rearrange("a (c p) d -> p (a c) d", p=128)).then_inc(sem("in_vnat"), 16)
            eng.dma_start(vnat[0:CA, FULL:NCH, :], d["ctx"][bass.ds(b, 1), FULL * 128:T, :]
                          .rearrange("a (c p) d -> p (a c) d", p=CA)).then_inc(sem("in_vnat"), 16)

        def stack_loads(eng, b, k, s):
            h = slice(GRP * s, GRP * s + GRP)
            at = 0
            for n in (3, 2, 1):
                for t in range(n):
                    src = parts[t, bass.ds(b, 1), GRP * HD * s:GRP * HD * (s + 1), :].rearrange("a (h r) k -> (a r) h k", r=HD)
                    eng.dma_start(kstk[k][at:at + HD, h, :], src).then_inc(sem(f"in_stk{k}{s}"), 16)
                    at += HD

        @block.sync
        def _(sp):
            def load(name, dst, src, **kw):
                sp.dma_start(dst, src, **kw).then_inc(sem(name), 16)

            load("in_x", x[:, :, :], d["x"].rearrange("b q d -> q b d"))
            load("in_const", ident[:, :], d["ident"])
            load("in_const", flip[:, :], d["flip"])
            load("in_const", iota[:, :], d["iota"].partition_broadcast(Q))
            load("in_decay", dk[:, 0:1], d["decay"].partition_broadcast(128))
            load("in_l0w", winT, d["winT"].rearrange("(m p) e -> p m e", p=128))
            load("in_l0w", woutT, d["woutT"].rearrange("(m p) e -> p m e", p=128))
            load("in_l0w", bin_c, d["b_in"])
            load("in_l0w", bout_b, d["b_out"].partition_broadcast(Q))
            load("in_l0w", gam_b, d["gamma"].partition_broadcast(Q))
            load("in_l0w", bet_b, d["beta"].partition_broadcast(Q))
            for n in range(4):
                load("in_gate", gate[n][:, :, :], d[f"gate{n}T"].rearrange("(m p) e -> p m e", p=128))

            def ct_load(u):
                sp.dma_start(ct[u % 3], d["ctxT"][u // DM, (u % DM) * 128:(u % DM) * 128 + 128, :]).then_inc(sem(f"in_ct{u % 3}"), 16)

            for u in range(3):
                ct_load(u)
            load("in_lora", mgu[:, :, :], d["l1_gu"].rearrange("c p n -> p c n"))
            load("in_lora", mdn[:, :, :], d["l1_dn"].rearrange("c p n -> p c n"))
            load("in_lora", agup, d["gupA"])
            load("in_lora", bdn, d["dnB"])
            load("in_lora", glA, d["glA"])
            load("in_lora", glB, d["glB"])
            load("in_lora", sim1, d["sim"])
            load("in_lora", attr_r, d["attr"])
            load("in_lora", wa_b, d["Wa"].partition_broadcast(128))
            sp.wait_ge(sem("zeroed"), 4)
            for e in range(8):
                s = slice(16 * e, 16 * e + 16)
                load("in_blk", bblk[s, :, :].rearrange("p c (g n) -> p c g n", g=2)[:, :, :, s],
                     d["gupB"][e].rearrange("r c g f -> r c g f"))
                load("in_blk", adn[s, :, s], d["dnA"][e])
            for j in range(4):
                load("in_blk", simb[32 * j:32 * j + 32, 32 * j:32 * j + 32], d["sim"])
            for u in range(DM * B):
                sp.wait_ge(sem("kl_done"), u + 1)
                sp.dma_start(parts[:, u // DM, (u % DM) * 128:(u % DM) * 128 + 128, :].rearrange("t p k -> p t k"), part[u % 3])\
                    .then_inc(sem(f"parts_out{u % 3}"), 16)
                if u + 3 < DM * B:
                    sp.wait_ge(sem("rest_done"), u + 1)
                    ct_load(u + 3)
            sp.wait_ge(sem("merged"), 2 * FFN1.C)
            sp.dma_start(merged_gu.rearrange("c p n -> p c n"), mgu).then_inc(sem("merged_out"), 16)
            sp.dma_start(merged_dn.rearrange("c p n -> p c n"), mdn).then_inc(sem("merged_out"), 16)

            def ffn_loads(f, gu, dn):
                def chunk(c, k):
                    if k is None:
                        k = c % 2
                    if not isinstance(c, int) or c >= 2:
                        sp.wait_ge(sem(f.name + "_gu_done"), 2 * c - 2)
                    sp.dma_start(wgu[k][:, 0:f.cols], gu(c)).then_inc(sem(f"{f.name}_wgu{k}"), 16)
                    if not isinstance(c, int) or c >= 2:
                        sp.wait_ge(sem(f.name + "_down_done"), 2 * c - 2)
                    sp.dma_start(wd[k][:, :], dn(c)).then_inc(sem(f"{f.name}_wd{k}"), 16)

                head = 3 if f.C % 2 else 2
                for c in range(head):
                    chunk(c, None)
                if f.C - head > 2:
                    with sp.Fori(0, (f.C - head) // 2) as i:
                        c = i * 2 + head
                        chunk(c, head % 2)
                        chunk(c + 1, (head + 1) % 2)
                else:
                    for c in range(head, f.C):
                        chunk(c, None)

            def dram_chunks(name):
                return (lambda c: d[name + "_gu"][bass.ds(c, 1), :, :].rearrange("a p n -> p (a n)"),
                        lambda c: d[name + "_dn"][bass.ds(c, 1), :, :].rearrange("a p n -> p (a n)"))

            ffn_loads(FFN0, *dram_chunks("l0"))

            sp.wait_ge(sem("l1_vfree"), 1)
            v_load(sp, 1)
            with sp.Fori(0, (B - 2) // 2) as i:
                for k in range(2):
                    b = i * 2 + (k + 2)
                    sp.wait_ge(sem("l1_vfree"), b)
                    sp.sem_inc(sem("sp_turns"), 1)
                    v_load(sp, b)
                    for s in range(SETS):
                        sp.wait_ge(sem("l1_sc"), b * (3 * HEADS) + 3 * GRP * (s + 1))
                        sp.sem_inc(sem("sp_turns"), 1)
                        stack_loads(sp, b, k, s)

            sp.wait_ge(sem("merged_out"), 32)
            ffn_loads(FFN1, lambda c: merged_gu[bass.ds(c, 1), :, :].rearrange("a p n -> p (a n)"),
                      lambda c: merged_dn[bass.ds(c, 1), :, :].rearrange("a p n -> p (a n)"))

            def key_loads(name, b, k, masked):
                sp.wait_ge(sem(name + "_sc"), b + 1)
                sp.sem_inc(sem("sp_turns"), 1)
                sp.dma_start(ctT[k][:, :, :], d["ctxT"][bass.ds(b, 1), :, :].rearrange("a (m p) k -> p (a m) k", p=128))\
                    .then_inc(sem(f"{name}_ink{k}"), 16)
                sp.wait_ge(sem(name + "_scfree"), b + 1)
                sp.sem_inc(sem("sp_turns"), 1)
                if masked:
                    sp.dma_start(bias[k], d["mask"][bass.ds(b, 1), :, :].rearrange("a q k -> q (a k)"))\
                        .then_inc(sem(f"{name}_inm{k}"), 16)
                else:
                    sp.dma_start(mk8[k], d["bkmask"][bass.ds(b, 1), :].rearrange("a k -> (a k)").partition_broadcast(Q))\
                        .then_inc(sem(f"{name}_inm{k}"), 16)

            def value_loads(name, b, k):
                sp.wait_ge(sem(name + "_o"), b + 1)
                sp.sem_inc(sem("sp_turns"), 1)
                sp.dma_start(vn2[k][:, 0:FULL, :], d["ctx"][bass.ds(b, 1), 0:FULL * 128, :]
                             .rearrange("a (c p) d -> p (a c) d", p=128)).then_inc(sem(f"{name}_inv{k}"), 16)
                at = FULL * 128
                for j, n in enumerate(CB):
                    sp.dma_start(vn2[k][0:n, FULL + j, :], d["ctx"][bass.ds(b, 1), at:at + n, :]
                                 .rearrange("a p d -> p (a d)")).then_inc(sem(f"{name}_inv{k}"), 16)
                    at += n

            def single_loads(name, masked):
                key_loads(name, 0, 0, masked)
                with sp.Fori(0, B // 2 - 1) as i:
                    key_loads(name, i * 2 + 1, 1, masked)
                    value_loads(name, i * 2, 0)
                    key_loads(name, i * 2 + 2, 0, masked)
                    value_loads(name, i * 2 + 1, 1)
                key_loads(name, B - 1, 1, masked)
                value_loads(name, B - 2, 0)
                value_loads(name, B - 1, 1)

            sp.wait_ge(sem("w_ready"), w_count("l1r"))
            load("in_qkv", wqkv[:, :, :, :], d["wqkvT"].rearrange("w (m p) e -> p w m e", p=128))
            load("in_qkv", bqk[:, :, :], d["bqk"])
            load("in_qkv", bv_b, d["bv"].partition_broadcast(Q))
            single_loads("l2a", True)
            ffn_loads(FFN2, *dram_chunks("l2"))
            sp.wait_ge(sem("w_ready"), w_count("l2r"))
            single_loads("l3a", False)
            ffn_loads(FFN3, *dram_chunks("l3"))
            for j in range(4):
                sp.wait_ge(sem("l3_x"), j + 1)
                sp.dma_start(out[2 * j:2 * j + 2, :, :].rearrange("b q d -> q b d"), x[:, 2 * j:2 * j + 2, :])\
                    .then_inc(sem("out_done"), 16)
            sp.wait_ge(sem("out_done"), 64)

        @block.gpsimd
        def _(pool):
            ch = Chain(pool, sem("pool_own"))

            def wait_register(name, value):
                pool.wait_ge(sem(name), value)
                pool.sem_inc(sem("pool_turns"), 1)

            pool.memset(mhalf[:, :], -0.5).then_inc(sem("mhalf_set"), 1)
            pool.memset(bblk[:, :, :], 0.0).then_inc(sem("zeroed"), 1)
            pool.memset(adn[:, :, :], 0.0).then_inc(sem("zeroed"), 1)
            pool.memset(simb[:, :], 0.0).then_inc(sem("zeroed"), 1)
            pool.memset(ones1, 1.0).then_inc(sem("zeroed"), 1)
            pool.memset(ot, 0.0).then_inc(sem("zeroed"), 1)
            pool.wait_ge(sem("in_const"), 48)
            ch.link(pool.tensor_copy(identb[:, :], ident[0:Q, 0:Q]))
            ch.link(pool.memset(farb[:, :], 0.0))
            pool.affine_select(out=farb[:, :], in_=farb[:, :], pattern=[[-1, Q]], compare_op=ALU.is_ge, fill=FAR,
                               base=0, channel_multiplier=1).then_inc(sem("far_ready"), 1)

            def norm(name):
                pool.wait_ge(sem("stat"), NORMS.index(name) + 1)
                ch.link(pool.tensor_scalar(rstd[:, :], mv[:, :, 1], LN_EPS, None, ALU.add))
                pool.tensor_tensor(rstd[:, :], rstd[:, :], mhalf[:, :], ALU.pow).then_inc(sem("rstd"), 1)
                pool.wait_ge(sem("rstd"), NORMS.index(name) + 1)

            pool.wait_ge(sem("mhalf_set"), 1)

            def prepare_queries(b, k, step):
                src = xn[:, bass.ds(b, 1), :].rearrange("q a (h r) -> q (a h) r", h=HEADS)
                if step == 0:
                    if not isinstance(b, int) or b >= 2:
                        wait_register("l1_qtr", b * 2 - 2)
                    ins = pool.tensor_copy(xs[k][:, :, 0:3, :], src.unsqueeze(2).broadcast_to([Q, HEADS, 3, HD]))
                elif step == 1:
                    ins = pool.tensor_tensor(xr, src, xs[k][:, :, 0, :], ALU.subtract)
                elif step == 2:
                    ins = pool.tensor_copy(xs[k][:, :, 3:5, :], xr.unsqueeze(2).broadcast_to([Q, HEADS, 2, HD]))
                else:
                    ins = pool.tensor_tensor(xs[k][:, :, 5, :], xr, xs[k][:, :, 3, :], ALU.subtract)
                ins.then_inc(sem("l1_xs"), 1)
                wait_register("l1_xs", b * 4 + (step + 1))

            def copy_values(b, k, c):
                if c == 0:
                    wait_register("in_vnat", b * 32 + 32)
                    if not isinstance(b, int) or b:
                        wait_register("l1_pv", (b - 1) * HEADS + 2)
                n = 128 if c < FULL else CA
                pool.tensor_copy(vaug[k][0:n, c, :, 0:HD], vnat[0:n, c, :].rearrange("p (h v) -> p h v", h=HEADS))\
                    .then_inc(sem("l1_vaug"), 1)
                if c == NCH - 1:
                    pool.wait_ge(sem("l1_vaug"), b * NCH + NCH)
                    pool.sem_inc(sem("l1_vfree"), 1)

            def masks(b, nk, k=None):
                for h in range(HEADS):
                    wait_register("l1_exp", (b * HEADS + h) * 4 + 8)
                    tail = pr[h % 2][0:CA, FULL:NCH, :]
                    pool.affine_select(out=tail, in_=tail, pattern=[[-CA, 2], [1, Q]], compare_op=ALU.is_ge, fill=0.0,
                                       base=PAST - FULL * 128, channel_multiplier=-1).then_inc(sem("l1_masked"), 1)
                    if nk is not None and h < NCH:
                        copy_values(b + 1, nk, h)
                    if k is not None and h >= NCH:
                        prepare_queries(b + 2, k, h - NCH)

            for u in range(DM * B):
                pool.wait_ge(sem("km_done"), u + 1)
                pool.tensor_tensor(part[u % 3][:, 2, :], rest[u % 2], part[u % 3][:, 1, :], ALU.subtract).then_inc(sem("kl_done"), 1)
            norm("n0")
            norm("n1")
            norm("n2")
            pool.wait_ge(sem("w_ready"), w_count("l0"))
            for n in range(3):
                pool.wait_ge(sem(f"parts_out{n}"), 16 * ((DM * B + 2 - n) // 3))
            pool.wait_ge(sem("merged_out"), 32)
            for k in range(2):
                pool.memset(kstk[k][96:97, :, :], 1.0).then_inc(sem("stack_ones"), 1)
                pool.wait_ge(sem("stack_ones"), k + 1)
            for k in range(2):
                pool.memset(vaug[k][:, :, :, HD], 1.0).then_inc(sem("value_ones"), 1)
                pool.wait_ge(sem("value_ones"), k + 1)
            pool.wait_ge(sem("in_vnat"), 32)
            for c in range(NCH):
                copy_values(0, 0, c)
            norm("n3")
            pool.wait_ge(sem("xn"), xn_count("n3"))
            for b in range(2):
                for step in range(4):
                    prepare_queries(b, b, step)
            with pool.Fori(0, (B - 2) // 2) as i:
                b = i * 2
                masks(b, 1, 0)
                masks(b + 1, 0, 1)
            masks(B - 2, 1)
            masks(B - 1, None)
            norm("n4")
            norm("n5")

            def stage_queries(name, src, b, k):
                wait_register(name + "_sc", b + 1)
                pool.tensor_copy(qst[k][:, :, :], src[:, :, bass.ds(b * Q, Q)]).then_inc(sem(name + "_q"), 1)

            pool.wait_ge(sem("l2a_qT"), 4)
            with pool.Fori(0, B // 2) as i:
                b = i * 2
                stage_queries("l2a", yT, b, 0)
                stage_queries("l2a", yT, b + 1, 1)
            norm("n6")
            norm("n7")
            pool.wait_ge(sem("xnT"), xnT_count("n7"))

            with pool.Fori(0, B // 2) as i:
                b = i * 2
                stage_queries("l3a", xnT, b, 0)
                stage_queries("l3a", xnT, b + 1, 1)
            norm("n8")

        @block.scalar
        def _(act):
            ch = Chain(act, sem("act_own"))
            act.wait_ge(sem("in_decay"), 16)
            act.activation(dk[:, 1:2], dk[:, 0:1], ACT.Sigmoid).then_inc(sem("decayed"), 1)
            act.sem_inc(sem("l1_exp"), 4)
            for u in range(DM * B + 1):
                if u < DM * B:
                    act.wait_ge(sem(f"in_ct{u % 3}"), 16 * (u // 3 + 1))
                    if u >= 3:
                        act.wait_ge(sem(f"parts_out{u % 3}"), 16 * (u // 3))
                    act.activation(part[u % 3][:, 0, :], ct[u % 3], ACT.Copy).then_inc(sem("kh_done"), 1)
                if u:
                    act.wait_ge(sem("rest_done"), u)
                    act.activation(part[(u - 1) % 3][:, 1, :], rest[(u - 1) % 2], ACT.Copy).then_inc(sem("km_done"), 1)
            act.wait_ge(sem("aw_dot"), 1)
            act.activation(awcol[:, :], aw_t[:, 0:1], ACT.Sigmoid).then_inc(sem("aw_sig"), 1)

            def transposed(name, dst=xnT):
                for j in range(2):
                    for m in range(DM):
                        act.wait_ge(sem("tr"), tr_count(name, 4 * (j + 1)))
                        act.activation(dst[:, m, j * HT:(j + 1) * HT], ps[:, 2 * j + m, 0:HT], ACT.Copy)\
                            .then_inc(sem("xnT"), 1)

            def router(r, f):
                act.wait_ge(sem("r_shift"), ROUTERS.index(r) + 1)
                act.activation(rp[:, 0:B * f.E], rp[:, 0:B * f.E], ACT.Exp).then_inc(sem("r_exp"), 1)
                for j in range(2):
                    act.wait_ge(sem("r_wT"), ROUTERS.index(r) * B + 4 * (j + 1))
                    act.activation(Wb[:, j * HT:(j + 1) * HT], ps[:, 5 + j, 0:HT], ACT.Copy)\
                        .then_inc(sem("w_ready"), 1)

            def ffn(f):
                def unit(c, hf):
                    act.wait_ge(sem(f.name + "_gu_done"), 2 * c + (hf + 1))
                    act.activation(sg[hf][:, :], ps[:, 2 * hf, 0:HT], ACT.Silu).then_inc(sem(f.name + "_silu"), 1)

                if f.gated:
                    head = 3 if f.C % 2 else 2
                    for c in range(head):
                        for hf in range(2):
                            unit(c, hf)
                    with act.Fori(head, f.C, 1) as c:
                        for hf in range(2):
                            unit(c, hf)
                for m in range(DM):
                    act.wait_ge(sem(f.name + "_down_done"), 2 * f.C)
                    act.activation(yT[:, m, 0:HT], ps[:, 4 + 2 * m, 0:HT], ACT.Copy).then_inc(sem(f.name + "_yT"), 1)

            transposed("n2")
            router("l0", FFN0)
            act.wait_ge(sem("w_ready"), w_count("l0"))
            for n in range(3):
                act.wait_ge(sem(f"parts_out{n}"), 16 * ((DM * B + 2 - n) // 3))
            act.wait_ge(sem("merged_out"), 32)
            v_load(act, 0)
            for k in range(2):
                for s in range(SETS):
                    stack_loads(act, k, k, s)
            ffn(FFN0)

            def query_copy(b, k, n):
                act.wait_ge(sem("l1_qtr"), b * 2 + (n + 1))
                act.activation(qs[k][0:96, 8 * n:8 * n + 8, :],
                               ps[0:96, 7, :].bitcast(BF16)[:, 0:8 * Q].rearrange("p (h q) -> p h q", h=8), ACT.Copy)\
                    .then_inc(sem("bank7"), 1)

            def max_copy(b, k, s):
                act.wait_ge(sem("l1_mtr"), b * SETS + (s + 1))
                act.activation(qs[k][96:97, GRP * s:GRP * s + GRP, :],
                               ps[96:97, 7, 0:GRP * Q].rearrange("p (h q) -> p h q", h=GRP), ACT.Copy).then_inc(sem("bank7"), 1)

            def sums_copies(b):
                act.wait_ge(sem("l1_pv"), b * HEADS + (HEADS + 2))
                for g in range(GRP):
                    act.activation(ot[32 * g:32 * g + VW, :], ps[32 * g:32 * g + VW, 6, 0:SETS * Q], ACT.Copy).then_inc(sem("l1_ot"), 1)

            def exps(b, h):
                n = b * HEADS + h
                act.wait_ge(sem("l1_pv"), n + 1)
                for j in range(3):
                    act.wait_ge(sem("l1_sc"), n * 3 + (j + 1 + 6 * HEADS))
                    for c0, c1, rows in (((0, 4, 128),), ((4, 8, 128),), ((8, 10, 128), (10, 12, CA)))[j]:
                        act.activation(pr[h % 2][0:rows, c0:c1, :],
                                       ps[0:rows, 3 + j, (c0 - 4 * j) * Q:(c1 - 4 * j) * Q].rearrange("p (c q) -> p c q", q=Q),
                                       ACT.Exp, scale=HD ** -0.5).then_inc(sem("l1_exp"), 1)

            def batch(b, k, ahead=True, before=True):
                for h in range(HEADS):
                    exps(b, h)
                    if h == 0 and before:
                        sums_copies(b - 1)
                    if h < 2 and ahead:
                        query_copy(b + 1, 1 - k, h)
                    if h == LAG:
                        max_copy(b, k, SETS - 1)
                    elif h % GRP == LAG and ahead:
                        max_copy(b + 1, 1 - k, h // GRP - 1)

            for n in range(2):
                query_copy(0, 0, n)
            for s in range(SETS - 1):
                max_copy(0, 0, s)
            batch(0, 0, before=False)
            batch(1, 1)
            with act.Fori(1, (B - 2) // 2) as i:
                batch(i * 2, 0)
                batch(i * 2 + 1, 1)
            batch(B - 2, 0)
            batch(B - 1, 1, ahead=False)
            sums_copies(B - 1)

            transposed("n4")
            router("l1r", FFN1)
            ffn(FFN1)
            transposed("n5")

            def single(name):
                act.sem_inc(sem(name + "_pt"), 3)

                def body(b, k):
                    act.wait_ge(sem(name + "_max"), b + 1)
                    act.activation(pb[k], sc, ACT.Exp, bias=nmx, accum_out=ssum).then_inc(sem(name + "_exp"), 1)
                    for j in range(3):
                        act.wait_ge(sem(name + "_ptr"), b * 3 + (j + 1))
                        if j < 2:
                            act.activation(ptt[:, 4 * j:4 * j + 4, :],
                                           ps[:, 3 + j, 0:4 * Q].rearrange("p (c q) -> p c q", c=4), ACT.Copy)\
                                .then_inc(sem(name + "_pt"), 1)
                        else:
                            ch.add(act.activation(ptt[:, 8:10, :],
                                                  ps[:, 5, 0:2 * Q].rearrange("p (c q) -> p c q", c=2), ACT.Copy))
                            ch.add(act.activation(ptt[0:CB[0], 10, :], ps[0:CB[0], 5, 2 * Q:3 * Q], ACT.Copy))
                            act.activation(ptt[0:CB[1], 11, :], ps[0:CB[1], 5, 3 * Q:4 * Q], ACT.Copy)\
                                .then_inc(sem(name + "_pt"), 1)

                with act.Fori(0, B // 2) as i:
                    b = i * 2
                    ch.enter(i, 0, 4)
                    body(b, 0)
                    body(b + 1, 1)
                    ch.leave(B // 2, 4)

            single("l2a")
            transposed("n6")
            router("l2r", FFN2)
            ffn(FFN2)
            transposed("n7")
            single("l3a")
            transposed("n8")
            router("l3r", FFN3)
            ffn(FFN3)

        @block.tensor
        def _(pe):
            def mm(o, l, r, start, stop, **kw):
                return pe.matmul(o, l, r, start=start, stop=stop, **kw)

            pe.wait_ge(sem("zeroed"), 5)
            pe.wait_ge(sem("in_const"), 48)
            pe.wait_ge(sem("in_lora"), 9 * 16)
            pe.wait_ge(sem("in_blk"), 20 * 16)
            for c in range(FFN1.C):
                if c >= 2:
                    pe.wait_ge(sem("merged"), 2 * (c - 1))
                k = 2 + 2 * (c % 2)
                for m in range(DM):
                    last = mm(ps[:, k, m * 256:m * 256 + 256], agup[:, m * 128:m * 128 + 128], bblk[:, c, :], True, True)
                last = mm(ps[:, k + 1, 0:D], adn[:, c, :], bdn, True, True)
                last.then_inc(sem("lora"), 1)
            for m in range(DM):
                last = mm(ps[:, 6, m * 8:m * 8 + 8], glA[:, m * 128:m * 128 + 128], glB, True, True)
            last.then_inc(sem("lora_gate"), 1)
            pe.wait_ge(sem("wkv_ready"), 1)
            pe.wait_ge(sem("in_l0w"), 96)
            for e in range(DM):
                for m in range(DM):
                    last = mm(ps[:, 7, e * B:(e + 1) * B], winT[:, m, e * 128:e * 128 + 128], wkv[:, m, :], m == 0, m == DM - 1)
            last.then_inc(sem("s1_done"), 1)
            pe.wait_ge(sem("s1_ready"), 2)
            for b in range(B):
                for m in range(DM):
                    last = mm(ps[0:Q, b // 2, (b % 2) * D:(b % 2) * D + D], s1r[:, m, b, :], woutT[:, m, :], m == 0, m == DM - 1)
            last.then_inc(sem("summed"), 1)

            def transposes(name):
                for b in range(B):
                    pe.wait_ge(sem("xn"), xn_count(name, b + 1))
                    for m in range(DM):
                        last = pe.transpose(ps[:, 2 * (b // 4) + m, (b % 4) * Q:(b % 4) * Q + Q],
                                            xn[:, b, m * 128:m * 128 + 128], ident[0:Q, 0:Q])
                    last.then_inc(sem("tr"), 1)

            def router(name, r, f, n):
                pe.wait_ge(sem("xnT"), xnT_count(name))
                for b in range(B):
                    for m in range(DM):
                        last = mm(ps[0:Q, 4, b * f.E:(b + 1) * f.E], xnT[:, m, b * Q:(b + 1) * Q], gate[n][:, m, :], m == 0, m == DM - 1)
                last.then_inc(sem("r_logits"), 1)
                if r == "l2r":
                    pe.wait_ge(sem("l2r_onehot"), 1)
                    for b in range(B):
                        last = pe.transpose(ps[:, 5 + b // 4, (b % 4) * Q:(b % 4) * Q + Q],
                                            oh[:, b * 256 + 128:b * 256 + 256], ident[0:Q, 0:Q])
                    last.then_inc(sem("l2r_secT"), 1)
                    pe.wait_ge(sem("l2r_secT_sb"), 1)
                    for b in range(B):
                        last = mm(ps[0:Q, b // 4, (b % 4) * 128:(b % 4) * 128 + 128], secT[:, b * Q:(b + 1) * Q], simb[:, :], True, True)
                    last.then_inc(sem("l2r_sims"), 1)
                pe.wait_ge(sem("r_wrep"), ROUTERS.index(r) + 1)
                for b in range(B):
                    pe.transpose(ps[:, 5 + b // 4, (b % 4) * Q:(b % 4) * Q + Q], wrep[:, b, :], ident[0:Q, 0:Q])\
                        .then_inc(sem("r_wT"), 1)

            def ffn(f):
                nm = f.name

                def gu(c, k, hf):
                    if hf == 0:
                        pe.wait_ge(sem(f"{nm}_wgu{k}"), (c // 2 + 1 if isinstance(c, int) else c[1]) * 16)
                    cc = c if isinstance(c, int) else c[0]
                    if not isinstance(c, int) or c >= 1:
                        pe.wait_ge(sem(nm + "_h"), 2 * cc + (hf - 1))
                    for w in range(2 if f.gated else 1):
                        for m in range(DM):
                            at = (m * 2 + w) * 128 if f.gated else m * 128
                            last = mm(ps[:, 2 * hf + w, 0:HT], wgu[k][:, at:at + 128], xnT[:, m, hf * HT:(hf + 1) * HT],
                                      m == 0, m == DM - 1)
                    last.then_inc(sem(nm + "_gu_done"), 1)

                def down(c, k, hf, first):
                    cc = c if isinstance(c, int) else c[0]
                    if hf == 0:
                        pe.wait_ge(sem(f"{nm}_wd{k}"), (c // 2 + 1 if isinstance(c, int) else c[1]) * 16)
                    pe.wait_ge(sem(nm + "_h"), 2 * cc + (hf + 1))
                    for m in range(DM):
                        last = mm(ps[:, 4 + 2 * m + hf, 0:HT], wd[k][:, m * 128:m * 128 + 128], hb[hf][:, :],
                                  first, True, skip_group_check=True)
                    last.then_inc(sem(nm + "_down_done"), 1)

                def chunk(c, k, prev, pk, prev_first):
                    gu(c, k, 0)
                    if prev is not None:
                        down(prev, pk, 1, prev_first)
                    gu(c, k, 1)
                    down(c, k, 0, prev is None)

                head = 3 if f.C % 2 else 2
                for c in range(head):
                    chunk(c, c % 2, c - 1 if c else None, (c - 1) % 2, c == 1)
                if f.C - head > 2:
                    with pe.Fori(0, (f.C - head) // 2) as i:
                        k0 = head % 2
                        c = i * 2 + head
                        n0 = i + (head // 2 + 1)
                        chunk((c, n0), k0, (c - 1, None), 1 - k0, False)
                        chunk((c + 1, i + ((head + 1) // 2 + 1)), 1 - k0, (c, None), k0, False)
                else:
                    for c in range(head, f.C):
                        chunk(c, c % 2, c - 1, (c - 1) % 2, False)
                down(f.C - 1, (f.C - 1) % 2, 1, False)
                pe.wait_ge(sem(nm + "_yT"), 4)
                for b in range(B):
                    for m in range(DM):
                        last = pe.transpose(ps[0:Q, b // 2, (b % 2) * D + m * 128:(b % 2) * D + m * 128 + 128],
                                            yT[:, m, b * Q:(b + 1) * Q], ident[:, :])
                    if b % 2:
                        last.then_inc(sem(nm + "_back"), 1)

            transposes("n2")
            router("n2", "l0", FFN0, 0)
            pe.wait_ge(sem("w_ready"), w_count("l0"))
            ffn(FFN0)

            pe.wait_ge(sem("far_ready"), 1)

            def query_turn(b, k, n):
                if n == 0:
                    pe.wait_ge(sem("l1_xs"), b * 4 + 4)
                if not isinstance(b, int) or b or n:
                    pe.wait_ge(sem("bank7"), q_turn(b, n))
                for h in range(8):
                    last = pe.transpose(ps[0:96, 7, :].bitcast(BF16)[:, h * Q:(h + 1) * Q],
                                        xs[k][:, 8 * n + h, :, :].rearrange("q t r -> q (t r)"), identb[:, :])
                last.then_inc(sem("l1_qtr"), 1)

            def max_turn(b, k, s):
                pe.wait_ge(sem("l1_nmax"), b * SETS + (s + 1))
                pe.wait_ge(sem("bank7"), m_turn(b, s))
                for g in range(GRP):
                    h = GRP * s + g
                    last = mm(ps[96:97, 7, g * Q:(g + 1) * Q], nm[k][:, h:h + 1], identb[:, :], True, True)
                last.then_inc(sem("l1_mtr"), 1)

            def skip_turns(turn, n):
                pe.wait_ge(sem("bank7"), turn)
                pe.sem_inc(sem("bank7"), n)

            def a_head(b, k, h):
                if h % GRP == 0:
                    s = h // GRP
                    pe.wait_ge(sem(f"in_stk{k}{s}"), b[1] if isinstance(b, tuple) else 96 * (b // 2 + 1))
                b = b[0] if isinstance(b, tuple) else b
                if h == 0:
                    pe.wait_ge(sem("bank7"), q_turn(b, 1) + 1)
                for j, a in enumerate(A0):
                    pe.wait_ge(sem("l1_amax"), b * (3 * HEADS) + (3 * h + j + 1))
                    last = mm(ps[0:Q, j, 0:AW], qs[k][0:96, h, :], kstk[k][0:96, h, a:a + AW], True, True)
                    if j == 2:
                        last = mm(ps[0:Q, 2, AW - Q:AW], identb[:, :], farb[:, :], False, True, skip_group_check=True)
                    last.then_inc(sem("l1_a"), 1)

            def chunk_keys(c):
                return (c * 128, 128) if c < FULL else (FULL * 128 + CA * (c - FULL), CA)

            def b_scores(b, k, h):
                if h % GRP == 0:
                    pe.wait_ge(sem("bank7"), m_turn(b, h // GRP) + 1)
                for j in range(3):
                    pe.wait_ge(sem("l1_exp"), (b * HEADS + h) * 4 + (1, 2, 4)[j])
                    for c in range(4 * j, 4 * j + 4):
                        at, n = chunk_keys(c)
                        last = mm(ps[0:n, 3 + j, (c % 4) * Q:(c % 4) * Q + Q], kstk[k][0:97, h, at:at + n],
                                  qs[k][0:97, h, :], True, True)
                    last.then_inc(sem("l1_sc"), 1)

            def b_values(b, k, h):
                s, g = h // GRP, h % GRP
                pe.wait_ge(sem("l1_masked"), b * HEADS + (h + 1))
                if h == 0:
                    if not isinstance(b, int) or b:
                        pe.wait_ge(sem("l1_ot"), b * GRP)
                    pe.wait_ge(sem("l1_vaug"), b * NCH + NCH)
                for c in range(NCH):
                    n = 128 if c < FULL else CA
                    last = mm(ps[32 * g:32 * g + VW, 6, s * Q:(s + 1) * Q], vaug[k][0:n, c, h, :], pr[h % 2][0:n, c, :],
                              c == 0, c == NCH - 1)
                last.then_inc(sem("l1_pv"), 1)

            def out_turn(b):
                pe.wait_ge(sem("l1_ot"), b * GRP + GRP)
                pe.wait_ge(sem("bank7"), o_turn(b) if not (isinstance(b, int) and b == B - 1) else m_turn(b, SETS - 1) + 1)
                for s in range(SETS):
                    last = pe.transpose(ps[0:Q, 7, s * 128:(s + 1) * 128], ot[:, s * Q:(s + 1) * Q], ident[:, :])
                last.then_inc(sem("l1_oT"), 1)

            def both(b, k, na, before=True):
                for h in range(HEADS):
                    b_scores(b, k, h)
                    if h < LAG:
                        a_head(b, k, HEADS - LAG + h)
                    elif na is not None:
                        a_head((b + 1, na), 1 - k, h - LAG)
                    if h:
                        b_values(b, k, h - 1)
                    elif before:
                        b_values(b - 1, 1 - k, HEADS - 1)
                    if h < 2:
                        if na is not None:
                            query_turn(b + 1, 1 - k, h)
                        else:
                            skip_turns(q_turn(b + 1, h), 1)
                    elif h == 2:
                        if before:
                            out_turn(b - 1)
                        else:
                            skip_turns(o_turn(b - 1), 1)
                    elif h == LAG:
                        max_turn(b, k, SETS - 1)
                    elif h % GRP == LAG and na is not None:
                        max_turn(b + 1, 1 - k, h // GRP - 1)

            pe.sem_inc(sem("l1_pv"), 2)
            pe.sem_inc(sem("l1_sc"), 6 * HEADS)
            for n in range(2):
                query_turn(0, 0, n)
            skip_turns(q_turn(0, 1) + 1, 2)
            for h in range(HEADS - LAG):
                a_head((0, 96) if h % GRP == 0 else 0, 0, h)
                if h and h % GRP == 0:
                    max_turn(0, 0, h // GRP - 1)
            both(0, 0, 96, before=False)
            both(1, 1, 192)
            with pe.Fori(1, (B - 2) // 2) as i:
                both(i * 2, 0, (i + 1) * 96)
                both(i * 2 + 1, 1, (i + 2) * 96)
            both(B - 2, 0, B // 2 * 96)
            both(B - 1, 1, None)
            b_values(B - 1, 1, HEADS - 1)
            out_turn(B - 1)

            transposes("n4")
            router("n4", "l1r", FFN1, 1)
            pe.wait_ge(sem("w_ready"), w_count("l1r"))
            ffn(FFN1)
            transposes("n5")
            pe.wait_ge(sem("xnT"), xnT_count("n5"))
            pe.wait_ge(sem("in_qkv"), 48)
            for w in range(2):
                for e in range(DM):
                    for hf in range(2):
                        for m in range(DM):
                            last = mm(ps[:, 4 * w + 2 * e + hf, 0:HT], wqkv[:, w, m, e * 128:e * 128 + 128],
                                      xnT[:, m, hf * HT:(hf + 1) * HT], m == 0, m == DM - 1)
                last.then_inc(sem("l2_proj"), 1)
            for b in range(B):
                if b < 4:
                    pe.wait_ge(sem("l2a_qT"), 4)
                else:
                    pe.wait_ge(sem("l2_vnew"), b - 3)
                for m in range(DM):
                    last = mm(ps[0:Q, b % 4, 0:D], xnT[:, m, b * Q:(b + 1) * Q], wqkv[:, 2, m, :], m == 0, m == DM - 1)
                last.then_inc(sem("l2_vproj"), 1)

            def single(name, new):
                def scores(b, k, n):
                    pe.wait_ge(sem(f"{name}_ink{k}"), n * 16)
                    pe.wait_ge(sem(name + "_q"), b + 1)
                    pe.wait_ge(sem(name + "_scfree"), b + 2)
                    for j, (a, w) in enumerate(((0, 512), (512, 512), (1024, T - 1024))):
                        if new and j == 2:
                            w -= Q
                        for m in range(DM):
                            last = mm(ps[0:Q, j, 0:w], qst[k][:, m, :], ctT[k][:, m, a:a + w], m == 0, m == DM - 1)
                    if new:
                        for m in range(DM):
                            last = mm(ps[0:Q, 2, w:w + Q], qst[k][:, m, :], knT[:, m, bass.ds(b * Q, Q)], m == 0, m == DM - 1)
                    last.then_inc(sem(name + "_sc"), 1)

                def values(b, k, turn):
                    pe.wait_ge(sem(name + "_p"), b + 1)
                    at = 0
                    for c in range(NCH):
                        n = 128 if c < FULL else CB[c - FULL]
                        if c % 4 == 0:
                            pe.wait_ge(sem(name + "_pt"), b * 3 + (c // 4 + 1))
                        last = pe.transpose(ps[0:n, 3 + c // 4, (c % 4) * Q:(c % 4) * Q + Q], pb[k][:, at:at + n], ident[0:Q, 0:Q])
                        at += n
                        if c % 4 == 3:
                            last.then_inc(sem(name + "_ptr"), 1)
                    pe.wait_ge(sem(name + "_ofree"), b + 1)
                    pe.wait_ge(sem(f"{name}_inv{k}"), turn * 48)
                    for c in range(NCH):
                        n = 128 if c < FULL else CB[c - FULL]
                        if c % 4 == 0:
                            pe.wait_ge(sem(name + "_pt"), b * 3 + (c // 4 + 4))
                        v = vnew[:, bass.ds(b, 1), :].rearrange("q a d -> q (a d)") if new and c == NCH - 1 else vn2[k][0:n, c, :]
                        last = mm(ps[0:Q, 6, 0:D], ptt[0:n, c, :], v, c == 0, c == NCH - 1)
                    last.then_inc(sem(name + "_o"), 1)

                pe.sem_inc(sem(name + "_sc"), 2)
                pe.sem_inc(sem(name + "_o"), 2)
                scores(0, 0, 1)
                with pe.Fori(0, (B - 2) // 2) as i:
                    scores(i * 2 + 1, 1, i + 1)
                    values(i * 2, 0, i + 1)
                    scores(i * 2 + 2, 0, i + 2)
                    values(i * 2 + 1, 1, i + 1)
                scores(B - 1, 1, B // 2)
                values(B - 2, 0, B // 2)
                values(B - 1, 1, B // 2)

            pe.wait_ge(sem("l2_vnew"), B)
            pe.wait_ge(sem("l2a_kT"), 4)
            single("l2a", True)
            transposes("n6")
            router("n6", "l2r", FFN2, 2)
            pe.wait_ge(sem("w_ready"), w_count("l2r"))
            ffn(FFN2)
            transposes("n7")
            pe.wait_ge(sem("xnT"), xnT_count("n7"))
            single("l3a", False)
            transposes("n8")
            router("n8", "l3r", FFN3, 3)
            pe.wait_ge(sem("w_ready"), w_count("l3r"))
            for hf in range(2):
                last = mm(ps[:, 1 + 2 * hf, 0:HT], awmat[:, :], Wb[:, hf * HT:(hf + 1) * HT], True, True)
            last.then_inc(sem("l3_gate"), 1)
            ffn(FFN3)

        @block.vector
        def _(dve):
            ch = Chain(dve, sem("dve_own"))
            link, add = ch.link, ch.add

            def bc(ap, shape):
                return ap.broadcast_to(shape)

            dve.sem_inc(sem("l1_amax"), 3)
            dve.wait_ge(sem("decayed"), 1)
            link(dve.memset(orow, 1.0))
            link(dve.tensor_scalar(krow, orow, dk[:, 1:2], None, ALU.mult))
            link(dve.tensor_tensor_scan(crow[:, ::-1], krow, orow, 0.0, ALU.mult, ALU.add))
            link(dve.tensor_reduce(csum[:, 0:1], crow, AX.X, ALU.add))
            for u in range(DM * B):
                dve.wait_ge(sem(f"in_ct{u % 3}"), 16 * (u // 3 + 1))
                add(dve.tensor_tensor_reduce(out=prod, in0=ct[u % 3], in1=crow, scale=1.0 / T, scalar=0.0, op0=ALU.mult, op1=ALU.add,
                                             accum_out=wkv[:, u % DM, u // DM:u // DM + 1]))
                dve.wait_ge(sem("kh_done"), u + 1)
                if u >= 2:
                    dve.wait_ge(sem("kl_done"), u - 1)
                ch.wait()
                dve.tensor_tensor(rest[u % 2], ct[u % 3], part[u % 3][:, 0, :], ALU.subtract).then_inc(sem("rest_done"), 1)
            dve.engine_nop().then_inc(sem("wkv_ready"), 1)
            dve.wait_ge(sem("in_lora"), 9 * 16)
            link(dve.tensor_tensor(aw_t, attr_r, wa_b, ALU.mult))
            dve.tensor_reduce(aw_t[:, 0:1], aw_t, AX.X, ALU.add).then_inc(sem("aw_dot"), 1)
            for c in range(FFN1.C):
                dve.wait_ge(sem("lora"), c + 1)
                k = 2 + 2 * (c % 2)
                dve.scalar_tensor_tensor(mgu[:, c, :], ps[:, k, :], 2.0, mgu[:, c, :], ALU.mult, ALU.add).then_inc(sem("merged"), 1)
                dve.scalar_tensor_tensor(mdn[:, c, :], ps[:, k + 1, 0:D], 2.0, mdn[:, c, :], ALU.mult, ALU.add).then_inc(sem("merged"), 1)
            dve.wait_ge(sem("lora_gate"), 1)
            dve.wait_ge(sem("in_gate"), 64)
            add(dve.scalar_tensor_tensor(gate[1][:, :, :], ps[:, 6, 0:16].rearrange("p (m e) -> p m e", m=DM), 2.0, gate[1][:, :, :], ALU.mult, ALU.add))
            dve.wait_ge(sem("in_blk"), 20 * 16)
            add(dve.tensor_scalar(awmat[:, :], ident[:, :], -1.0, 1.0, ALU.mult, ALU.add))
            ch.wait()
            link(dve.tensor_tensor(simb[:, :], simb[:, :], awmat[:, :], ALU.mult))
            link(dve.tensor_tensor(simb[:, :], simb[:, :], ident[:, :], ALU.add))
            dve.wait_ge(sem("aw_sig"), 1)
            link(dve.memset(awmat[:, :], 0.2 / FFN3.rep))
            link(dve.tensor_scalar(awmat[:, :], awmat[:, :], awcol[:, :], None, ALU.mult))

            def stats(name, src):
                for b in range(B):
                    add(dve.bn_stats(stat[:, b, :], src[:, b, :]))
                ch.wait()
                for b in range(B):
                    last = dve.bn_aggr(mv[:, b, :], stat[:, b, :])
                    if b < B - 1:
                        add(last)
                last.then_inc(sem("stat"), 1)
                dve.wait_ge(sem("rstd"), NORMS.index(name) + 1)

            def norm(name, src=x):
                stats(name, src)
                for b in range(B):
                    dve.tensor_scalar(xn[:, b, :], src[:, b, :], mv[:, b, 0:1], rstd[:, b:b + 1], ALU.subtract, ALU.mult)\
                        .then_inc(sem("xn"), 1)

            dve.wait_ge(sem("in_x"), 16)
            norm("n0")
            dve.wait_ge(sem("s1_done"), 1)
            for m in range(DM):
                link(dve.tensor_scalar(csum[:, 1:2], csum[:, 0:1], bin_c[:, m:m + 1], 1.0 / T, ALU.mult, ALU.mult))
                link(dve.tensor_scalar(s1[:, m, :], ps[:, 7, m * B:(m + 1) * B], csum[:, 1:2], None, ALU.add))
            for m in range(DM):
                dve.tensor_copy(s1r[:, m, :, :], bc(s1[:, m, :].unsqueeze(2), [128, B, Q])).then_inc(sem("s1_ready"), 1)
            dve.wait_ge(sem("summed"), 1)
            dve.wait_ge(sem("xn"), xn_count("n0"))
            for j in range(4):
                add(dve.tensor_tensor(xn[:, 2 * j:2 * j + 2, :], xn[:, 2 * j:2 * j + 2, :], ps[0:Q, j, :].rearrange("q (b d) -> q b d", b=2), ALU.add))
            ch.wait()
            link(dve.tensor_tensor(xn[:, :, :], xn[:, :, :], bc(bout_b.unsqueeze(1), [Q, B, D]), ALU.add))
            norm("n1", xn)
            dve.wait_ge(sem("xn"), xn_count("n1"))
            link(dve.tensor_tensor(xn[:, :, :], xn[:, :, :], bc(gam_b.unsqueeze(1), [Q, B, D]), ALU.mult))
            link(dve.tensor_tensor(x[:, :, :], x[:, :, :], xn[:, :, :], ALU.add))
            link(dve.tensor_tensor(x[:, :, :], x[:, :, :], bc(bet_b.unsqueeze(1), [Q, B, D]), ALU.add))

            def router(r, f):
                E, K = f.E, f.K

                def v3(t):
                    return t[:, 0:B * E].rearrange("q (b e) -> q b e", b=B)

                dve.wait_ge(sem("r_logits"), ROUTERS.index(r) + 1)
                link(dve.tensor_copy(rl[:, 0:B * E], ps[0:Q, 4, 0:B * E]))
                link(dve.tensor_reduce(rmx, v3(rl), AX.X, ALU.max))
                dve.tensor_tensor(v3(rp), v3(rl), bc(rmx.unsqueeze(2), [Q, B, E]), ALU.subtract).then_inc(sem("r_shift"), 1)
                dve.wait_ge(sem("r_exp"), ROUTERS.index(r) + 1)
                link(dve.tensor_reduce(rsum, v3(rp), AX.X, ALU.add))
                link(dve.reciprocal(rsum, rsum))
                link(dve.tensor_tensor(v3(rp), v3(rp), bc(rsum.unsqueeze(2), [Q, B, E]), ALU.mult))
                src = v3(rl) if r == "l3r" else v3(rp)
                for b in range(B):
                    add(dve.max(v8[:, b, :], src[:, b, :]))
                ch.wait()
                for b in range(B):
                    add(dve.max_index(i8[:, b, :], v8[:, b, :], src[:, b, :]))
                ch.wait()
                link(dve.tensor_copy(if8, i8))
                o = oh[:, 0:B * K * E].rearrange("q (b k e) -> q b k e", b=B, k=K)
                ins = dve.tensor_tensor(o, bc(iota[:, 0:E].unsqueeze(1).unsqueeze(1), [Q, B, K, E]),
                                        bc(if8[:, :, 0:K].unsqueeze(3), [Q, B, K, E]), ALU.is_equal)
                w = v3(rw)
                if r != "l2r":
                    link(ins)
                    link(dve.tensor_reduce(v3(rsel), o.rearrange("q b k e -> q b e k"), AX.X, ALU.add))
                    link(dve.tensor_tensor(w, v3(rp), v3(rsel), ALU.mult))
                    if r != "l0":
                        link(dve.tensor_reduce(rsum, w, AX.X, ALU.add))
                        if r == "l3r":
                            link(dve.tensor_scalar(rsum, rsum, 1e-8, None, ALU.add))
                        link(dve.reciprocal(rsum, rsum))
                        link(dve.tensor_tensor(w, w, bc(rsum.unsqueeze(2), [Q, B, E]), ALU.mult))
                else:
                    ins.then_inc(sem("l2r_onehot"), 1)
                    dve.wait_ge(sem("l2r_onehot"), 1)
                    link(dve.tensor_reduce(rsum, v8, AX.X, ALU.add))
                    link(dve.tensor_scalar(rsum, rsum, 1e-12, None, ALU.max))
                    link(dve.reciprocal(rsum, rsum))
                    link(dve.tensor_tensor(w8, v8, bc(rsum.unsqueeze(2), [Q, B, 8]), ALU.mult))
                    dve.wait_ge(sem("l2r_secT"), 1)
                    add(dve.tensor_copy(secT[:, 0:HT], ps[:, 5, 0:HT]))
                    ch.wait()
                    dve.tensor_copy(secT[:, HT:TOK], ps[:, 6, 0:HT]).then_inc(sem("l2r_secT_sb"), 1)
                    dve.wait_ge(sem("l2r_sims"), 1)
                    for j in range(2):
                        add(dve.tensor_copy(scand[:, j * 512:j * 512 + 512], ps[0:Q, j, :]))
                    ch.wait()
                    for b in range(B):
                        add(dve.tensor_tensor(cand[:, b * 512:(b + 1) * 512].rearrange("q (j i e) -> q j i e", j=4, i=4),
                                              bc(scand[:, b * 128:(b + 1) * 128].rearrange("q (j e) -> q j e", j=4).unsqueeze(2), [Q, 4, 4, 32]),
                                              bc(o[:, b, 0:4, :].unsqueeze(1), [Q, 4, 4, 32]), ALU.mult))
                    ch.wait()
                    link(dve.tensor_reduce(pick, cand.rearrange("q (b j i e) -> q (b j) i e", b=B, j=4, i=4), AX.X, ALU.add))
                    link(dve.tensor_reduce(best, pick, AX.X, ALU.max))
                    link(dve.tensor_scalar(keep, best, 0.5, None, ALU.is_lt))
                    link(dve.tensor_scalar(left, keep, -1.0, 1.0, ALU.mult, ALU.add))
                    link(dve.tensor_tensor(pick, pick, bc(best.unsqueeze(3), [Q, B, 4, 4]), ALU.is_equal))
                    for i in range(4):
                        link(dve.tensor_tensor(first[:, :, :, i], left, pick[:, :, :, i], ALU.mult))
                        if i < 3:
                            link(dve.tensor_tensor(left, left, first[:, :, :, i], ALU.subtract))
                    link(dve.tensor_tensor(first, first, bc(w8[:, :, 4:8].unsqueeze(3), [Q, B, 4, 4]), ALU.mult))
                    link(dve.tensor_reduce(moved, first.rearrange("q b j i -> q b i j"), AX.X, ALU.add))
                    link(dve.tensor_tensor(w8[:, :, 0:4], w8[:, :, 0:4], moved, ALU.add))
                    link(dve.tensor_tensor(w8[:, :, 4:8], w8[:, :, 4:8], keep, ALU.mult))
                    link(dve.tensor_tensor(o, o, bc(w8.unsqueeze(3), [Q, B, 8, 32]), ALU.mult))
                    link(dve.tensor_reduce(w, o.rearrange("q b k e -> q b e k"), AX.X, ALU.add))
                dve.tensor_copy(wrep.rearrange("q b (e r) -> q b e r", e=E), bc(w.unsqueeze(3), [Q, B, E, f.rep]))\
                    .then_inc(sem("r_wrep"), 1)
                dve.wait_ge(sem("w_ready"), w_count(r))
                if r == "l3r":
                    dve.wait_ge(sem("l3_gate"), 1)
                    for hf in range(2):
                        t = Wb[:, hf * HT:(hf + 1) * HT]
                        add(dve.scalar_tensor_tensor(t, ps[:, 1 + 2 * hf, 0:HT], 0.9, t, ALU.add, ALU.mult))
                    ch.wait()

            def ffn(f):
                nm = f.name

                def unit(c, hf, weighted, i=None):
                    if f.gated:
                        dve.wait_ge(sem(nm + "_silu"), 2 * c + (hf + 1))
                        if weighted:
                            link(dve.tensor_tensor(sg[hf][:, :], sg[hf][:, :], Wb[:, hf * HT:(hf + 1) * HT], ALU.mult))
                        a, o = sg[hf][:, :], ps[:, 2 * hf + 1, 0:HT]
                    else:
                        dve.wait_ge(sem(nm + "_gu_done"), 2 * c + (hf + 1))
                        a, o = Wb[:, hf * HT:(hf + 1) * HT], ps[:, 2 * hf, 0:HT]
                    if not isinstance(c, int) or c >= 1:
                        dve.wait_ge(sem(nm + "_down_done"), 2 * c + (hf - 1))
                    dve.tensor_tensor(hb[hf][:, :], a, o, ALU.mult).then_inc(sem(nm + "_h"), 1)

                head = 3 if f.C % 2 else 2
                if f.C - head <= 2:
                    head = f.C
                for c in range(head):
                    for hf in range(2):
                        unit(c, hf, c >= f.shared)
                if head < f.C:
                    with dve.Fori(head, f.C, 1) as c:
                        ch.enter(c, head, 2)
                        for hf in range(2):
                            unit(c, hf, True)
                        ch.leave(f.C - head, 2)
                dve.wait_ge(sem(nm + "_down_done"), 2 * f.C)
                for m in range(DM):
                    dve.tensor_copy(yT[:, m, HT:TOK], ps[:, 5 + 2 * m, 0:HT]).then_inc(sem(nm + "_yT"), 1)
                for j in range(4):
                    dve.wait_ge(sem(nm + "_back"), j + 1)
                    o = ps[0:Q, j, :].rearrange("q (b d) -> q b d", b=2)
                    ins = dve.tensor_tensor(x[:, 2 * j:2 * j + 2, :], x[:, 2 * j:2 * j + 2, :], o, ALU.add)
                    if nm == "l3":
                        ins.then_inc(sem("l3_x"), 1)
                    else:
                        add(ins)
                ch.wait()

            norm("n2")
            for n in range(3):
                dve.wait_ge(sem(f"parts_out{n}"), 16 * ((DM * B + 2 - n) // 3))
            router("l0", FFN0)
            ffn(FFN0)
            norm("n3")

            def l1_o(b):
                dve.wait_ge(sem("l1_oT"), b + 1)
                o = ps[0:Q, 7, :].rearrange("q (h v) -> q h v", h=HEADS)
                link(dve.reciprocal(den[:, :], o[:, :, HD]))
                link(dve.tensor_tensor(att[:, :, :], o[:, :, 0:HD], bc(den[:, :].unsqueeze(2), [Q, HEADS, HD]), ALU.mult))
                dve.sem_inc(sem("bank7"), 1)
                xb = x[:, bass.ds(b, 1), :].rearrange("q a d -> q (a d)")
                add(dve.tensor_tensor(xb, xb, att[:, :, :].rearrange("q h v -> q (h v)"), ALU.add))

            def l1_a(b, k):
                for h in range(HEADS):
                    s = h // GRP
                    if h % GRP == 0 and not (isinstance(b, int) and b == h == 0):
                        dve.wait_ge(sem("l1_nmax"), b * SETS + s)
                    for j in range(3):
                        dve.wait_ge(sem("l1_a"), b * (3 * HEADS) + (3 * h + j + 1))
                        dve.tensor_reduce(mx[:, h % GRP, j:j + 1], ps[0:Q, j, 0:AW], AX.X, ALU.max).then_inc(sem("l1_amax"), 1)
                    if h % GRP == GRP - 1:
                        dve.wait_ge(sem("l1_amax"), b * (3 * HEADS) + (3 * h + 6))
                        dve.tensor_reduce(nm[k][:, GRP * s:GRP * s + GRP], mx[:, :, :], AX.X, ALU.max, negate=True)\
                            .then_inc(sem("l1_nmax"), 1)

            l1_a(0, 0)
            l1_a(1, 1)
            l1_o(0)
            with dve.Fori(1, B // 2) as i:
                ch.enter(i, 1, 6)
                l1_a(i * 2, 0)
                l1_o(i * 2 - 1)
                l1_a(i * 2 + 1, 1)
                l1_o(i * 2)
                ch.leave(B // 2 - 1, 6)
            l1_o(B - 1)
            ch.wait()

            norm("n4")
            router("l1r", FFN1)
            ffn(FFN1)
            norm("n5")
            dve.wait_ge(sem("in_qkv"), 48)
            for w, dst in ((0, yT), (1, knT)):
                dve.wait_ge(sem("l2_proj"), w + 1)
                for e in range(DM):
                    for hf in range(2):
                        dve.tensor_scalar(dst[:, e, hf * HT:(hf + 1) * HT], ps[:, 4 * w + 2 * e + hf, 0:HT], bqk[:, w, e:e + 1], None, ALU.add)\
                            .then_inc(sem("l2a_qT" if w == 0 else "l2a_kT"), 1)
            dve.wait_ge(sem("l2a_kT"), 4)

            def single(name, masked):
                def front(b, k, n):
                    dve.wait_ge(sem(f"{name}_inm{k}"), n * 16)
                    if not masked:
                        link(dve.tensor_copy(bias[k], mk8[k]))
                        link(dve.tensor_reduce(anym[k], bias[k], AX.X, ALU.max))
                        link(dve.tensor_scalar(bias[k], bias[k], -1.0, -FAR, ALU.add, ALU.mult))
                    dve.wait_ge(sem(name + "_sc"), b + 3)
                    flat = ps[0:Q, 0:3, :].rearrange("q j n -> q (j n)")[:, 0:T]
                    dve.scalar_tensor_tensor(sc, flat, D ** -0.5, bias[k], ALU.mult, ALU.add).then_inc(sem(name + "_scfree"), 1)
                    dve.wait_ge(sem(name + "_scfree"), b + 3)
                    dve.tensor_reduce(nmx, sc, AX.X, ALU.max, negate=True).then_inc(sem(name + "_max"), 1)

                def middle(b, k):
                    dve.wait_ge(sem(name + "_exp"), b + 1)
                    link(dve.reciprocal(rsm, ssum))
                    if not masked:
                        link(dve.tensor_tensor(rsm, rsm, anym[k], ALU.mult))
                    dve.tensor_scalar(pb[k], pb[k], rsm, None, ALU.mult).then_inc(sem(name + "_p"), 1)

                def end(b):
                    dve.wait_ge(sem(name + "_o"), b + 3)
                    xb = x[:, bass.ds(b, 1), :].rearrange("q a d -> q (a d)")
                    dve.tensor_tensor(xb, xb, ps[0:Q, 6, 0:D], ALU.add).then_inc(sem(name + "_ofree"), 1)

                dve.sem_inc(sem(name + "_scfree"), 2)
                dve.sem_inc(sem(name + "_ofree"), 1)
                per = 1 if masked else 5
                front(0, 0, 1)
                with dve.Fori(0, B // 2 - 1) as i:
                    ch.enter(i, 0, 2 * per)
                    middle(i * 2, 0)
                    front(i * 2 + 1, 1, i + 1)
                    end(i * 2)
                    middle(i * 2 + 1, 1)
                    front(i * 2 + 2, 0, i + 2)
                    end(i * 2 + 1)
                    ch.leave(B // 2 - 1, 2 * per)
                middle(B - 2, 0)
                front(B - 1, 1, B // 2)
                end(B - 2)
                middle(B - 1, 1)
                end(B - 1)
                dve.wait_ge(sem(name + "_ofree"), B + 1)

            for b in range(B):
                dve.wait_ge(sem("l2_vproj"), b + 1)
                dve.tensor_tensor(vnew[:, b, :], ps[0:Q, b % 4, 0:D], bv_b, ALU.add).then_inc(sem("l2_vnew"), 1)
            single("l2a", True)
            norm("n6")
            router("l2r", FFN2)
            ffn(FFN2)
            norm("n7")
            single("l3a", False)
            norm("n8")
            router("l3r", FFN3)
            ffn(FFN3)


def kernel(**inputs):
    import numpy as _np
    import concourse.bacc as _bacc
    from concourse import mybir as _mybir
    from concourse.bass_utils import run_bass_kernel_spmd as _run

    a = {k: _np.asarray(v) for k, v in inputs.items()}

    def halves(t):
        c, w, n = t.shape
        return t.reshape(c, w // 128, 128, n).transpose(0, 2, 1, 3).reshape(c, 128, (w // 128) * n)

    def gated(gu, dn, experts):
        e, f2, w = gu.shape
        per, f = 128 // experts, f2 // 2
        g = gu.reshape(e, 2, f // per, per, w).transpose(2, 4, 1, 0, 3).reshape(f // per, w, 2 * 128)
        n = dn.reshape(e, w, f // per, per).transpose(2, 0, 3, 1).reshape(f // per, 128, w)
        return halves(g), n

    gu0, dn0 = gated(a["L0_ffn_gate_up_weights"], a["L0_ffn_down_weights"], FFN0.E)
    sgu, sdn = a["L0_ffn_shared_gate_up"], a["L0_ffn_shared_down"]
    fs = sdn.shape[1]
    fill = FFN0.shared * 128 - fs
    sgu = _np.pad(sgu.reshape(2, fs, D), ((0, 0), (0, fill), (0, 0))).reshape(1, 2 * (fs + fill), D)
    sdn = _np.pad(sdn, ((0, 0), (0, fill))).reshape(1, D, fs + fill)
    gus, dns = gated(sgu, sdn, 1)
    gu2, dn2 = gated(a["L2_ffn_gate_up_proj"], a["L2_ffn_down_proj"], FFN2.E)
    e1 = FFN1.E
    gup = a["L1_ffn_gate_up_proj"].reshape(e1, D, 2, FFN1.C, FFN1.rep).transpose(3, 1, 2, 0, 4).reshape(FFN1.C, D, 256)
    dnp = a["L1_ffn_down_proj"].reshape(e1, FFN1.C, FFN1.rep, D).transpose(1, 0, 2, 3).reshape(FFN1.C, 128, D)
    u3 = a["L3_ffn_U"].reshape(32, D, FFN3.C, FFN3.rep).transpose(2, 1, 0, 3).reshape(FFN3.C, D, 128)
    v3 = a["L3_ffn_V"].reshape(32, FFN3.C, FFN3.rep, D).transpose(1, 0, 2, 3).reshape(FFN3.C, 128, D)
    ctx = a["ctx_2048"]
    arrays = {
        "x": a["x"], "ctx": ctx, "ctxT": ctx.transpose(0, 2, 1), "mask": a["mask_BxSxS2_ff0"],
        "bkmask": a["mask_BxS2_bk0"],
        "decay": a["L0_xattn_decay"].reshape(1, 1), "winT": a["L0_xattn_W_in"].T, "woutT": a["L0_xattn_W_out"].T,
        "b_in": a["L0_xattn_b_in"].reshape(DM, 128).T, "b_out": a["L0_xattn_b_out"], "gamma": a["L0_xattn_gamma"], "beta": a["L0_xattn_beta"],
        "gate0T": a["L0_ffn_gate_weight"].T, "gate1T": a["L1_ffn_gate_weight"].T,
        "gate2T": a["L2_ffn_gate_weight"].T, "gate3T": a["L3_ffn_Wr"].T,
        "l0_gu": _np.concatenate([gus, gu0]), "l0_dn": _np.concatenate([dns, dn0]),
        "l1_gu": halves(gup), "l1_dn": dnp, "l2_gu": gu2, "l2_dn": dn2, "l3_gu": halves(u3), "l3_dn": v3,
        "gupA": a["L1_ffn_gup_lora_A"].reshape(128, D),
        "gupB": a["L1_ffn_gup_lora_B"].transpose(0, 2, 1).reshape(e1, 16, 2, FFN1.C, 16).transpose(0, 1, 3, 2, 4),
        "dnA": a["L1_ffn_down_lora_A"].reshape(e1, 16, FFN1.C, 16),
        "dnB": a["L1_ffn_down_lora_B"].transpose(0, 2, 1).reshape(128, D),
        "glA": a["L1_ffn_gate_lora_A"], "glB": a["L1_ffn_gate_lora_B"].T,
        "sim": a["L2_ffn_similarity"],
        "attr": _np.repeat(a["L3_ffn_attr"], FFN3.rep, axis=0), "Wa": a["L3_ffn_Wa"].reshape(32),
        "wqkvT": _np.stack([a["L2_xattn_Wq"].T, a["L2_xattn_Wk"].T, a["L2_xattn_Wv"].T]),
        "bqk": _np.stack([a["L2_xattn_bq"], a["L2_xattn_bk"]]).reshape(2, DM, 128).transpose(2, 0, 1), "bv": a["L2_xattn_bv"],
        "ident": _np.eye(128, dtype=_np.float32), "flip": _np.eye(128, dtype=_np.float32)[::-1],
        "iota": _np.arange(32, dtype=_np.float32),
    }
    nc = _bacc.Bacc("TRN2", target_bir_lowering=False, num_devices=1)
    maps, d = {}, {}
    for name, v in arrays.items():
        v = _np.ascontiguousarray(v)
        maps["in_" + name] = v
        d[name] = nc.dram_tensor("in_" + name, v.shape, _mybir.dt.from_np(v.dtype), kind="ExternalInput").ap()
    out = nc.dram_tensor("out_x", (B, Q, D), F32, kind="ExternalOutput").ap()
    build(nc, d, out)
    r = _run(nc, [maps], core_ids=[0])
    return r.results[0]["out_x"]
```

```python
from contextlib import ExitStack

import numpy as np

import concourse.bass as bass
from concourse import mybir

F32 = mybir.dt.float32
F32R = mybir.dt.float32r
BF16 = mybir.dt.bfloat16
U32 = mybir.dt.uint32
U8 = mybir.dt.uint8
ACT = mybir.ActivationFunctionType
ALU = mybir.AluOpType
AX = mybir.AxisListType

B, Q, D, T = 8, 100, 256, 1444
TOK = B * Q
DM = D // 128
HT = TOK // 2
PAST = T - Q
HEADS, HD = 16, 16
SETS, GRP = 4, 4
VW = HD + 1
LN_EPS = 1e-5
FAR = -1.0e30
FULL = PAST // 128
NCH = 12
CA = (T - FULL * 128) // 2
CB = (PAST - FULL * 128, Q)
UNITS = DM * B
RING = 11
EARLY = 11
CUTS = (0, 6, 12, 12)
LAG = 3
AW = T // 3 + 1
A0 = (0, T // 3, T - AW)


class Ffn:

    chunks_before = 0

    def __init__(self, name, norm, experts, top, chunks, shared=0, gated=True):
        self.name, self.E, self.K, self.C, self.shared, self.gated = name, experts, top, chunks, shared, gated
        self.rep = 128 // experts
        self.norm = norm
        self.index = int(name[1])
        self.base = Ffn.chunks_before
        Ffn.chunks_before += chunks
        self.cols = DM * (2 if gated else 1) * 128
        self.head = 3 - chunks % 2

    def loop(self, eng, step):
        for c in range(self.head):
            step(c, c % 2)
        pairs = (self.C - 1 - self.head) // 2
        if pairs:
            with eng.Fori(0, pairs) as i:
                step(i * 2 + self.head, self.head % 2)
                step(i * 2 + (self.head + 1), 1 - self.head % 2)
        step(self.C - 1, (self.C - 1) % 2)


FFN0 = Ffn("l0", "n2", 16, 4, 25, shared=3)
FFN1 = Ffn("l1", "n4", 8, 2, 8)
FFN2 = Ffn("l2", "n6", 32, 8, 24)
FFN3 = Ffn("l3", "n8", 32, 2, 4, gated=False)


NORMS = ("n0", "n1", "n2", "n3", "n4", "n5", "n6", "n7", "n8")
TURNED = ("n2", "n4", "n5", "n6", "n7", "n8")
ROUTERS = ("l0", "l1r", "l2r", "l3r")


def xn_count(name, b=B):
    return NORMS.index(name) * B + b


def tr_count(name, b):
    return TURNED.index(name) * B + b


def xnT_count(name):
    return TURNED.index(name) * 4 + 4


def w_count(r):
    return ROUTERS.index(r) * 2 + 2


def q_turn(b, n):
    return b * 7 + n


def o_turn(b):
    return b * 7 + 16


def m_turn(b, s):
    return b * 7 + (4 + s if s < SETS - 1 else 10)


class Chain:

    def __init__(self, eng, sem):
        self.eng, self.sem, self.n, self.base = eng, sem, 0, 0

    def add(self, ins):
        ins.then_inc(self.sem, 1)
        self.n += 1

    def wait(self):
        self.eng.wait_ge(self.sem, self.base + self.n)

    def link(self, ins):
        self.add(ins)
        self.wait()

    def enter(self, i, first, per):
        self.base = (i - first) * per
        self.n0 = self.n

    def leave(self, turns, per):
        assert self.n - self.n0 == per, (self.n - self.n0, per)
        self.n = self.n0 + turns * per
        self.base = 0


def build(nc, d, out):
    ctx = ExitStack()
    with ctx:
        def sb(name, shape, dt=F32):
            return ctx.enter_context(nc.sbuf_tensor("sb_" + name, shape, dt))

        sems = {}

        def sem(name):
            if name not in sems:
                sems[name] = ctx.enter_context(nc.semaphore(name))
            return sems[name]

        x = sb("x", [Q, B, D])
        xn = sb("xn", [Q, B, D])
        xnT = sb("xnT", [128, DM, TOK])
        with nc.sbuf_tensor("sb_l0w", [128, 2 * DM * D], F32) as l0w:
            pass
        xhi = sb("xhi", [128, DM, TOK], F32R)
        with nc.sbuf_tensor("sb_xlo", [128, DM, TOK], F32R) as xlo:
            pass
        yT = sb("yT", [128, DM, TOK])
        ident = sb("ident", [128, 128])
        identb = sb("identb", [Q, Q], BF16)
        farb = sb("farb", [Q, Q], BF16)
        iota = sb("iota", [Q, 32])
        mhalf = sb("mhalf", [Q, B])
        Wb = sb("Wb", [128, TOK])
        stat = sb("stat", [Q, B, 6])
        mv = sb("mv", [Q, B, 2])
        rstd = sb("rstd", [Q, B])
        WC = FFN0.cols + D
        wraw = [sb(f"wraw{i}", [128, WC]) for i in range(2)]
        sg = [sb(f"sg{i}", [128, HT]) for i in range(2)]
        hb = [sb(f"hb{i}", [128, HT]) for i in range(2)]
        gate = {0: sb("gate0", [128, DM, 16]), 1: sb("gate1", [128, DM, 8]),
                2: sb("gate2", [128, DM, 32]), 3: sb("gate3", [128, DM, 32])}
        awcol = sb("awcol", [128, 1])
        awmat = sb("awmat", [128, 128])
        simb = sb("simb", [128, 128])
        with ExitStack() as halves:
            def half(name, n):
                return halves.enter_context(nc.sbuf_tensor("sb_" + name, [128, n], F32R))

            whi = [half(f"whi{i}", WC) for i in range(2)]
            wlo = [half(f"wlo{i}", WC) for i in range(2)]
            hhi = [half(f"hhi{i}", HT) for i in range(2)]
            hlo = [half(f"hlo{i}", HT) for i in range(2)]
        tail = sb("tail", [128, 6208])
        arena = sb("arena", [128, 32704])
        parts = nc.dram_tensor("parts", (3, B, D, T), BF16).ap()
        merged_w = nc.dram_tensor("merged_w", (FFN1.C, 128, WC), F32).ap()

        def ar(at, n, p=128):
            return arena[0:p, at:at + n]

        def tl(at, n, p=128):
            return tail[0:p, at:at + n]

        ps = ctx.enter_context(nc.psum_tensor("ps", [128, 8, 512], F32))

        ct = [ar(T * i, T) for i in range(RING)]
        part = [ar(22100 + 2166 * i, 2166).bitcast(BF16).rearrange("p (t k) -> p t k", t=3) for i in range(3)]
        rest = [ar(28600 + T * i, T) for i in range(2)]
        crow = tl(4096, T)
        orow, krow = ct[RING - 2:]
        prod = xnT[:, :, :].rearrange("p m t -> p (m t)")[:, 0:T]
        csum = ar(31500, 2)
        dk = ar(31510, 2)
        wkv = ar(31520, DM * B).rearrange("p (m b) -> p m b", m=DM)
        s1 = ar(31540, DM * B).rearrange("p (m b) -> p m b", m=DM)
        bin_c = ar(31560, DM)
        bout_b = ar(31600, D, Q)
        gam_b = ar(31860, D, Q)
        bet_b = ar(32120, D, Q)
        s1r = yT[:, :, :].rearrange("p m (b q) -> p m b q", b=B)
        winT = l0w[:, 0:DM * D].rearrange("p (m e) -> p m e", m=DM)
        woutT = l0w[:, DM * D:2 * DM * D].rearrange("p (m e) -> p m e", m=DM)
        agup = ar(15900, D)
        bblk = ar(16160, 2048).rearrange("p (c n) -> p c n", c=FFN1.C)
        adn = ar(18210, 1024).rearrange("p (c n) -> p c n", c=FFN1.C)
        bdn = ar(19240, D)
        glA = ar(19500, D, 16)
        glB = ar(19760, 8, 16)
        attr_r = ar(19840, 32)
        wa_b = ar(19880, 32)
        aw_t = ar(19920, 32)
        mgu = tl(0, FFN1.C * FFN1.cols).rearrange("p (c n) -> p c n", c=FFN1.C)
        mdn = ar(20000, FFN1.C * D).rearrange("p (c n) -> p c n", c=FFN1.C)
        rl = ar(28000, B * 32, Q)
        rp = ar(28260, B * 32, Q)
        rmx = ar(28520, B, Q)
        rsum = ar(28530, B, Q)
        v8 = ar(28540, B * 8, Q).rearrange("p (b k) -> p b k", b=B)
        i8 = ar(28610, B * 8, Q).bitcast(U32).rearrange("p (b k) -> p b k", b=B)
        if8 = ar(28680, B * 8, Q).rearrange("p (b k) -> p b k", b=B)
        rw = ar(28750, B * 32, Q)
        rsel = ar(29010, B * 32, Q)
        wrep = ar(29270, B * 128, Q).rearrange("p (b n) -> p b n", b=B)
        oh = ar(0, B * 8 * 32, Q)
        cand = ar(2100, B * 16 * 32, Q)
        pick = ar(6300, B * 16, Q).rearrange("p (b j i) -> p b j i", b=B, j=4)
        first = ar(6440, B * 16, Q).rearrange("p (b j i) -> p b j i", b=B, j=4)
        left = ar(6580, B * 4, Q).rearrange("p (b j) -> p b j", b=B)
        best = ar(6620, B * 4, Q).rearrange("p (b j) -> p b j", b=B)
        keep = ar(6660, B * 4, Q).rearrange("p (b j) -> p b j", b=B)
        moved = ar(6700, B * 4, Q).rearrange("p (b j) -> p b j", b=B)
        w8 = ar(6740, B * 8, Q).rearrange("p (b k) -> p b k", b=B)
        secT = ar(6810, TOK)
        scand = ar(7700, B * 128, Q)
        kstk = [ar(11552 * i, 11552).bitcast(BF16).rearrange("p (h k) -> p h k", h=HEADS) for i in range(2)]
        vnat = ar(23104, 3072).rearrange("p (c d) -> p c d", c=NCH)
        vaug = [ar(26176 + 3264 * i, 3264).rearrange("p (c h v) -> p c h v", c=NCH, h=HEADS) for i in range(2)]
        pr = [tl(1200 * i, 1200).rearrange("p (c q) -> p c q", c=NCH) for i in range(2)]
        qs = [tl(2400 + 800 * i, 800).bitcast(BF16).rearrange("p (h q) -> p h q", h=HEADS) for i in range(2)]
        xs = [tl(4000 + 768 * i, 768, Q).bitcast(BF16).rearrange("p (h t r) -> p h t r", h=HEADS, t=6) for i in range(2)]
        xr = tl(5536, D, Q).rearrange("p (h r) -> p h r", h=HEADS)
        nm = [tl(5792 + 8 * i, 8, Q).bitcast(BF16) for i in range(2)]
        ot = tl(5808, SETS * Q)
        mx = sb("mx", [Q, GRP, 3])
        den = sb("den", [Q, HEADS])
        att = sb("att", [Q, HEADS, HD])
        ctT = [ar(2888 * i, 2888).rearrange("p (m k) -> p m k", m=DM) for i in range(2)]
        vn2 = [ar(5776 + 3072 * i, 3072).rearrange("p (c d) -> p c d", c=NCH) for i in range(2)]
        bias = [ar(11920 + T * i, T, Q) for i in range(2)]
        sc = ar(14808, T, Q)
        pb = [ar(16252, T, Q), ar(27000, T, Q)]
        mk8 = [ar(17700 + 361 * i, 361, Q).bitcast(U8) for i in range(2)]
        ptt = ar(18500, 1200).rearrange("p (c q) -> p c q", c=NCH)
        qst = [ar(20900 + 200 * i, 200).rearrange("p (m q) -> p m q", m=DM) for i in range(2)]
        knT = ar(21300, DM * TOK).rearrange("p (m t) -> p m t", m=DM)
        vnew = ar(22900, B * D, Q).rearrange("p (b d) -> p b d", b=B)
        wqkv = ar(24950, 3 * 512).rearrange("p (w m e) -> p w m e", w=3, m=DM)
        bqk = ar(26500, 4).rearrange("p (w m) -> p w m", w=2)
        bv_b = ar(26510, D, Q)
        nmx = ar(26770, 1, Q)
        ssum = ar(26772, 1, Q)
        rsm = ar(26774, 1, Q)
        anym = [ar(26776 + 2 * i, 1, Q) for i in range(2)]

        block = ctx.enter_context(nc.Block())

        def v_load(eng, b):
            eng.dma_start(vnat[:, 0:FULL, :], d["ctx"][bass.ds(b, 1), 0:FULL * 128, :]
                          .rearrange("a (c p) d -> p (a c) d", p=128)).then_inc(sem("in_vnat"), 16)
            eng.dma_start(vnat[0:CA, FULL:NCH, :], d["ctx"][bass.ds(b, 1), FULL * 128:T, :]
                          .rearrange("a (c p) d -> p (a c) d", p=CA)).then_inc(sem("in_vnat"), 16)

        def stack_loads(eng, b, k, s):
            h = slice(GRP * s, GRP * s + GRP)
            at = 0
            for n in (3, 2, 1):
                for t in range(n):
                    src = parts[t, bass.ds(b, 1), GRP * HD * s:GRP * HD * (s + 1), :].rearrange("a (h r) k -> (a r) h k", r=HD)
                    eng.dma_start(kstk[k][at:at + HD, h, :], src).then_inc(sem(f"in_stk{k}{s}"), 16)
                    at += HD

        @block.sync
        def _(sp):
            def load(name, dst, src, **kw):
                sp.dma_start(dst, src, **kw).then_inc(sem(name), 16)

            load("in_x", x[:, :, :], d["x"].rearrange("b q d -> q b d"))
            load("in_const", ident[:, :], d["ident"])
            load("in_const", iota[:, :], d["iota"].partition_broadcast(Q))
            load("in_decay", dk[:, 0:1], d["decay"].partition_broadcast(128))
            def ct_load(u):
                sp.dma_start(ct[u % RING], d["ctxT"][u // DM, (u % DM) * 128:(u % DM) * 128 + 128, :]).then_inc(sem(f"in_ct{u % RING}"), 16)

            for u in range(RING):
                if u == RING - 2:
                    sp.wait_ge(sem("crow_ready"), 1)
                ct_load(u)
            load("in_l0w", winT, d["winT"].rearrange("(m p) e -> p m e", p=128))
            load("in_l0w", woutT, d["woutT"].rearrange("(m p) e -> p m e", p=128))
            load("in_l0w", bin_c, d["b_in"])
            load("in_l0w", bout_b, d["b_out"].partition_broadcast(Q))
            load("in_l0w", gam_b, d["gamma"].partition_broadcast(Q))
            load("in_l0w", bet_b, d["beta"].partition_broadcast(Q))
            for n in range(4):
                load("in_gate", gate[n][:, :, :], d[f"gate{n}T"].rearrange("(m p) e -> p m e", p=128))
            load("in_lora", mgu[:, :, :], d["l1_gu"].rearrange("c p n -> p c n"))
            load("in_lora", mdn[:, :, :], d["l1_dn"].rearrange("c p n -> p c n"))
            load("in_lora", agup, d["gupA"])
            load("in_lora", bdn, d["dnB"])
            load("in_lora", glA, d["glA"])
            load("in_lora", glB, d["glB"])
            load("in_lora", attr_r, d["attr"])
            load("in_lora", wa_b, d["Wa"].partition_broadcast(128))
            sp.wait_ge(sem("zeroed"), 4)
            for e in range(8):
                s = slice(16 * e, 16 * e + 16)
                load("in_blk", bblk[s, :, :].rearrange("p c (g n) -> p c g n", g=2)[:, :, :, s],
                     d["gupB"][e].rearrange("r c g f -> r c g f"))
                load("in_blk", adn[s, :, s], d["dnA"][e])
            for j in range(4):
                load("in_blk", simb[32 * j:32 * j + 32, 32 * j:32 * j + 32], d["sim"])
            for u in range(UNITS):
                if u + RING < UNITS:
                    sp.wait_ge(sem("rest_done"), u + 1)
                    ct_load(u + RING)
                if u == 8:
                    sp.wait_ge(sem("merged"), 2 * FFN1.C)
                    sp.dma_start(merged_w[:, :, 0:FFN1.cols].rearrange("c p n -> p c n"), mgu).then_inc(sem("merged_out"), 16)
                    sp.dma_start(merged_w[:, :, FFN1.cols:WC].rearrange("c p n -> p c n"), mdn).then_inc(sem("merged_out"), 16)
                sp.wait_ge(sem("kl_done"), u + 1)
                sp.dma_start(parts[:, u // DM, (u % DM) * 128:(u % DM) * 128 + 128, :].rearrange("t p k -> p t k"), part[u % 3])\
                    .then_inc(sem(f"parts_out{u % 3}"), 16)

            def ffn_loads(f, w):
                def step(c, k):
                    if not isinstance(c, int) or c >= 2:
                        sp.wait_ge(sem("ffn_wl"), 2 * f.base + 2 * c - 2)
                    sp.dma_start(wraw[k][:, 0:f.cols + D], w[bass.ds(c, 1), :, :].rearrange("a p n -> p (a n)"))\
                        .then_inc(sem(f"{f.name}_w{k}"), 16)

                f.loop(sp, step)

            ffn_loads(FFN0, d["l0_w"])

            sp.wait_ge(sem("l1_vfree"), 1)
            v_load(sp, 1)
            with sp.Fori(0, (B - 2) // 2) as i:
                for k in range(2):
                    b = i * 2 + (k + 2)
                    sp.wait_ge(sem("l1_vfree"), b)
                    sp.sem_inc(sem("sp_turns"), 1)
                    v_load(sp, b)
                    for s in range(SETS):
                        sp.wait_ge(sem("l1_sc"), b * (3 * HEADS) + 3 * GRP * (s + 1))
                        sp.sem_inc(sem("sp_turns"), 1)
                        stack_loads(sp, b, k, s)

            sp.wait_ge(sem("merged_out"), 32)
            ffn_loads(FFN1, merged_w)

            def key_loads(name, b, k, masked):
                sp.wait_ge(sem(name + "_sc"), b + 1)
                sp.sem_inc(sem("sp_turns"), 1)
                sp.dma_start(ctT[k][:, :, :], d["ctxT"][bass.ds(b, 1), :, :].rearrange("a (m p) k -> p (a m) k", p=128))\
                    .then_inc(sem(f"{name}_ink{k}"), 16)
                sp.wait_ge(sem(name + "_scfree"), b + 1)
                sp.sem_inc(sem("sp_turns"), 1)
                if masked:
                    sp.dma_start(bias[k], d["mask"][bass.ds(b, 1), :, :].rearrange("a q k -> q (a k)"))\
                        .then_inc(sem(f"{name}_inm{k}"), 16)
                else:
                    sp.dma_start(mk8[k], d["bkmask"][bass.ds(b, 1), :].rearrange("a k -> (a k)").partition_broadcast(Q))\
                        .then_inc(sem(f"{name}_inm{k}"), 16)

            def value_loads(name, b, k):
                sp.wait_ge(sem(name + "_o"), b + 1)
                sp.sem_inc(sem("sp_turns"), 1)
                sp.dma_start(vn2[k][:, 0:FULL, :], d["ctx"][bass.ds(b, 1), 0:FULL * 128, :]
                             .rearrange("a (c p) d -> p (a c) d", p=128)).then_inc(sem(f"{name}_inv{k}"), 16)
                at = FULL * 128
                for j, n in enumerate(CB):
                    sp.dma_start(vn2[k][0:n, FULL + j, :], d["ctx"][bass.ds(b, 1), at:at + n, :]
                                 .rearrange("a p d -> p (a d)")).then_inc(sem(f"{name}_inv{k}"), 16)
                    at += n

            def single_loads(name, masked):
                key_loads(name, 0, 0, masked)
                with sp.Fori(0, B // 2 - 1) as i:
                    key_loads(name, i * 2 + 1, 1, masked)
                    value_loads(name, i * 2, 0)
                    key_loads(name, i * 2 + 2, 0, masked)
                    value_loads(name, i * 2 + 1, 1)
                key_loads(name, B - 1, 1, masked)
                value_loads(name, B - 2, 0)
                value_loads(name, B - 1, 1)

            sp.wait_ge(sem("w_ready"), w_count("l1r"))
            load("in_qkv", wqkv[:, :, :, :], d["wqkvT"].rearrange("w (m p) e -> p w m e", p=128))
            load("in_qkv", bqk[:, :, :], d["bqk"])
            load("in_qkv", bv_b, d["bv"].partition_broadcast(Q))
            single_loads("l2a", True)
            ffn_loads(FFN2, d["l2_w"])
            sp.wait_ge(sem("w_ready"), w_count("l2r"))
            single_loads("l3a", False)
            ffn_loads(FFN3, d["l3_w"])
            for j in range(4):
                sp.wait_ge(sem("l3_x"), j + 1)
                sp.dma_start(out[2 * j:2 * j + 2, :, :].rearrange("b q d -> q b d"), x[:, 2 * j:2 * j + 2, :])\
                    .then_inc(sem("out_done"), 16)
            sp.wait_ge(sem("out_done"), 64)

        @block.gpsimd
        def _(pool):
            ch = Chain(pool, sem("pool_own"))

            def wait_register(name, value):
                pool.wait_ge(sem(name), value)
                pool.sem_inc(sem("pool_turns"), 1)

            pool.memset(mhalf[:, :], -0.5).then_inc(sem("mhalf_set"), 1)
            pool.memset(bblk[:, :, :], 0.0).then_inc(sem("zeroed"), 1)
            pool.memset(adn[:, :, :], 0.0).then_inc(sem("zeroed"), 1)
            pool.memset(simb[:, :], 0.0).then_inc(sem("zeroed"), 1)
            pool.memset(ot, 0.0).then_inc(sem("zeroed"), 1)
            pool.wait_ge(sem("in_const"), 32)
            ch.link(pool.tensor_copy(identb[:, :], ident[0:Q, 0:Q]))
            ch.link(pool.memset(farb[:, :], 0.0))
            pool.affine_select(out=farb[:, :], in_=farb[:, :], pattern=[[-1, Q]], compare_op=ALU.is_ge, fill=FAR,
                               base=0, channel_multiplier=1).then_inc(sem("far_ready"), 1)

            def norm(name):
                pool.wait_ge(sem("stat"), NORMS.index(name) + 1)
                ch.link(pool.tensor_scalar(rstd[:, :], mv[:, :, 1], LN_EPS, None, ALU.add))
                pool.tensor_tensor(rstd[:, :], rstd[:, :], mhalf[:, :], ALU.pow).then_inc(sem("rstd"), 1)
                pool.wait_ge(sem("rstd"), NORMS.index(name) + 1)

            pool.wait_ge(sem("mhalf_set"), 1)

            def low_halves(f, n):
                for m in range(DM):
                    pool.wait_ge(sem("xhi"), DM * n + m + 1)
                    pool.tensor_tensor(xlo[:, m, :], xnT[:, m, :], xhi[:, m, :], ALU.subtract).then_inc(sem("xlo"), 1)

                def step(c, k):
                    for part, (a, z) in enumerate(((0, f.cols), (f.cols, f.cols + D))):
                        wait_register("ffn_wh", 2 * f.base + 2 * c + (part + 1))
                        pool.tensor_tensor(wlo[k][:, a:z], wraw[k][:, a:z], whi[k][:, a:z], ALU.subtract)\
                            .then_inc(sem("ffn_wl"), 1)

                f.loop(pool, step)

            def prepare_queries(b, k, step):
                src = xn[:, bass.ds(b, 1), :].rearrange("q a (h r) -> q (a h) r", h=HEADS)
                if step == 0:
                    if not isinstance(b, int) or b >= 2:
                        wait_register("l1_qtr", b * 2 - 2)
                    ins = pool.tensor_copy(xs[k][:, :, 0:3, :], src.unsqueeze(2).broadcast_to([Q, HEADS, 3, HD]))
                elif step == 1:
                    ins = pool.tensor_tensor(xr, src, xs[k][:, :, 0, :], ALU.subtract)
                elif step == 2:
                    ins = pool.tensor_copy(xs[k][:, :, 3:5, :], xr.unsqueeze(2).broadcast_to([Q, HEADS, 2, HD]))
                else:
                    ins = pool.tensor_tensor(xs[k][:, :, 5, :], xr, xs[k][:, :, 3, :], ALU.subtract)
                ins.then_inc(sem("l1_xs"), 1)
                wait_register("l1_xs", b * 4 + (step + 1))

            def copy_values(b, k, c):
                if c == 0:
                    wait_register("in_vnat", b * 32 + 32)
                    if not isinstance(b, int) or b:
                        wait_register("l1_pv", (b - 1) * HEADS + 2)
                n = 128 if c < FULL else CA
                pool.tensor_copy(vaug[k][0:n, c, :, 0:HD], vnat[0:n, c, :].rearrange("p (h v) -> p h v", h=HEADS))\
                    .then_inc(sem("l1_vaug"), 1)
                if c == NCH - 1:
                    pool.wait_ge(sem("l1_vaug"), b * NCH + NCH)
                    pool.sem_inc(sem("l1_vfree"), 1)

            def masks(b, nk, k=None):
                for h in range(HEADS):
                    wait_register("l1_exp", (b * HEADS + h) * 4 + 8)
                    tail = pr[h % 2][0:CA, FULL:NCH, :]
                    pool.affine_select(out=tail, in_=tail, pattern=[[-CA, 2], [1, Q]], compare_op=ALU.is_ge, fill=0.0,
                                       base=PAST - FULL * 128, channel_multiplier=-1).then_inc(sem("l1_masked"), 1)
                    if nk is not None and h < NCH:
                        copy_values(b + 1, nk, h)
                    if k is not None and h >= NCH:
                        prepare_queries(b + 2, k, h - NCH)

            def lowest(u):
                pool.wait_ge(sem("km_done"), u + 1)
                pool.tensor_tensor(part[u % 3][:, 2, :], rest[u % 2], part[u % 3][:, 1, :], ALU.subtract).then_inc(sem("kl_done"), 1)

            norm("n0")
            for u in range(EARLY):
                lowest(u)
            norm("n1")
            for u in range(EARLY, EARLY + 2):
                lowest(u)
            norm("n2")
            for u in range(EARLY + 2, UNITS):
                lowest(u)
            low_halves(FFN0, 0)
            for k in range(2):
                pool.memset(vaug[k][:, :, :, HD], 1.0).then_inc(sem("value_ones"), 1)
                pool.wait_ge(sem("value_ones"), k + 1)
            norm("n3")
            pool.wait_ge(sem("xn"), xn_count("n3"))
            pool.wait_ge(sem("l1_xs"), 4)
            for step in range(4):
                prepare_queries(1, 1, step)
            pool.wait_ge(sem("in_vnat"), 32)
            for c in range(NCH):
                copy_values(0, 0, c)
            with pool.Fori(0, (B - 2) // 2) as i:
                b = i * 2
                masks(b, 1, 0)
                masks(b + 1, 0, 1)
            masks(B - 2, 1)
            masks(B - 1, None)
            norm("n4")
            low_halves(FFN1, 1)
            norm("n5")

            def stage_queries(name, src, b, k):
                wait_register(name + "_sc", b + 1)
                pool.tensor_copy(qst[k][:, :, :], src[:, :, bass.ds(b * Q, Q)]).then_inc(sem(name + "_q"), 1)

            pool.wait_ge(sem("l2a_qT"), 4)
            with pool.Fori(0, B // 2) as i:
                b = i * 2
                stage_queries("l2a", yT, b, 0)
                stage_queries("l2a", yT, b + 1, 1)
            norm("n6")
            low_halves(FFN2, 2)
            norm("n7")
            pool.wait_ge(sem("xnT"), xnT_count("n7"))

            with pool.Fori(0, B // 2) as i:
                b = i * 2
                stage_queries("l3a", xnT, b, 0)
                stage_queries("l3a", xnT, b + 1, 1)
            norm("n8")
            low_halves(FFN3, 3)

        @block.scalar
        def _(act):
            ch = Chain(act, sem("act_own"))
            act.wait_ge(sem("in_decay"), 16)
            act.activation(dk[:, 1:2], dk[:, 0:1], ACT.Sigmoid).then_inc(sem("decayed"), 1)
            act.sem_inc(sem("l1_exp"), 4)
            def high_parts(first, end):
                for u in range(first, end + 1):
                    if u < end:
                        act.wait_ge(sem(f"in_ct{u % RING}"), 16 * (u // RING + 1))
                        if u >= 3:
                            act.wait_ge(sem(f"parts_out{u % 3}"), 16 * (u // 3))
                        act.activation(part[u % 3][:, 0, :], ct[u % RING], ACT.Copy).then_inc(sem("kh_done"), 1)
                    if u > first:
                        act.wait_ge(sem("rest_done"), u)
                        act.activation(part[(u - 1) % 3][:, 1, :], rest[(u - 1) % 2], ACT.Copy).then_inc(sem("km_done"), 1)

            high_parts(0, EARLY + 3)

            def transposed(name, dst=xnT):
                for j in range(2):
                    for m in range(DM):
                        act.wait_ge(sem("tr"), tr_count(name, 4 * (j + 1)))
                        act.activation(dst[:, m, j * HT:(j + 1) * HT], ps[:, 2 * j + m, 0:HT], ACT.Copy)\
                            .then_inc(sem("xnT"), 1)

            def router(r, f):
                act.wait_ge(sem("r_shift"), ROUTERS.index(r) + 1)
                act.activation(rp[:, 0:B * f.E], rp[:, 0:B * f.E], ACT.Exp).then_inc(sem("r_exp"), 1)
                for j in range(2):
                    act.wait_ge(sem("r_wT"), ROUTERS.index(r) * B + 4 * (j + 1))
                    act.activation(Wb[:, j * HT:(j + 1) * HT], ps[:, 5 + j, 0:HT], ACT.Copy)\
                        .then_inc(sem("w_ready"), 1)

            def weights_high(f, c, k, part):
                a, z = ((0, f.cols), (f.cols, f.cols + D))[part]
                if part == 0:
                    act.wait_ge(sem(f"{f.name}_w{k}"), 16 * (c // 2 + 1) if isinstance(c, int) else c[1])
                c = c[0] if isinstance(c, tuple) else c
                if not isinstance(c, int) or c >= 2:
                    act.wait_ge(sem(f.name + ("_gu_done", "_down_done")[part]), 2 * c - 2)
                act.activation(whi[k][:, a:z], wraw[k][:, a:z], ACT.Copy).then_inc(sem("ffn_wh"), 1)

            def tokens_high(f):
                for m in range(DM):
                    act.wait_ge(sem("xnT"), xnT_count(f.norm))
                    act.activation(xhi[:, m, :], xnT[:, m, :], ACT.Copy).then_inc(sem("xhi"), 1)
                for part in range(2):
                    weights_high(f, 0, 0, part)

            def ffn(f):
                nm = f.name

                def high(c, hf):
                    act.wait_ge(sem(nm + "_h"), 2 * c + (hf + 1))
                    if not isinstance(c, int) or c >= 1:
                        act.wait_ge(sem(nm + "_down_done"), 2 * c + (hf - 1))
                    act.activation(hhi[hf][:, :], hb[hf][:, :], ACT.Copy).then_inc(sem("ffn_hh"), 1)

                def step(c, k, loads):
                    for hf in range(2):
                        if f.gated:
                            act.wait_ge(sem(nm + "_gu_done"), 2 * c + (hf + 1))
                            act.activation(sg[hf][:, :], ps[:, 2 * hf, 0:HT], ACT.Silu).then_inc(sem("ffn_silu"), 1)
                        if hf:
                            high(c, 0)
                        elif not isinstance(c, int) or c:
                            high(c - 1, 1)
                        if loads is not None:
                            weights_high(f, (c + 1, loads), 1 - k, hf)

                for c in range(f.head):
                    step(c, c % 2, 16 * ((c + 1) // 2 + 1))
                pairs = (f.C - 1 - f.head) // 2
                if pairs:
                    with act.Fori(0, pairs) as i:
                        c = i * 2 + f.head
                        step(c, f.head % 2, i * 16 + 16 * ((f.head + 1) // 2 + 1))
                        step(c + 1, 1 - f.head % 2, i * 16 + 16 * ((f.head + 2) // 2 + 1))
                step(f.C - 1, (f.C - 1) % 2, None)
                high(f.C - 1, 1)
                for m in range(DM):
                    act.wait_ge(sem(f.name + "_down_done"), 2 * f.C)
                    act.activation(yT[:, m, 0:HT], ps[:, 4 + 2 * m, 0:HT], ACT.Copy).then_inc(sem("ffn_yT"), 1)

            transposed("n2")
            high_parts(EARLY + 3, UNITS)
            act.wait_ge(sem("aw_dot"), 1)
            act.activation(awcol[:, :], aw_t[:, 0:1], ACT.Sigmoid).then_inc(sem("aw_sig"), 1)
            act.wait_ge(sem("merged_out"), 32)
            tokens_high(FFN0)
            router("l0", FFN0)
            act.wait_ge(sem("w_ready"), w_count("l0"))
            for n in range(3):
                act.wait_ge(sem(f"parts_out{n}"), 16 * ((DM * B + 2 - n) // 3))
            v_load(act, 0)
            act.dma_start(arena[96:97, 0:23104], d["ones"]).then_inc(sem("in_ones"), 16)
            for k in range(2):
                for s in range(SETS):
                    stack_loads(act, k, k, s)
            ffn(FFN0)

            def query_copy(b, k, n):
                act.wait_ge(sem("l1_qtr"), b * 2 + (n + 1))
                act.activation(qs[k][0:96, 8 * n:8 * n + 8, :],
                               ps[0:96, 7, :].bitcast(BF16)[:, 0:8 * Q].rearrange("p (h q) -> p h q", h=8), ACT.Copy)\
                    .then_inc(sem("bank7"), 1)

            def max_copy(b, k, s):
                act.wait_ge(sem("l1_mtr"), b * SETS + (s + 1))
                act.activation(qs[k][96:97, GRP * s:GRP * s + GRP, :],
                               ps[96:97, 7, 0:GRP * Q].rearrange("p (h q) -> p h q", h=GRP), ACT.Copy).then_inc(sem("bank7"), 1)

            def sums_copies(b):
                act.wait_ge(sem("l1_pv"), b * HEADS + (HEADS + 2))
                for g in range(GRP):
                    act.activation(ot[32 * g:32 * g + VW, :], ps[32 * g:32 * g + VW, 6, 0:SETS * Q], ACT.Copy).then_inc(sem("l1_ot"), 1)

            def exps(b, h):
                n = b * HEADS + h
                act.wait_ge(sem("l1_pv"), n + 1)
                for j in range(3):
                    act.wait_ge(sem("l1_sc"), n * 3 + (j + 1 + 6 * HEADS))
                    for c0, c1, rows in (((0, 4, 128),), ((4, 8, 128),), ((8, 10, 128), (10, 12, CA)))[j]:
                        act.activation(pr[h % 2][0:rows, c0:c1, :],
                                       ps[0:rows, 3 + j, (c0 - 4 * j) * Q:(c1 - 4 * j) * Q].rearrange("p (c q) -> p c q", q=Q),
                                       ACT.Exp, scale=HD ** -0.5).then_inc(sem("l1_exp"), 1)

            def batch(b, k, ahead=True, before=True):
                for h in range(HEADS):
                    exps(b, h)
                    if h == 0 and before:
                        sums_copies(b - 1)
                    if h < 2 and ahead:
                        query_copy(b + 1, 1 - k, h)
                    if h == LAG:
                        max_copy(b, k, SETS - 1)
                    elif h % GRP == LAG and ahead:
                        max_copy(b + 1, 1 - k, h // GRP - 1)

            for n in range(2):
                query_copy(0, 0, n)
            for s in range(SETS - 1):
                max_copy(0, 0, s)
            batch(0, 0, before=False)
            batch(1, 1)
            with act.Fori(1, (B - 2) // 2) as i:
                batch(i * 2, 0)
                batch(i * 2 + 1, 1)
            batch(B - 2, 0)
            batch(B - 1, 1, ahead=False)
            sums_copies(B - 1)

            transposed("n4")
            tokens_high(FFN1)
            router("l1r", FFN1)
            ffn(FFN1)
            transposed("n5")

            def single(name):
                act.sem_inc(sem(name + "_pt"), 3)

                def body(b, k):
                    act.wait_ge(sem(name + "_max"), b + 1)
                    act.activation(pb[k], sc, ACT.Exp, bias=nmx, accum_out=ssum).then_inc(sem(name + "_exp"), 1)
                    for j in range(3):
                        act.wait_ge(sem(name + "_ptr"), b * 3 + (j + 1))
                        if j < 2:
                            act.activation(ptt[:, 4 * j:4 * j + 4, :],
                                           ps[:, 3 + j, 0:4 * Q].rearrange("p (c q) -> p c q", c=4), ACT.Copy)\
                                .then_inc(sem(name + "_pt"), 1)
                        else:
                            ch.add(act.activation(ptt[:, 8:10, :],
                                                  ps[:, 5, 0:2 * Q].rearrange("p (c q) -> p c q", c=2), ACT.Copy))
                            ch.add(act.activation(ptt[0:CB[0], 10, :], ps[0:CB[0], 5, 2 * Q:3 * Q], ACT.Copy))
                            act.activation(ptt[0:CB[1], 11, :], ps[0:CB[1], 5, 3 * Q:4 * Q], ACT.Copy)\
                                .then_inc(sem(name + "_pt"), 1)

                with act.Fori(0, B // 2) as i:
                    b = i * 2
                    ch.enter(i, 0, 4)
                    body(b, 0)
                    body(b + 1, 1)
                    ch.leave(B // 2, 4)

            single("l2a")
            transposed("n6")
            tokens_high(FFN2)
            router("l2r", FFN2)
            ffn(FFN2)
            transposed("n7")
            single("l3a")
            transposed("n8")
            tokens_high(FFN3)
            router("l3r", FFN3)
            ffn(FFN3)

        @block.tensor
        def _(pe):
            def mm(o, l, r, start, stop, **kw):
                return pe.matmul(o, l, r, start=start, stop=stop, **kw)

            pe.wait_ge(sem("zeroed"), 4)
            pe.wait_ge(sem("in_const"), 32)
            pe.wait_ge(sem("in_lora"), 8 * 16)
            pe.wait_ge(sem("in_blk"), 20 * 16)
            for c in range(FFN1.C):
                if c >= 2:
                    pe.wait_ge(sem("merged"), 2 * (c - 1))
                k = 2 + 2 * (c % 2)
                for m in range(DM):
                    last = mm(ps[:, k, m * 256:m * 256 + 256], agup[:, m * 128:m * 128 + 128], bblk[:, c, :], True, True)
                last = mm(ps[:, k + 1, 0:D], adn[:, c, :], bdn, True, True)
                last.then_inc(sem("lora"), 1)
            for m in range(DM):
                last = mm(ps[:, 6, m * 8:m * 8 + 8], glA[:, m * 128:m * 128 + 128], glB, True, True)
            last.then_inc(sem("lora_gate"), 1)
            pe.wait_ge(sem("wkv_ready"), 1)
            pe.wait_ge(sem("in_l0w"), 96)
            for e in range(DM):
                for m in range(DM):
                    last = mm(ps[:, 7, e * B:(e + 1) * B], winT[:, m, e * 128:e * 128 + 128], wkv[:, m, :], m == 0, m == DM - 1)
            last.then_inc(sem("s1_done"), 1)
            pe.wait_ge(sem("s1_ready"), 2)
            for b in range(B):
                for m in range(DM):
                    last = mm(ps[0:Q, b // 2, (b % 2) * D:(b % 2) * D + D], s1r[:, m, b, :], woutT[:, m, :], m == 0, m == DM - 1)
            last.then_inc(sem("summed"), 1)

            def transposes(name):
                for b in range(B):
                    pe.wait_ge(sem("xn"), xn_count(name, b + 1))
                    for m in range(DM):
                        last = pe.transpose(ps[:, 2 * (b // 4) + m, (b % 4) * Q:(b % 4) * Q + Q],
                                            xn[:, b, m * 128:m * 128 + 128], ident[0:Q, 0:Q])
                    last.then_inc(sem("tr"), 1)

            def router(name, r, f, n):
                pe.wait_ge(sem("xnT"), xnT_count(name))
                for b in range(B):
                    for m in range(DM):
                        last = mm(ps[0:Q, 4, b * f.E:(b + 1) * f.E], xnT[:, m, b * Q:(b + 1) * Q], gate[n][:, m, :], m == 0, m == DM - 1)
                last.then_inc(sem("r_logits"), 1)
                if r == "l2r":
                    pe.wait_ge(sem("l2r_onehot"), 1)
                    for b in range(B):
                        last = pe.transpose(ps[:, 5 + b // 4, (b % 4) * Q:(b % 4) * Q + Q],
                                            oh[:, b * 256 + 128:b * 256 + 256], ident[0:Q, 0:Q])
                    last.then_inc(sem("l2r_secT"), 1)
                    pe.wait_ge(sem("l2r_secT_sb"), 1)
                    for b in range(B):
                        last = mm(ps[0:Q, b // 4, (b % 4) * 128:(b % 4) * 128 + 128], secT[:, b * Q:(b + 1) * Q], simb[:, :], True, True)
                    last.then_inc(sem("l2r_sims"), 1)
                pe.wait_ge(sem("r_wrep"), ROUTERS.index(r) + 1)
                for b in range(B):
                    pe.transpose(ps[:, 5 + b // 4, (b % 4) * Q:(b % 4) * Q + Q], wrep[:, b, :], ident[0:Q, 0:Q])\
                        .then_inc(sem("r_wT"), 1)

            def ffn(f):
                nm = f.name

                def products(o, hi, lo, a, z, xh, xl, first, last, **kw):
                    mm(o, hi[:, a:z], xh, first, kw != {}, **kw)
                    mm(o, hi[:, a:z], xl, False, kw != {}, **kw)
                    return mm(o, lo[:, a:z], xh, False, last, **kw)

                def gu(c, k, hf):
                    if hf == 0:
                        pe.wait_ge(sem("ffn_wl"), 2 * f.base + 2 * c + 1)
                    if not isinstance(c, int) or c >= 1:
                        pe.wait_ge(sem(nm + "_h"), 2 * c + (hf - 1))
                    t = slice(hf * HT, (hf + 1) * HT)
                    for w in range(2 if f.gated else 1):
                        for m in range(DM):
                            at = (m * 2 + w) * 128 if f.gated else m * 128
                            last = products(ps[:, 2 * hf + w, 0:HT], whi[k], wlo[k], at, at + 128, xhi[:, m, t], xlo[:, m, t],
                                            m == 0, m == DM - 1)
                    last.then_inc(sem(nm + "_gu_done"), 1)

                def down(c, k, hf, first):
                    if hf == 0:
                        pe.wait_ge(sem("ffn_wl"), 2 * f.base + 2 * c + 2)
                    pe.wait_ge(sem("ffn_hl"), 2 * f.base + 2 * c + (hf + 1))
                    for m in range(DM):
                        at = f.cols + m * 128
                        last = products(ps[:, 4 + 2 * m + hf, 0:HT], whi[k], wlo[k], at, at + 128, hhi[hf][:, :], hlo[hf][:, :],
                                        first, True, skip_group_check=True)
                    last.then_inc(sem(nm + "_down_done"), 1)

                def step(c, k):
                    gu(c, k, 0)
                    for hf in range(2):
                        if hf:
                            gu(c, k, 1)
                        if not isinstance(c, int) or c:
                            down(c - 1, 1 - k, hf, isinstance(c, int) and c == 1)

                pe.wait_ge(sem("xlo"), (f.index + 1) * DM)
                f.loop(pe, step)
                for hf in range(2):
                    down(f.C - 1, (f.C - 1) % 2, hf, False)
                pe.wait_ge(sem("ffn_yT"), 4 * f.index + 4)
                for b in range(B):
                    for m in range(DM):
                        last = pe.transpose(ps[0:Q, b // 2, (b % 2) * D + m * 128:(b % 2) * D + m * 128 + 128],
                                            yT[:, m, b * Q:(b + 1) * Q], ident[:, :])
                    if b % 2:
                        last.then_inc(sem("ffn_back"), 1)

            transposes("n2")
            router("n2", "l0", FFN0, 0)
            pe.wait_ge(sem("w_ready"), w_count("l0"))
            ffn(FFN0)

            pe.wait_ge(sem("far_ready"), 1)

            def query_turn(b, k, n):
                if n == 0:
                    pe.wait_ge(sem("l1_xs"), b * 4 + 4)
                if not isinstance(b, int) or b or n:
                    pe.wait_ge(sem("bank7"), q_turn(b, n))
                for h in range(8):
                    last = pe.transpose(ps[0:96, 7, :].bitcast(BF16)[:, h * Q:(h + 1) * Q],
                                        xs[k][:, 8 * n + h, :, :].rearrange("q t r -> q (t r)"), identb[:, :])
                last.then_inc(sem("l1_qtr"), 1)

            def max_turn(b, k, s):
                pe.wait_ge(sem("l1_nmax"), b * SETS + (s + 1))
                pe.wait_ge(sem("bank7"), m_turn(b, s))
                for g in range(GRP):
                    h = GRP * s + g
                    last = mm(ps[96:97, 7, g * Q:(g + 1) * Q], nm[k][:, h:h + 1], identb[:, :], True, True)
                last.then_inc(sem("l1_mtr"), 1)

            def skip_turns(turn, n):
                pe.wait_ge(sem("bank7"), turn)
                pe.sem_inc(sem("bank7"), n)

            def a_bank(b, k, h, j):
                if h % GRP == 0 and j == 0:
                    s = h // GRP
                    pe.wait_ge(sem(f"in_stk{k}{s}"), b[1] if isinstance(b, tuple) else 96 * (b // 2 + 1))
                b = b[0] if isinstance(b, tuple) else b
                if h == 0 and j == 0:
                    pe.wait_ge(sem("bank7"), q_turn(b, 1) + 1)
                pe.wait_ge(sem("l1_amax"), b * (3 * HEADS) + (3 * h + j + 1))
                last = mm(ps[0:Q, j, 0:AW], qs[k][0:96, h, :], kstk[k][0:96, h, A0[j]:A0[j] + AW], True, True)
                if j == 2:
                    last = mm(ps[0:Q, 2, AW - Q:AW], identb[:, :], farb[:, :], False, True, skip_group_check=True)
                last.then_inc(sem("l1_a"), 1)

            def chunk_keys(c):
                return (c * 128, 128) if c < FULL else (FULL * 128 + CA * (c - FULL), CA)

            def b_scores(b, k, h):
                if h % GRP == 0:
                    pe.wait_ge(sem("bank7"), m_turn(b, h // GRP) + 1)
                for j in range(3):
                    pe.wait_ge(sem("l1_exp"), (b * HEADS + h) * 4 + (1, 2, 4)[j])
                    for c in range(4 * j, 4 * j + 4):
                        at, n = chunk_keys(c)
                        last = mm(ps[0:n, 3 + j, (c % 4) * Q:(c % 4) * Q + Q], kstk[k][0:97, h, at:at + n],
                                  qs[k][0:97, h, :], True, True)
                    last.then_inc(sem("l1_sc"), 1)

            def b_values(b, k, h, first=0, end=NCH):
                s, g = h // GRP, h % GRP
                if first == 0:
                    pe.wait_ge(sem("l1_masked"), b * HEADS + (h + 1))
                    if h == 0:
                        if not isinstance(b, int) or b:
                            pe.wait_ge(sem("l1_ot"), b * GRP)
                        pe.wait_ge(sem("l1_vaug"), b * NCH + NCH)
                for c in range(first, end):
                    n = 128 if c < FULL else CA
                    last = mm(ps[32 * g:32 * g + VW, 6, s * Q:(s + 1) * Q], vaug[k][0:n, c, h, :], pr[h % 2][0:n, c, :],
                              c == 0, c == NCH - 1)
                if end == NCH:
                    last.then_inc(sem("l1_pv"), 1)

            def out_turn(b):
                pe.wait_ge(sem("l1_ot"), b * GRP + GRP)
                pe.wait_ge(sem("bank7"), o_turn(b) if not (isinstance(b, int) and b == B - 1) else m_turn(b, SETS - 1) + 1)
                for s in range(SETS):
                    last = pe.transpose(ps[0:Q, 7, s * 128:(s + 1) * 128], ot[:, s * Q:(s + 1) * Q], ident[:, :])
                last.then_inc(sem("l1_oT"), 1)

            def both(b, k, na, before=True):
                for h in range(HEADS):
                    b_scores(b, k, h)
                    for j in range(3):
                        if h < LAG:
                            a_bank(b, k, HEADS - LAG + h, j)
                        elif na is not None:
                            a_bank((b + 1, na), 1 - k, h - LAG, j)
                        if CUTS[j] == CUTS[j + 1]:
                            continue
                        if h:
                            b_values(b, k, h - 1, CUTS[j], CUTS[j + 1])
                        elif before:
                            b_values(b - 1, 1 - k, HEADS - 1, CUTS[j], CUTS[j + 1])
                    if h < 2:
                        if na is not None:
                            query_turn(b + 1, 1 - k, h)
                        else:
                            skip_turns(q_turn(b + 1, h), 1)
                    elif h == 2:
                        if before:
                            out_turn(b - 1)
                        else:
                            skip_turns(o_turn(b - 1), 1)
                    elif h == LAG:
                        max_turn(b, k, SETS - 1)
                    elif h % GRP == LAG and na is not None:
                        max_turn(b + 1, 1 - k, h // GRP - 1)

            pe.sem_inc(sem("l1_pv"), 2)
            pe.sem_inc(sem("l1_sc"), 6 * HEADS)
            for n in range(2):
                query_turn(0, 0, n)
            skip_turns(q_turn(0, 1) + 1, 2)
            pe.wait_ge(sem("in_ones"), 16)
            for h in range(HEADS - LAG):
                for j in range(3):
                    a_bank((0, 96) if h % GRP == 0 else 0, 0, h, j)
                if h and h % GRP == 0:
                    max_turn(0, 0, h // GRP - 1)
            both(0, 0, 96, before=False)
            both(1, 1, 192)
            with pe.Fori(1, (B - 2) // 2) as i:
                both(i * 2, 0, (i + 1) * 96)
                both(i * 2 + 1, 1, (i + 2) * 96)
            both(B - 2, 0, B // 2 * 96)
            both(B - 1, 1, None)
            b_values(B - 1, 1, HEADS - 1)
            out_turn(B - 1)

            transposes("n4")
            router("n4", "l1r", FFN1, 1)
            pe.wait_ge(sem("w_ready"), w_count("l1r"))
            ffn(FFN1)
            transposes("n5")
            pe.wait_ge(sem("xnT"), xnT_count("n5"))
            pe.wait_ge(sem("in_qkv"), 48)
            for w in range(2):
                for e in range(DM):
                    for hf in range(2):
                        for m in range(DM):
                            last = mm(ps[:, 4 * w + 2 * e + hf, 0:HT], wqkv[:, w, m, e * 128:e * 128 + 128],
                                      xnT[:, m, hf * HT:(hf + 1) * HT], m == 0, m == DM - 1)
                last.then_inc(sem("l2_proj"), 1)
            for b in range(B):
                if b < 4:
                    pe.wait_ge(sem("l2a_qT"), 4)
                else:
                    pe.wait_ge(sem("l2_vnew"), b - 3)
                for m in range(DM):
                    last = mm(ps[0:Q, b % 4, 0:D], xnT[:, m, b * Q:(b + 1) * Q], wqkv[:, 2, m, :], m == 0, m == DM - 1)
                last.then_inc(sem("l2_vproj"), 1)

            def single(name, new):
                def scores(b, k, n):
                    pe.wait_ge(sem(f"{name}_ink{k}"), n * 16)
                    pe.wait_ge(sem(name + "_q"), b + 1)
                    pe.wait_ge(sem(name + "_scfree"), b + 2)
                    for j, (a, w) in enumerate(((0, 512), (512, 512), (1024, T - 1024))):
                        if new and j == 2:
                            w -= Q
                        for m in range(DM):
                            last = mm(ps[0:Q, j, 0:w], qst[k][:, m, :], ctT[k][:, m, a:a + w], m == 0, m == DM - 1)
                    if new:
                        for m in range(DM):
                            last = mm(ps[0:Q, 2, w:w + Q], qst[k][:, m, :], knT[:, m, bass.ds(b * Q, Q)], m == 0, m == DM - 1)
                    last.then_inc(sem(name + "_sc"), 1)

                def values(b, k, turn):
                    pe.wait_ge(sem(name + "_p"), b + 1)
                    at = 0
                    for c in range(NCH):
                        n = 128 if c < FULL else CB[c - FULL]
                        if c % 4 == 0:
                            pe.wait_ge(sem(name + "_pt"), b * 3 + (c // 4 + 1))
                        last = pe.transpose(ps[0:n, 3 + c // 4, (c % 4) * Q:(c % 4) * Q + Q], pb[k][:, at:at + n], ident[0:Q, 0:Q])
                        at += n
                        if c % 4 == 3:
                            last.then_inc(sem(name + "_ptr"), 1)
                    pe.wait_ge(sem(name + "_ofree"), b + 1)
                    pe.wait_ge(sem(f"{name}_inv{k}"), turn * 48)
                    for c in range(NCH):
                        n = 128 if c < FULL else CB[c - FULL]
                        if c % 4 == 0:
                            pe.wait_ge(sem(name + "_pt"), b * 3 + (c // 4 + 4))
                        v = vnew[:, bass.ds(b, 1), :].rearrange("q a d -> q (a d)") if new and c == NCH - 1 else vn2[k][0:n, c, :]
                        last = mm(ps[0:Q, 6, 0:D], ptt[0:n, c, :], v, c == 0, c == NCH - 1)
                    last.then_inc(sem(name + "_o"), 1)

                pe.sem_inc(sem(name + "_sc"), 2)
                pe.sem_inc(sem(name + "_o"), 2)
                scores(0, 0, 1)
                with pe.Fori(0, (B - 2) // 2) as i:
                    scores(i * 2 + 1, 1, i + 1)
                    values(i * 2, 0, i + 1)
                    scores(i * 2 + 2, 0, i + 2)
                    values(i * 2 + 1, 1, i + 1)
                scores(B - 1, 1, B // 2)
                values(B - 2, 0, B // 2)
                values(B - 1, 1, B // 2)

            pe.wait_ge(sem("l2_vnew"), B)
            pe.wait_ge(sem("l2a_kT"), 4)
            single("l2a", True)
            transposes("n6")
            router("n6", "l2r", FFN2, 2)
            pe.wait_ge(sem("w_ready"), w_count("l2r"))
            ffn(FFN2)
            transposes("n7")
            pe.wait_ge(sem("xnT"), xnT_count("n7"))
            single("l3a", False)
            transposes("n8")
            router("n8", "l3r", FFN3, 3)
            pe.wait_ge(sem("w_ready"), w_count("l3r"))
            for hf in range(2):
                last = mm(ps[:, 1 + 2 * hf, 0:HT], awmat[:, :], Wb[:, hf * HT:(hf + 1) * HT], True, True)
            last.then_inc(sem("l3_gate"), 1)
            ffn(FFN3)

        @block.vector
        def _(dve):
            ch = Chain(dve, sem("dve_own"))
            link, add = ch.link, ch.add

            def bc(ap, shape):
                return ap.broadcast_to(shape)

            def stats(name, src, between):
                for b in range(B):
                    add(dve.bn_stats(stat[:, b, :], src[:, b, :]))
                ch.wait()
                for b in range(B):
                    last = dve.bn_aggr(mv[:, b, :], stat[:, b, :])
                    if b < B - 1:
                        add(last)
                last.then_inc(sem("stat"), 1)
                if between is not None:
                    split(between)
                dve.wait_ge(sem("rstd"), NORMS.index(name) + 1)

            def norm(name, src=x, between=None, then=None):
                stats(name, src, between)
                for b in range(B):
                    dve.tensor_scalar(xn[:, b, :], src[:, b, :], mv[:, b, 0:1], rstd[:, b:b + 1], ALU.subtract, ALU.mult)\
                        .then_inc(sem("xn"), 1)
                    if b == 0 and then is not None:
                        then()

            dve.sem_inc(sem("l1_amax"), 3)
            dve.wait_ge(sem("decayed"), 1)
            link(dve.memset(orow, 1.0))
            link(dve.tensor_scalar(krow, orow, dk[:, 1:2], None, ALU.mult))
            dve.tensor_tensor_scan(crow[:, ::-1], krow, orow, 0.0, ALU.mult, ALU.add).then_inc(sem("crow_ready"), 1)
            dve.wait_ge(sem("crow_ready"), 1)
            link(dve.tensor_reduce(csum[:, 0:1], crow, AX.X, ALU.add))

            def split(u):
                dve.wait_ge(sem("kh_done"), u + 1)
                if u >= 2:
                    dve.wait_ge(sem("kl_done"), u - 1)
                dve.tensor_tensor(rest[u % 2], ct[u % RING], part[u % 3][:, 0, :], ALU.subtract).then_inc(sem("rest_done"), 1)

            dve.wait_ge(sem("in_x"), 16)
            norm("n0")
            for u in range(UNITS):
                dve.wait_ge(sem(f"in_ct{u % RING}"), 16 * (u // RING + 1))
                link(dve.tensor_tensor_reduce(out=prod, in0=ct[u % RING], in1=crow, scale=1.0 / T, scalar=0.0, op0=ALU.mult, op1=ALU.add,
                                              accum_out=wkv[:, u % DM, u // DM:u // DM + 1]))
                if u % 2:
                    split(u // 2)
            dve.engine_nop().then_inc(sem("wkv_ready"), 1)
            dve.wait_ge(sem("in_lora"), 8 * 16)
            link(dve.tensor_tensor(aw_t, attr_r, wa_b, ALU.mult))
            dve.tensor_reduce(aw_t[:, 0:1], aw_t, AX.X, ALU.add).then_inc(sem("aw_dot"), 1)
            for c in range(FFN1.C):
                dve.wait_ge(sem("lora"), c + 1)
                k = 2 + 2 * (c % 2)
                dve.scalar_tensor_tensor(mgu[:, c, :], ps[:, k, :], 2.0, mgu[:, c, :], ALU.mult, ALU.add).then_inc(sem("merged"), 1)
                dve.scalar_tensor_tensor(mdn[:, c, :], ps[:, k + 1, 0:D], 2.0, mdn[:, c, :], ALU.mult, ALU.add).then_inc(sem("merged"), 1)
            dve.wait_ge(sem("lora_gate"), 1)
            dve.wait_ge(sem("in_gate"), 64)
            add(dve.scalar_tensor_tensor(gate[1][:, :, :], ps[:, 6, 0:16].rearrange("p (m e) -> p m e", m=DM), 2.0, gate[1][:, :, :], ALU.mult, ALU.add))
            dve.wait_ge(sem("s1_done"), 1)
            for m in range(DM):
                link(dve.tensor_scalar(csum[:, 1:2], csum[:, 0:1], bin_c[:, m:m + 1], 1.0 / T, ALU.mult, ALU.mult))
                link(dve.tensor_scalar(s1[:, m, :], ps[:, 7, m * B:(m + 1) * B], csum[:, 1:2], None, ALU.add))
            for m in range(DM):
                dve.tensor_copy(s1r[:, m, :, :], bc(s1[:, m, :].unsqueeze(2), [128, B, Q])).then_inc(sem("s1_ready"), 1)
            for u in range(UNITS // 2, EARLY):
                split(u)
            dve.wait_ge(sem("summed"), 1)
            dve.wait_ge(sem("xn"), xn_count("n0"))
            for j in range(4):
                add(dve.tensor_tensor(xn[:, 2 * j:2 * j + 2, :], xn[:, 2 * j:2 * j + 2, :], ps[0:Q, j, :].rearrange("q (b d) -> q b d", b=2), ALU.add))
            ch.wait()
            link(dve.tensor_tensor(xn[:, :, :], xn[:, :, :], bc(bout_b.unsqueeze(1), [Q, B, D]), ALU.add))
            norm("n1", xn, between=EARLY)
            dve.wait_ge(sem("xn"), xn_count("n1"))
            split(EARLY + 1)
            link(dve.tensor_tensor(xn[:, :, :], xn[:, :, :], bc(gam_b.unsqueeze(1), [Q, B, D]), ALU.mult))
            link(dve.tensor_tensor(x[:, :, :], x[:, :, :], xn[:, :, :], ALU.add))
            link(dve.tensor_tensor(x[:, :, :], x[:, :, :], bc(bet_b.unsqueeze(1), [Q, B, D]), ALU.add))

            def router(r, f):
                E, K = f.E, f.K

                def v3(t):
                    return t[:, 0:B * E].rearrange("q (b e) -> q b e", b=B)

                dve.wait_ge(sem("r_logits"), ROUTERS.index(r) + 1)
                link(dve.tensor_copy(rl[:, 0:B * E], ps[0:Q, 4, 0:B * E]))
                link(dve.tensor_reduce(rmx, v3(rl), AX.X, ALU.max))
                dve.tensor_tensor(v3(rp), v3(rl), bc(rmx.unsqueeze(2), [Q, B, E]), ALU.subtract).then_inc(sem("r_shift"), 1)
                dve.wait_ge(sem("r_exp"), ROUTERS.index(r) + 1)
                link(dve.tensor_reduce(rsum, v3(rp), AX.X, ALU.add))
                link(dve.reciprocal(rsum, rsum))
                link(dve.tensor_tensor(v3(rp), v3(rp), bc(rsum.unsqueeze(2), [Q, B, E]), ALU.mult))
                src = v3(rl) if r == "l3r" else v3(rp)
                for b in range(B):
                    add(dve.max(v8[:, b, :], src[:, b, :]))
                ch.wait()
                for b in range(B):
                    add(dve.max_index(i8[:, b, :], v8[:, b, :], src[:, b, :]))
                ch.wait()
                link(dve.tensor_copy(if8, i8))
                o = oh[:, 0:B * K * E].rearrange("q (b k e) -> q b k e", b=B, k=K)
                ins = dve.tensor_tensor(o, bc(iota[:, 0:E].unsqueeze(1).unsqueeze(1), [Q, B, K, E]),
                                        bc(if8[:, :, 0:K].unsqueeze(3), [Q, B, K, E]), ALU.is_equal)
                w = v3(rw)
                if r != "l2r":
                    link(ins)
                    link(dve.tensor_reduce(v3(rsel), o.rearrange("q b k e -> q b e k"), AX.X, ALU.add))
                    link(dve.tensor_tensor(w, v3(rp), v3(rsel), ALU.mult))
                    if r != "l0":
                        link(dve.tensor_reduce(rsum, w, AX.X, ALU.add))
                        if r == "l3r":
                            link(dve.tensor_scalar(rsum, rsum, 1e-8, None, ALU.add))
                        link(dve.reciprocal(rsum, rsum))
                        link(dve.tensor_tensor(w, w, bc(rsum.unsqueeze(2), [Q, B, E]), ALU.mult))
                else:
                    ins.then_inc(sem("l2r_onehot"), 1)
                    dve.wait_ge(sem("l2r_onehot"), 1)
                    link(dve.tensor_reduce(rsum, v8, AX.X, ALU.add))
                    link(dve.tensor_scalar(rsum, rsum, 1e-12, None, ALU.max))
                    link(dve.reciprocal(rsum, rsum))
                    link(dve.tensor_tensor(w8, v8, bc(rsum.unsqueeze(2), [Q, B, 8]), ALU.mult))
                    dve.wait_ge(sem("l2r_secT"), 1)
                    add(dve.tensor_copy(secT[:, 0:HT], ps[:, 5, 0:HT]))
                    ch.wait()
                    dve.tensor_copy(secT[:, HT:TOK], ps[:, 6, 0:HT]).then_inc(sem("l2r_secT_sb"), 1)
                    dve.wait_ge(sem("l2r_sims"), 1)
                    for j in range(2):
                        add(dve.tensor_copy(scand[:, j * 512:j * 512 + 512], ps[0:Q, j, :]))
                    ch.wait()
                    for b in range(B):
                        add(dve.tensor_tensor(cand[:, b * 512:(b + 1) * 512].rearrange("q (j i e) -> q j i e", j=4, i=4),
                                              bc(scand[:, b * 128:(b + 1) * 128].rearrange("q (j e) -> q j e", j=4).unsqueeze(2), [Q, 4, 4, 32]),
                                              bc(o[:, b, 0:4, :].unsqueeze(1), [Q, 4, 4, 32]), ALU.mult))
                    ch.wait()
                    link(dve.tensor_reduce(pick, cand.rearrange("q (b j i e) -> q (b j) i e", b=B, j=4, i=4), AX.X, ALU.add))
                    link(dve.tensor_reduce(best, pick, AX.X, ALU.max))
                    link(dve.tensor_scalar(keep, best, 0.5, None, ALU.is_lt))
                    link(dve.tensor_scalar(left, keep, -1.0, 1.0, ALU.mult, ALU.add))
                    link(dve.tensor_tensor(pick, pick, bc(best.unsqueeze(3), [Q, B, 4, 4]), ALU.is_equal))
                    for i in range(4):
                        link(dve.tensor_tensor(first[:, :, :, i], left, pick[:, :, :, i], ALU.mult))
                        if i < 3:
                            link(dve.tensor_tensor(left, left, first[:, :, :, i], ALU.subtract))
                    link(dve.tensor_tensor(first, first, bc(w8[:, :, 4:8].unsqueeze(3), [Q, B, 4, 4]), ALU.mult))
                    link(dve.tensor_reduce(moved, first.rearrange("q b j i -> q b i j"), AX.X, ALU.add))
                    link(dve.tensor_tensor(w8[:, :, 0:4], w8[:, :, 0:4], moved, ALU.add))
                    link(dve.tensor_tensor(w8[:, :, 4:8], w8[:, :, 4:8], keep, ALU.mult))
                    link(dve.tensor_tensor(o, o, bc(w8.unsqueeze(3), [Q, B, 8, 32]), ALU.mult))
                    link(dve.tensor_reduce(w, o.rearrange("q b k e -> q b e k"), AX.X, ALU.add))
                dve.tensor_copy(wrep.rearrange("q b (e r) -> q b e r", e=E), bc(w.unsqueeze(3), [Q, B, E, f.rep]))\
                    .then_inc(sem("r_wrep"), 1)
                dve.wait_ge(sem("w_ready"), w_count(r))
                if r == "l3r":
                    dve.wait_ge(sem("l3_gate"), 1)
                    for hf in range(2):
                        t = Wb[:, hf * HT:(hf + 1) * HT]
                        add(dve.scalar_tensor_tensor(t, ps[:, 1 + 2 * hf, 0:HT], 0.9, t, ALU.add, ALU.mult))
                    ch.wait()

            def ffn(f):
                nm = f.name

                def unit(c, hf, weighted):
                    if f.gated:
                        dve.wait_ge(sem("ffn_silu"), 2 * f.base + 2 * c + (hf + 1))
                        if weighted:
                            link(dve.tensor_tensor(sg[hf][:, :], sg[hf][:, :], Wb[:, hf * HT:(hf + 1) * HT], ALU.mult))
                        a, o = sg[hf][:, :], ps[:, 2 * hf + 1, 0:HT]
                    else:
                        dve.wait_ge(sem(nm + "_gu_done"), 2 * c + (hf + 1))
                        a, o = Wb[:, hf * HT:(hf + 1) * HT], ps[:, 2 * hf, 0:HT]
                    if not isinstance(c, int) or c >= 1:
                        dve.wait_ge(sem("ffn_hl"), 2 * f.base + 2 * c + (hf - 1))
                    dve.tensor_tensor(hb[hf][:, :], a, o, ALU.mult).then_inc(sem(nm + "_h"), 1)

                def low(c, hf):
                    dve.wait_ge(sem("ffn_hh"), 2 * f.base + 2 * c + (hf + 1))
                    dve.tensor_tensor(hlo[hf][:, :], hb[hf][:, :], hhi[hf][:, :], ALU.subtract).then_inc(sem("ffn_hl"), 1)

                def step(c, weighted):
                    unit(c, 0, weighted)
                    if not isinstance(c, int) or c:
                        low(c - 1, 1)
                    unit(c, 1, weighted)
                    low(c, 0)

                head = f.C if f.C <= 4 else 3
                for c in range(head):
                    step(c, c >= f.shared)
                if head < f.C:
                    with dve.Fori(head, f.C, 1) as c:
                        ch.enter(c, head, 2)
                        step(c, True)
                        ch.leave(f.C - head, 2)
                low(f.C - 1, 1)
                dve.wait_ge(sem(nm + "_down_done"), 2 * f.C)
                for m in range(DM):
                    dve.tensor_copy(yT[:, m, HT:TOK], ps[:, 5 + 2 * m, 0:HT]).then_inc(sem("ffn_yT"), 1)
                for j in range(4):
                    dve.wait_ge(sem("ffn_back"), 4 * f.index + j + 1)
                    o = ps[0:Q, j, :].rearrange("q (b d) -> q b d", b=2)
                    ins = dve.tensor_tensor(x[:, 2 * j:2 * j + 2, :], x[:, 2 * j:2 * j + 2, :], o, ALU.add)
                    if nm == "l3":
                        ins.then_inc(sem("l3_x"), 1)
                    else:
                        add(ins)
                ch.wait()

            norm("n2", between=EARLY + 2)
            for u in range(EARLY + 3, UNITS):
                split(u)
            dve.wait_ge(sem("in_blk"), 20 * 16)
            add(dve.tensor_scalar(awmat[:, :], ident[:, :], -1.0, 1.0, ALU.mult, ALU.add))
            ch.wait()
            link(dve.tensor_tensor(simb[:, :], simb[:, :], awmat[:, :], ALU.mult))
            link(dve.tensor_tensor(simb[:, :], simb[:, :], ident[:, :], ALU.add))
            dve.wait_ge(sem("aw_sig"), 1)
            link(dve.memset(awmat[:, :], 0.2 / FFN3.rep))
            link(dve.tensor_scalar(awmat[:, :], awmat[:, :], awcol[:, :], None, ALU.mult))
            for n in range(3):
                dve.wait_ge(sem(f"parts_out{n}"), 16 * ((DM * B + 2 - n) // 3))
            router("l0", FFN0)
            ffn(FFN0)

            def first_queries():
                dve.wait_ge(sem("xn"), xn_count("n3", 1))
                src = xn[:, 0, :].rearrange("q (h r) -> q h r", h=HEADS)
                dve.tensor_copy(xs[0][:, :, 0:3, :], bc(src.unsqueeze(2), [Q, HEADS, 3, HD])).then_inc(sem("l1_xs"), 1)
                dve.wait_ge(sem("l1_xs"), 1)
                dve.tensor_tensor(xr, src, xs[0][:, :, 0, :], ALU.subtract).then_inc(sem("l1_xs"), 1)
                dve.wait_ge(sem("l1_xs"), 2)
                dve.tensor_copy(xs[0][:, :, 3:5, :], bc(xr.unsqueeze(2), [Q, HEADS, 2, HD])).then_inc(sem("l1_xs"), 1)
                dve.wait_ge(sem("l1_xs"), 3)
                dve.tensor_tensor(xs[0][:, :, 5, :], xr, xs[0][:, :, 3, :], ALU.subtract).then_inc(sem("l1_xs"), 1)

            norm("n3", then=first_queries)

            def l1_o(b):
                dve.wait_ge(sem("l1_oT"), b + 1)
                o = ps[0:Q, 7, :].rearrange("q (h v) -> q h v", h=HEADS)
                link(dve.reciprocal(den[:, :], o[:, :, HD]))
                link(dve.tensor_tensor(att[:, :, :], o[:, :, 0:HD], bc(den[:, :].unsqueeze(2), [Q, HEADS, HD]), ALU.mult))
                dve.sem_inc(sem("bank7"), 1)
                xb = x[:, bass.ds(b, 1), :].rearrange("q a d -> q (a d)")
                add(dve.tensor_tensor(xb, xb, att[:, :, :].rearrange("q h v -> q (h v)"), ALU.add))

            def l1_a(b, k):
                for h in range(HEADS):
                    s = h // GRP
                    if h % GRP == 0 and not (isinstance(b, int) and b == h == 0):
                        dve.wait_ge(sem("l1_nmax"), b * SETS + s)
                    for j in range(3):
                        dve.wait_ge(sem("l1_a"), b * (3 * HEADS) + (3 * h + j + 1))
                        dve.tensor_reduce(mx[:, h % GRP, j:j + 1], ps[0:Q, j, 0:AW], AX.X, ALU.max).then_inc(sem("l1_amax"), 1)
                    if h % GRP == GRP - 1:
                        dve.wait_ge(sem("l1_amax"), b * (3 * HEADS) + (3 * h + 6))
                        dve.tensor_reduce(nm[k][:, GRP * s:GRP * s + GRP], mx[:, :, :], AX.X, ALU.max, negate=True)\
                            .then_inc(sem("l1_nmax"), 1)

            l1_a(0, 0)
            l1_a(1, 1)
            l1_o(0)
            with dve.Fori(1, B // 2) as i:
                ch.enter(i, 1, 6)
                l1_a(i * 2, 0)
                l1_o(i * 2 - 1)
                l1_a(i * 2 + 1, 1)
                l1_o(i * 2)
                ch.leave(B // 2 - 1, 6)
            l1_o(B - 1)
            ch.wait()

            norm("n4")
            router("l1r", FFN1)
            ffn(FFN1)
            norm("n5")
            dve.wait_ge(sem("in_qkv"), 48)
            for w, dst in ((0, yT), (1, knT)):
                dve.wait_ge(sem("l2_proj"), w + 1)
                for e in range(DM):
                    for hf in range(2):
                        dve.tensor_scalar(dst[:, e, hf * HT:(hf + 1) * HT], ps[:, 4 * w + 2 * e + hf, 0:HT], bqk[:, w, e:e + 1], None, ALU.add)\
                            .then_inc(sem("l2a_qT" if w == 0 else "l2a_kT"), 1)
            dve.wait_ge(sem("l2a_kT"), 4)

            def single(name, masked):
                def front(b, k, n):
                    dve.wait_ge(sem(f"{name}_inm{k}"), n * 16)
                    if not masked:
                        link(dve.tensor_copy(bias[k], mk8[k]))
                        link(dve.tensor_reduce(anym[k], bias[k], AX.X, ALU.max))
                        link(dve.tensor_scalar(bias[k], bias[k], -1.0, -FAR, ALU.add, ALU.mult))
                    dve.wait_ge(sem(name + "_sc"), b + 3)
                    flat = ps[0:Q, 0:3, :].rearrange("q j n -> q (j n)")[:, 0:T]
                    dve.scalar_tensor_tensor(sc, flat, D ** -0.5, bias[k], ALU.mult, ALU.add).then_inc(sem(name + "_scfree"), 1)
                    dve.wait_ge(sem(name + "_scfree"), b + 3)
                    dve.tensor_reduce(nmx, sc, AX.X, ALU.max, negate=True).then_inc(sem(name + "_max"), 1)

                def middle(b, k):
                    dve.wait_ge(sem(name + "_exp"), b + 1)
                    link(dve.reciprocal(rsm, ssum))
                    if not masked:
                        link(dve.tensor_tensor(rsm, rsm, anym[k], ALU.mult))
                    dve.tensor_scalar(pb[k], pb[k], rsm, None, ALU.mult).then_inc(sem(name + "_p"), 1)

                def end(b):
                    dve.wait_ge(sem(name + "_o"), b + 3)
                    xb = x[:, bass.ds(b, 1), :].rearrange("q a d -> q (a d)")
                    dve.tensor_tensor(xb, xb, ps[0:Q, 6, 0:D], ALU.add).then_inc(sem(name + "_ofree"), 1)

                dve.sem_inc(sem(name + "_scfree"), 2)
                dve.sem_inc(sem(name + "_ofree"), 1)
                per = 1 if masked else 5
                front(0, 0, 1)
                with dve.Fori(0, B // 2 - 1) as i:
                    ch.enter(i, 0, 2 * per)
                    middle(i * 2, 0)
                    front(i * 2 + 1, 1, i + 1)
                    end(i * 2)
                    middle(i * 2 + 1, 1)
                    front(i * 2 + 2, 0, i + 2)
                    end(i * 2 + 1)
                    ch.leave(B // 2 - 1, 2 * per)
                middle(B - 2, 0)
                front(B - 1, 1, B // 2)
                end(B - 2)
                middle(B - 1, 1)
                end(B - 1)
                dve.wait_ge(sem(name + "_ofree"), B + 1)

            for b in range(B):
                dve.wait_ge(sem("l2_vproj"), b + 1)
                dve.tensor_tensor(vnew[:, b, :], ps[0:Q, b % 4, 0:D], bv_b, ALU.add).then_inc(sem("l2_vnew"), 1)
            single("l2a", True)
            norm("n6")
            router("l2r", FFN2)
            ffn(FFN2)
            norm("n7")
            single("l3a", False)
            norm("n8")
            router("l3r", FFN3)
            ffn(FFN3)


def kernel(**inputs):
    import numpy as _np
    import concourse.bacc as _bacc
    from concourse import mybir as _mybir
    from concourse.bass_utils import run_bass_kernel_spmd as _run

    a = {k: _np.asarray(v) for k, v in inputs.items()}

    def halves(t):
        c, w, n = t.shape
        return t.reshape(c, w // 128, 128, n).transpose(0, 2, 1, 3).reshape(c, 128, (w // 128) * n)

    def gated(gu, dn, experts):
        e, f2, w = gu.shape
        per, f = 128 // experts, f2 // 2
        g = gu.reshape(e, 2, f // per, per, w).transpose(2, 4, 1, 0, 3).reshape(f // per, w, 2 * 128)
        n = dn.reshape(e, w, f // per, per).transpose(2, 0, 3, 1).reshape(f // per, 128, w)
        return halves(g), n

    gu0, dn0 = gated(a["L0_ffn_gate_up_weights"], a["L0_ffn_down_weights"], FFN0.E)
    sgu, sdn = a["L0_ffn_shared_gate_up"], a["L0_ffn_shared_down"]
    fs = sdn.shape[1]
    fill = FFN0.shared * 128 - fs
    sgu = _np.pad(sgu.reshape(2, fs, D), ((0, 0), (0, fill), (0, 0))).reshape(1, 2 * (fs + fill), D)
    sdn = _np.pad(sdn, ((0, 0), (0, fill))).reshape(1, D, fs + fill)
    gus, dns = gated(sgu, sdn, 1)
    gu2, dn2 = gated(a["L2_ffn_gate_up_proj"], a["L2_ffn_down_proj"], FFN2.E)
    e1 = FFN1.E
    gup = a["L1_ffn_gate_up_proj"].reshape(e1, D, 2, FFN1.C, FFN1.rep).transpose(3, 1, 2, 0, 4).reshape(FFN1.C, D, 256)
    dnp = a["L1_ffn_down_proj"].reshape(e1, FFN1.C, FFN1.rep, D).transpose(1, 0, 2, 3).reshape(FFN1.C, 128, D)
    u3 = a["L3_ffn_U"].reshape(32, D, FFN3.C, FFN3.rep).transpose(2, 1, 0, 3).reshape(FFN3.C, D, 128)
    v3 = a["L3_ffn_V"].reshape(32, FFN3.C, FFN3.rep, D).transpose(1, 0, 2, 3).reshape(FFN3.C, 128, D)
    ctx = a["ctx_2048"]
    arrays = {
        "x": a["x"], "ctx": ctx, "ctxT": ctx.transpose(0, 2, 1), "mask": a["mask_BxSxS2_ff0"],
        "bkmask": a["mask_BxS2_bk0"],
        "decay": a["L0_xattn_decay"].reshape(1, 1), "winT": a["L0_xattn_W_in"].T, "woutT": a["L0_xattn_W_out"].T,
        "b_in": a["L0_xattn_b_in"].reshape(DM, 128).T, "b_out": a["L0_xattn_b_out"], "gamma": a["L0_xattn_gamma"], "beta": a["L0_xattn_beta"],
        "gate0T": a["L0_ffn_gate_weight"].T, "gate1T": a["L1_ffn_gate_weight"].T,
        "gate2T": a["L2_ffn_gate_weight"].T, "gate3T": a["L3_ffn_Wr"].T,
        "l0_w": _np.concatenate([_np.concatenate([gus, gu0]), _np.concatenate([dns, dn0])], axis=2),
        "l1_gu": halves(gup), "l1_dn": dnp, "l2_w": _np.concatenate([gu2, dn2], axis=2),
        "l3_w": _np.concatenate([halves(u3), v3], axis=2),
        "ones": _np.full((1, 2 * 11552), 0x3F803F80, _np.uint32).view(_np.float32),
        "gupA": a["L1_ffn_gup_lora_A"].reshape(128, D),
        "gupB": a["L1_ffn_gup_lora_B"].transpose(0, 2, 1).reshape(e1, 16, 2, FFN1.C, 16).transpose(0, 1, 3, 2, 4),
        "dnA": a["L1_ffn_down_lora_A"].reshape(e1, 16, FFN1.C, 16),
        "dnB": a["L1_ffn_down_lora_B"].transpose(0, 2, 1).reshape(128, D),
        "glA": a["L1_ffn_gate_lora_A"], "glB": a["L1_ffn_gate_lora_B"].T,
        "sim": a["L2_ffn_similarity"],
        "attr": _np.repeat(a["L3_ffn_attr"], FFN3.rep, axis=0), "Wa": a["L3_ffn_Wa"].reshape(32),
        "wqkvT": _np.stack([a["L2_xattn_Wq"].T, a["L2_xattn_Wk"].T, a["L2_xattn_Wv"].T]),
        "bqk": _np.stack([a["L2_xattn_bq"], a["L2_xattn_bk"]]).reshape(2, DM, 128).transpose(2, 0, 1), "bv": a["L2_xattn_bv"],
        "ident": _np.eye(128, dtype=_np.float32),
        "iota": _np.arange(32, dtype=_np.float32),
    }
    nc = _bacc.Bacc("TRN2", target_bir_lowering=False, num_devices=1)
    maps, d = {}, {}
    for name, v in arrays.items():
        v = _np.ascontiguousarray(v)
        maps["in_" + name] = v
        d[name] = nc.dram_tensor("in_" + name, v.shape, _mybir.dt.from_np(v.dtype), kind="ExternalInput").ap()
    out = nc.dram_tensor("out_x", (B, Q, D), F32, kind="ExternalOutput").ap()
    build(nc, d, out)
    r = _run(nc, [maps], core_ids=[0])
    return r.results[0]["out_x"]
```
